# Optimizing a Trainium2 kernel written in Bass

```python
import numpy as np
import jax
import jax.numpy as jnp

def _softmax(x, axis=-1):
    return jax.nn.softmax(x, axis=axis)

def _gelu(x):
    return jax.nn.gelu(x, approximate=True)

def _silu(x):
    return jax.nn.silu(x)

def _sigmoid(x):
    return jax.nn.sigmoid(x)

def _layernorm(x, axis=-1, eps=1e-05):
    m = jnp.mean(x, axis=axis, keepdims=True)
    v = jnp.var(x, axis=axis, keepdims=True)
    return (x - m) / jnp.sqrt(v + eps)

def _scatter_add(tgt, idx, src, axis=0):
    return tgt.at[idx].add(src)

def _segment_sum(src, seg, n):
    return jax.ops.segment_sum(src, seg, n)
kernel_name = 'mk_xattn_ffn_d4_seqx_r4_e07c26'

def setup_inputs(seed: int=0):
    np.random.seed(seed)
    _w = jnp.asarray

    def _rec_inputs():
        import jax
        import jax.numpy as jnp
        _rk = jax.random.key(seed)
        x = 7.22e-05 + 1 * jax.random.normal(jax.random.fold_in(_rk, 1), (2, 1024, 256), jnp.float32)
        _lenS = 1024 - jax.random.randint(jax.random.fold_in(_rk, 7), (2,), 0, max(1, 1024 // 4) + 1, jnp.int32)
        _lenS2 = 77 - jax.random.randint(jax.random.fold_in(_rk, 8), (2,), 0, max(1, 77 // 4) + 1, jnp.int32)
        _ctx_1024P = jax.random.normal(jax.random.fold_in(_rk, 11), (2, 16, 256), jnp.float32)
        _ctx_1024c = jax.random.dirichlet(jax.random.fold_in(_rk, 511), 0.3 * jnp.ones((16,), jnp.float32), (2, 77))
        _ctx_1024t = jnp.einsum('bsk,bkd->bsd', _ctx_1024c, _ctx_1024P)
        _ctx_1024t = _ctx_1024t * jax.lax.rsqrt(jnp.mean(jnp.square(_ctx_1024t)) + 1e-12) * 0.953939
        ctx_1024 = 4.13588e-05 + 0.999923 * (_ctx_1024t + 0.3 * jax.random.normal(jax.random.fold_in(_rk, 611), (2, 77, 256), jnp.float32))
        _validS = jnp.arange(1024)[None, :] < _lenS[:, None]
        _validS2 = jnp.arange(77)[None, :] < _lenS2[:, None]
        _causal = jnp.tril(jnp.ones((1024, 1024), dtype=bool))
        mask_BxSxS2_bk1 = jnp.broadcast_to(_validS2[:, None, :], (2, 1024, 77))
        mask_BxS2_bk0 = jnp.logical_not(jnp.broadcast_to(_validS2[:, :], (2, 77)))
        return (x, ctx_1024, mask_BxSxS2_bk1, mask_BxS2_bk0)
    x, ctx_1024, mask_BxSxS2_bk1, mask_BxS2_bk0 = _rec_inputs()

    def _L0_xattn_setup():
        import jax, jax.numpy as jnp
        import numpy as np
        B, S, D_MODEL, N_HEAD = (4, 512, 256, 16)
        D_HEAD = D_MODEL // N_HEAD
        D_Q = D_K = D_V = 64
        key = jax.random.key(seed)
        ks = jax.random.split(key, 12)
        s = 1.0 / np.sqrt(D_HEAD)
        return {'q': jax.random.normal(ks[0], (B, S, D_MODEL), jnp.float32), 'k': jax.random.normal(ks[1], (B, S, D_MODEL), jnp.float32), 'v': jax.random.normal(ks[2], (B, S, D_MODEL), jnp.float32), 'mask': jax.random.randint(ks[3], (B, S, S), 0, 2) == 1, 'Wq': jax.random.uniform(ks[4], (N_HEAD, D_HEAD, D_Q), jnp.float32, -s, s), 'bq': jax.random.uniform(ks[5], (N_HEAD, D_Q), jnp.float32, -s, s), 'Wk': jax.random.uniform(ks[6], (N_HEAD, D_HEAD, D_K), jnp.float32, -s, s), 'bk': jax.random.uniform(ks[7], (N_HEAD, D_K), jnp.float32, -s, s), 'Wv': jax.random.uniform(ks[8], (N_HEAD, D_HEAD, D_V), jnp.float32, -s, s), 'bv': jax.random.uniform(ks[9], (N_HEAD, D_V), jnp.float32, -s, s), 'Wo': jax.random.uniform(ks[10], (D_MODEL, D_V * N_HEAD), jnp.float32, -s, s), 'bo': jax.random.uniform(ks[11], (D_MODEL,), jnp.float32, -s, s)}
    _L0_xattn_all = _L0_xattn_setup()
    _L0_xattn_in = {k: v for k, v in _L0_xattn_all.items() if k in ('Wq', 'bq', 'Wk', 'bk', 'Wv', 'bv', 'Wo', 'bo')}
    del _L0_xattn_all

    def _L0_ffn_setup():
        import jax, jax.numpy as jnp
        import numpy as np
        B, S, D = (1, 512, 256)
        E, K, F = (64, 8, 192)
        SF = 192
        C = 128
        ROUTED_SCALE = 1.0

        def _moe_forward(x, router_w, w_gate, w_up, w_down, ws_gate_up, ws_down):
            T = x.shape[0]
            logits = x.astype(jnp.float32) @ router_w.T
            probs = jax.nn.softmax(logits, axis=-1)
            topk_w, topk_ids = jax.lax.top_k(probs, K)
            topk_w = topk_w / jnp.sum(topk_w, axis=-1, keepdims=True)
            topk_w = topk_w.astype(x.dtype)
            N = T * K
            flat_e = topk_ids.reshape(-1)
            flat_w = topk_w.reshape(-1)
            tok = jnp.arange(N) // K
            onehot = flat_e[:, None] == jnp.arange(E)[None, :]
            pos = jnp.cumsum(onehot, axis=0)[jnp.arange(N), flat_e] - 1
            valid = pos < C
            idx = jnp.where(valid, flat_e * C + pos, E * C)
            x_buf = jnp.zeros((E * C + 1, x.shape[1]), x.dtype).at[idx].set(x[tok])
            xb = x_buf[:E * C].reshape(E, C, -1)
            g = jnp.einsum('ecd,edf->ecf', xb, w_gate)
            u = jnp.einsum('ecd,edf->ecf', xb, w_up)
            h = jax.nn.silu(g) * u
            y = jnp.einsum('ecf,efd->ecd', h, w_down).reshape(E * C, -1)
            safe = jnp.where(valid, idx, 0)
            contrib = y[safe] * (flat_w * valid.astype(flat_w.dtype))[:, None]
            routed = jax.ops.segment_sum(contrib, tok, num_segments=T)
            routed = routed * ROUTED_SCALE
            gu = x @ ws_gate_up
            sg, su = (gu[:, :SF], gu[:, SF:])
            shared = jax.nn.silu(sg) * su @ ws_down
            return routed + shared
        key = jax.random.key(seed)
        ks = jax.random.split(key, 7)
        w = 0.02
        return {'hidden_states': jax.random.normal(ks[0], (B, S, D), jnp.float32), 'router_w': jax.random.normal(ks[1], (E, D), jnp.float32) * w, 'w_gate': jax.random.normal(ks[2], (E, D, F), jnp.float32) * w, 'w_up': jax.random.normal(ks[3], (E, D, F), jnp.float32) * w, 'w_down': jax.random.normal(ks[4], (E, F, D), jnp.float32) * w, 'ws_gate_up': jax.random.normal(ks[5], (D, 2 * SF), jnp.float32) * w, 'ws_down': jax.random.normal(ks[6], (SF, D), jnp.float32) * w}
    _L0_ffn_all = _L0_ffn_setup()
    _L0_ffn_in = {k: v for k, v in _L0_ffn_all.items() if k in ('router_w', 'w_gate', 'w_up', 'w_down', 'ws_gate_up', 'ws_down')}
    del _L0_ffn_all

    def _L1_xattn_setup():
        import jax, jax.numpy as jnp
        import numpy as np
        B, LQ, LKV = (8, 256, 512)
        QDIM, KDIM, HID = (256, 256, 256)
        key = jax.random.key(seed)
        ks = jax.random.split(key, 12)
        s = lambda d: 1.0 / np.sqrt(d)
        return {'query': jax.random.normal(ks[0], (B, LQ, QDIM), jnp.float32), 'key_value': jax.random.normal(ks[1], (B, LKV, KDIM), jnp.float32), 'key_mask': jax.random.randint(ks[2], (B, LKV), 0, 2).astype(bool), 'Wq': jax.random.uniform(ks[3], (QDIM, HID), jnp.float32, -s(QDIM), s(QDIM)), 'bq': jax.random.uniform(ks[4], (HID,), jnp.float32, -s(QDIM), s(QDIM)), 'Wk': jax.random.uniform(ks[5], (KDIM, HID), jnp.float32, -s(KDIM), s(KDIM)), 'bk': jax.random.uniform(ks[6], (HID,), jnp.float32, -s(KDIM), s(KDIM)), 'Wv': jax.random.uniform(ks[7], (KDIM, HID), jnp.float32, -s(KDIM), s(KDIM)), 'bv': jax.random.uniform(ks[8], (HID,), jnp.float32, -s(KDIM), s(KDIM)), 'Wo': jax.random.uniform(ks[9], (HID, QDIM), jnp.float32, -s(HID), s(HID)), 'bo': jax.random.uniform(ks[10], (QDIM,), jnp.float32, -s(HID), s(HID))}
    _L1_xattn_all = _L1_xattn_setup()
    _L1_xattn_in = {k: v for k, v in _L1_xattn_all.items() if k in ('Wq', 'bq', 'Wk', 'bk', 'Wv', 'bv', 'Wo', 'bo')}
    del _L1_xattn_all

    def _L1_ffn_setup():
        import jax, jax.numpy as jnp
        import numpy as np
        DIM = 256
        DEPTH = 2
        HEADS = 8
        DIM_HEAD = 64
        WINDOW = 128
        INNER = HEADS * DIM_HEAD
        HID = int(DIM * 4 * 2 / 3)
        B, N = (2, 2048)
        QK_SCALE = 8.0

        def shift_token(t):
            t1, t2 = jnp.split(t, 2, axis=-1)
            t2 = jnp.pad(t2, ((0, 0), (1, 0), (0, 0)))[:, :-1]
            return jnp.concatenate([t1, t2], axis=-1)

        def l2norm(t):
            return t / jnp.clip(jnp.linalg.norm(t, axis=-1, keepdims=True), 1e-12)

        def rotate_half(x):
            x1, x2 = jnp.split(x, 2, axis=-1)
            return jnp.concatenate([-x2, x1], axis=-1)

        def rotary_xpos(q, k):
            n = q.shape[-2]
            half_idx = jnp.arange(0, DIM_HEAD, 2, dtype=jnp.float32)
            inv_freq = 1.0 / 10000.0 ** (half_idx / DIM_HEAD)
            t = jnp.arange(n, dtype=jnp.float32)
            freqs = t[:, None] * inv_freq[None, :]
            freqs = jnp.concatenate([freqs, freqs], axis=-1)
            base = (half_idx + 0.4 * DIM_HEAD) / (1.4 * DIM_HEAD)
            power = (t - n // 2) / float(WINDOW // 2)
            scale = base[None, :] ** power[:, None]
            scale = jnp.concatenate([scale, scale], axis=-1)
            cos, sin = (jnp.cos(freqs), jnp.sin(freqs))
            q = q * cos * scale + rotate_half(q) * sin * scale
            k = k * cos / scale + rotate_half(k) * sin / scale
            return (q, k)

        def local_attention(q, k, v):
            b, h, n, d = q.shape
            w = n // WINDOW
            bq = q.reshape(b, h, w, WINDOW, d) * QK_SCALE
            bk = k.reshape(b, h, w, WINDOW, d)
            bv = v.reshape(b, h, w, WINDOW, d)

            def look_around(t):
                p = jnp.pad(t, ((0, 0), (0, 0), (1, 0), (0, 0), (0, 0)))
                return jnp.concatenate([p[:, :, :w], p[:, :, 1:]], axis=3)
            bk, bv = (look_around(bk), look_around(bv))
            bt = jnp.arange(n).reshape(w, WINDOW)
            btp = jnp.pad(bt, ((1, 0), (0, 0)), constant_values=-1)
            btk = jnp.concatenate([btp[:w], btp[1:]], axis=1)
            sim = jnp.einsum('bhwid,bhwjd->bhwij', bq, bk)
            i = bt[:, :, None]
            j = btk[:, None, :]
            mask = (i < j) | (i > j + WINDOW) | (j == -1)
            sim = jnp.where(mask, -jnp.finfo(sim.dtype).max, sim)
            attn = jax.nn.softmax(sim, axis=-1)
            out = jnp.einsum('bhwij,bhwjd->bhwid', attn, bv)
            return out.reshape(b, h, n, d)

        def _layer(x, wqkv, qs, ksc, wo, lg, lb, w1, b1, w2, b2):
            b, n, _ = x.shape
            h = shift_token(x)
            qkv = h @ wqkv
            q, k, v = jnp.split(qkv, 3, axis=-1)
            to_heads = lambda t: t.reshape(b, n, HEADS, DIM_HEAD).transpose(0, 2, 1, 3)
            q, k, v = (to_heads(q), to_heads(k), to_heads(v))
            q = l2norm(q) * qs
            k = l2norm(k) * ksc
            q, k = rotary_xpos(q, k)
            o = local_attention(q, k, v)
            o = o.transpose(0, 2, 1, 3).reshape(b, n, INNER)
            x = x + o @ wo
            h = shift_token(x)
            mu = h.mean(-1, keepdims=True)
            var = h.var(-1, keepdims=True)
            h = (h - mu) / jnp.sqrt(var + 1e-05) * lg + lb
            h = h @ w1 + b1
            a, g = jnp.split(h, 2, axis=-1)
            h = a * jax.nn.gelu(g, approximate=False)
            x = x + h @ w2 + b2
            return x
        key = jax.random.key(seed)
        ks = jax.random.split(key, 6)
        return {'x': jax.random.normal(ks[0], (B, N, DIM), jnp.float32), 'wqkv': jax.random.normal(ks[1], (DEPTH, DIM, 3 * INNER), jnp.float32) * 0.02, 'q_scale': jnp.ones((DEPTH, DIM_HEAD), jnp.float32), 'k_scale': jnp.ones((DEPTH, DIM_HEAD), jnp.float32), 'wo': jax.random.normal(ks[2], (DEPTH, INNER, DIM), jnp.float32) * 0.02, 'ln_g': jnp.ones((DEPTH, DIM), jnp.float32), 'ln_b': jnp.zeros((DEPTH, DIM), jnp.float32), 'w1': jax.random.normal(ks[3], (DEPTH, DIM, 2 * HID), jnp.float32) * 0.02, 'b1': jnp.zeros((DEPTH, 2 * HID), jnp.float32), 'w2': jax.random.normal(ks[4], (DEPTH, HID, DIM), jnp.float32) * 0.02, 'b2': jnp.zeros((DEPTH, DIM), jnp.float32)}
    _L1_ffn_all = _L1_ffn_setup()
    _L1_ffn_in = {k: v for k, v in _L1_ffn_all.items() if k in ('wqkv', 'q_scale', 'k_scale', 'wo', 'ln_g', 'ln_b', 'w1', 'b1', 'w2', 'b2')}
    del _L1_ffn_all

    def _L2_xattn_setup():
        import jax, jax.numpy as jnp
        import numpy as np
        EMBED_DIM = 256
        HEADS = 16
        HEAD_DIM = EMBED_DIM // HEADS
        key = jax.random.key(seed)
        ks = jax.random.split(key, 12)
        B, Sq, Sk, E = (4, 512, 512, EMBED_DIM)
        s = 1.0 / np.sqrt(E)
        return {'query': jax.random.normal(ks[0], (B, Sq, E), jnp.float32), 'key': jax.random.normal(ks[1], (B, Sk, E), jnp.float32), 'value': jax.random.normal(ks[2], (B, Sk, E), jnp.float32), 'Wq': jax.random.normal(ks[3], (E, E), jnp.float32) * s, 'bq': jnp.zeros((E,), jnp.float32), 'Wk': jax.random.normal(ks[4], (E, E), jnp.float32) * s, 'bk': jnp.zeros((E,), jnp.float32), 'Wv': jax.random.normal(ks[5], (E, E), jnp.float32) * s, 'bv': jnp.zeros((E,), jnp.float32), 'Wo': jax.random.normal(ks[6], (E, E), jnp.float32) * s, 'bo': jnp.zeros((E,), jnp.float32)}
    _L2_xattn_all = _L2_xattn_setup()
    _L2_xattn_in = {k: v for k, v in _L2_xattn_all.items() if k in ('Wq', 'bq', 'Wk', 'bk', 'Wv', 'bv', 'Wo', 'bo')}
    del _L2_xattn_all

    def _L2_ffn_setup():
        import math
        import jax, jax.numpy as jnp
        import numpy as np
        B, S, D, H, E, K = (4, 512, 256, 1024, 8, 2)
        CAPACITY_RATIO = 1.05
        key = jax.random.key(seed)
        k0, k1, k2, k3 = jax.random.split(key, 4)
        x = jax.random.normal(k0, (B, S, D), jnp.float32)
        Wg = jax.random.normal(k1, (D, E), jnp.float32) * 0.02
        W1 = jax.random.normal(k2, (E, D, H), jnp.float32) * 0.02
        b1 = jnp.zeros((E, H), jnp.float32)
        W2 = jax.random.normal(k3, (E, H, D), jnp.float32) * 0.02
        b2 = jnp.zeros((E, D), jnp.float32)
        return {'x': x, 'Wg': Wg, 'W1': W1, 'b1': b1, 'W2': W2, 'b2': b2}
    _L2_ffn_all = _L2_ffn_setup()
    _L2_ffn_in = {k: v for k, v in _L2_ffn_all.items() if k in ('Wg', 'W1', 'b1', 'W2', 'b2')}
    del _L2_ffn_all

    def _L3_xattn_setup():
        import jax, jax.numpy as jnp
        import numpy as np
        HEADS = 16
        DIM_HEAD = 64
        SCALE = DIM_HEAD ** (-0.5)

        def _split_heads(x):
            b, l, n = x.shape
            return x.reshape(b, l, HEADS, DIM_HEAD).transpose(0, 2, 1, 3)
        key = jax.random.key(seed)
        ks = jax.random.split(key, 6)
        B, L, D = (4, 512, 256)
        inner = HEADS * DIM_HEAD
        s = lambda fan_in: 1.0 / np.sqrt(fan_in)
        return {'x1': jax.random.normal(ks[0], (B, L, D), jnp.float32), 'x2': jax.random.normal(ks[1], (B, L, D), jnp.float32), 'Wq': jax.random.normal(ks[2], (D, inner), jnp.float32) * s(D), 'Wkv': jax.random.normal(ks[3], (D, 2 * inner), jnp.float32) * s(D), 'Wo': jax.random.normal(ks[4], (inner, D), jnp.float32) * s(inner), 'bo': jax.random.normal(ks[5], (D,), jnp.float32) * 0.02}
    _L3_xattn_all = _L3_xattn_setup()
    _L3_xattn_in = {k: v for k, v in _L3_xattn_all.items() if k in ('Wq', 'Wkv', 'Wo', 'bo')}
    del _L3_xattn_all

    def _L3_ffn_setup():
        import jax, jax.numpy as jnp
        import numpy as np
        B, T, D, H, E, K = (2, 512, 256, 1024, 8, 2)
        EPS = 1e-12

        def moe_forward(x, Wg, bg, W1, b1, W2, b2):
            gates = jax.nn.softmax(x @ Wg + bg, axis=-1)
            _, top_idx = jax.lax.top_k(gates, K)
            mask = jax.nn.one_hot(top_idx, E, dtype=gates.dtype).sum(axis=-2)
            g = gates * mask
            g = g / jnp.maximum(jnp.sum(jnp.abs(g), axis=-1, keepdims=True), EPS)
            h = jnp.einsum('btd,edh->bteh', x, W1) + b1[None, None]
            h = jax.nn.gelu(h, approximate=False)
            eo = jnp.einsum('bteh,ehd->bted', h, W2) + b2[None, None]
            return jnp.einsum('bte,bted->btd', g, eo)
        key = jax.random.key(seed)
        ks = jax.random.split(key, 8)
        s_d = 1.0 / np.sqrt(D)
        s_h = 1.0 / np.sqrt(H)
        return {'x': jax.random.normal(ks[0], (B, T, D), dtype=jnp.float32), 'Wg': jax.random.uniform(ks[1], (D, E), jnp.float32, -s_d, s_d), 'bg': jax.random.uniform(ks[2], (E,), jnp.float32, -s_d, s_d), 'W1': jax.random.uniform(ks[3], (E, D, H), jnp.float32, -s_d, s_d), 'b1': jax.random.uniform(ks[4], (E, H), jnp.float32, -s_d, s_d), 'W2': jax.random.uniform(ks[5], (E, H, D), jnp.float32, -s_h, s_h), 'b2': jax.random.uniform(ks[6], (E, D), jnp.float32, -s_h, s_h)}
    _L3_ffn_all = _L3_ffn_setup()
    _L3_ffn_in = {k: v for k, v in _L3_ffn_all.items() if k in ('Wg', 'bg', 'W1', 'b1', 'W2', 'b2')}
    del _L3_ffn_all
    return {'x': x, 'ctx_1024': ctx_1024, 'mask_BxSxS2_bk1': mask_BxSxS2_bk1, 'mask_BxS2_bk0': mask_BxS2_bk0, 'L0_xattn_Wq': _L0_xattn_in['Wq'], 'L0_xattn_bq': _L0_xattn_in['bq'], 'L0_xattn_Wk': _L0_xattn_in['Wk'], 'L0_xattn_bk': _L0_xattn_in['bk'], 'L0_xattn_Wv': _L0_xattn_in['Wv'], 'L0_xattn_bv': _L0_xattn_in['bv'], 'L0_xattn_Wo': _L0_xattn_in['Wo'], 'L0_xattn_bo': _L0_xattn_in['bo'], 'L0_ffn_router_w': _L0_ffn_in['router_w'], 'L0_ffn_w_gate': _L0_ffn_in['w_gate'], 'L0_ffn_w_up': _L0_ffn_in['w_up'], 'L0_ffn_w_down': _L0_ffn_in['w_down'], 'L0_ffn_ws_gate_up': _L0_ffn_in['ws_gate_up'], 'L0_ffn_ws_down': _L0_ffn_in['ws_down'], 'L1_xattn_Wq': _L1_xattn_in['Wq'], 'L1_xattn_bq': _L1_xattn_in['bq'], 'L1_xattn_Wk': _L1_xattn_in['Wk'], 'L1_xattn_bk': _L1_xattn_in['bk'], 'L1_xattn_Wv': _L1_xattn_in['Wv'], 'L1_xattn_bv': _L1_xattn_in['bv'], 'L1_xattn_Wo': _L1_xattn_in['Wo'], 'L1_xattn_bo': _L1_xattn_in['bo'], 'L1_ffn_wqkv': _L1_ffn_in['wqkv'], 'L1_ffn_q_scale': _L1_ffn_in['q_scale'], 'L1_ffn_k_scale': _L1_ffn_in['k_scale'], 'L1_ffn_wo': _L1_ffn_in['wo'], 'L1_ffn_ln_g': _L1_ffn_in['ln_g'], 'L1_ffn_ln_b': _L1_ffn_in['ln_b'], 'L1_ffn_w1': _L1_ffn_in['w1'], 'L1_ffn_b1': _L1_ffn_in['b1'], 'L1_ffn_w2': _L1_ffn_in['w2'], 'L1_ffn_b2': _L1_ffn_in['b2'], 'L2_xattn_Wq': _L2_xattn_in['Wq'], 'L2_xattn_bq': _L2_xattn_in['bq'], 'L2_xattn_Wk': _L2_xattn_in['Wk'], 'L2_xattn_bk': _L2_xattn_in['bk'], 'L2_xattn_Wv': _L2_xattn_in['Wv'], 'L2_xattn_bv': _L2_xattn_in['bv'], 'L2_xattn_Wo': _L2_xattn_in['Wo'], 'L2_xattn_bo': _L2_xattn_in['bo'], 'L2_ffn_Wg': _L2_ffn_in['Wg'], 'L2_ffn_W1': _L2_ffn_in['W1'], 'L2_ffn_b1': _L2_ffn_in['b1'], 'L2_ffn_W2': _L2_ffn_in['W2'], 'L2_ffn_b2': _L2_ffn_in['b2'], 'L3_xattn_Wq': _L3_xattn_in['Wq'], 'L3_xattn_Wkv': _L3_xattn_in['Wkv'], 'L3_xattn_Wo': _L3_xattn_in['Wo'], 'L3_xattn_bo': _L3_xattn_in['bo'], 'L3_ffn_Wg': _L3_ffn_in['Wg'], 'L3_ffn_bg': _L3_ffn_in['bg'], 'L3_ffn_W1': _L3_ffn_in['W1'], 'L3_ffn_b1': _L3_ffn_in['b1'], 'L3_ffn_W2': _L3_ffn_in['W2'], 'L3_ffn_b2': _L3_ffn_in['b2']}

def reference(x, ctx_1024, mask_BxSxS2_bk1, mask_BxS2_bk0, L0_xattn_Wq, L0_xattn_bq, L0_xattn_Wk, L0_xattn_bk, L0_xattn_Wv, L0_xattn_bv, L0_xattn_Wo, L0_xattn_bo, L0_ffn_router_w, L0_ffn_w_gate, L0_ffn_w_up, L0_ffn_w_down, L0_ffn_ws_gate_up, L0_ffn_ws_down, L1_xattn_Wq, L1_xattn_bq, L1_xattn_Wk, L1_xattn_bk, L1_xattn_Wv, L1_xattn_bv, L1_xattn_Wo, L1_xattn_bo, L1_ffn_wqkv, L1_ffn_q_scale, L1_ffn_k_scale, L1_ffn_wo, L1_ffn_ln_g, L1_ffn_ln_b, L1_ffn_w1, L1_ffn_b1, L1_ffn_w2, L1_ffn_b2, L2_xattn_Wq, L2_xattn_bq, L2_xattn_Wk, L2_xattn_bk, L2_xattn_Wv, L2_xattn_bv, L2_xattn_Wo, L2_xattn_bo, L2_ffn_Wg, L2_ffn_W1, L2_ffn_b1, L2_ffn_W2, L2_ffn_b2, L3_xattn_Wq, L3_xattn_Wkv, L3_xattn_Wo, L3_xattn_bo, L3_ffn_Wg, L3_ffn_bg, L3_ffn_W1, L3_ffn_b1, L3_ffn_W2, L3_ffn_b2):
    import jax
    import jax.numpy as jnp

    def _L0_xattn_ref(q, k, v, mask, Wq, bq, Wk, bk, Wv, bv, Wo, bo):
        import jax, jax.numpy as jnp
        import numpy as np
        B, S, D_MODEL, N_HEAD = (4, 512, 256, 16)
        D_HEAD = D_MODEL // N_HEAD
        D_Q = D_K = D_V = 64
        Bq, Sq, _ = q.shape
        H = Wq.shape[0]
        qh = q.reshape(Bq, Sq, H, -1)
        kh = k.reshape(k.shape[0], k.shape[1], H, -1)
        vh = v.reshape(v.shape[0], v.shape[1], H, -1)
        Q = jnp.einsum('bshd,hde->bhse', qh, Wq) + bq[None, :, None, :]
        K = jnp.einsum('bshd,hde->bhse', kh, Wk) + bk[None, :, None, :]
        V = jnp.einsum('bshd,hde->bhse', vh, Wv) + bv[None, :, None, :]
        scale = 1.0 / jnp.sqrt(jnp.asarray(Q.shape[-1], Q.dtype))
        scores = jnp.einsum('bhqe,bhke->bhqk', Q, K) * scale
        scores = jnp.where(mask[:, None, :, :], jnp.asarray(-1000000000.0, scores.dtype), scores)
        attn = jax.nn.softmax(scores, axis=-1)
        ctx = jnp.einsum('bhqk,bhkv->bqhv', attn, V)
        ctx = ctx.reshape(Bq, Sq, -1)
        return ctx @ Wo.T + bo

    def _L0_ffn_ref(hidden_states, router_w, w_gate, w_up, w_down, ws_gate_up, ws_down):
        import jax, jax.numpy as jnp
        import numpy as np
        B, S, D = (1, 512, 256)
        E, K, F = (64, 8, 192)
        SF = 192
        C = 128
        ROUTED_SCALE = 1.0

        def _moe_forward(x, router_w, w_gate, w_up, w_down, ws_gate_up, ws_down):
            T = x.shape[0]
            logits = x.astype(jnp.float32) @ router_w.T
            probs = jax.nn.softmax(logits, axis=-1)
            topk_w, topk_ids = jax.lax.top_k(probs, K)
            topk_w = topk_w / jnp.sum(topk_w, axis=-1, keepdims=True)
            topk_w = topk_w.astype(x.dtype)
            N = T * K
            flat_e = topk_ids.reshape(-1)
            flat_w = topk_w.reshape(-1)
            tok = jnp.arange(N) // K
            onehot = flat_e[:, None] == jnp.arange(E)[None, :]
            pos = jnp.cumsum(onehot, axis=0)[jnp.arange(N), flat_e] - 1
            valid = pos < C
            idx = jnp.where(valid, flat_e * C + pos, E * C)
            x_buf = jnp.zeros((E * C + 1, x.shape[1]), x.dtype).at[idx].set(x[tok])
            xb = x_buf[:E * C].reshape(E, C, -1)
            g = jnp.einsum('ecd,edf->ecf', xb, w_gate)
            u = jnp.einsum('ecd,edf->ecf', xb, w_up)
            h = jax.nn.silu(g) * u
            y = jnp.einsum('ecf,efd->ecd', h, w_down).reshape(E * C, -1)
            safe = jnp.where(valid, idx, 0)
            contrib = y[safe] * (flat_w * valid.astype(flat_w.dtype))[:, None]
            routed = jax.ops.segment_sum(contrib, tok, num_segments=T)
            routed = routed * ROUTED_SCALE
            gu = x @ ws_gate_up
            sg, su = (gu[:, :SF], gu[:, SF:])
            shared = jax.nn.silu(sg) * su @ ws_down
            return routed + shared
        b, s, d = hidden_states.shape
        x = hidden_states.reshape(-1, d)
        out = _moe_forward(x, router_w, w_gate, w_up, w_down, ws_gate_up, ws_down)
        return out.reshape(b, s, d)

    def _L1_xattn_ref(query, key_value, key_mask, Wq, bq, Wk, bk, Wv, bv, Wo, bo):
        import jax, jax.numpy as jnp
        import numpy as np
        B, LQ, LKV = (8, 256, 512)
        QDIM, KDIM, HID = (256, 256, 256)
        Q = query @ Wq + bq
        K = key_value @ Wk + bk
        V = key_value @ Wv + bv
        hid = Q.shape[-1]
        scores = jnp.einsum('bqh,bkh->bqk', Q, K) / jnp.sqrt(jnp.float32(hid))
        scores = jnp.where(key_mask[:, None, :], scores, jnp.float32(-1000000000.0))
        attn = jax.nn.softmax(scores, axis=-1)
        context = jnp.einsum('bqk,bkh->bqh', attn, V)
        return context @ Wo + bo

    def _L1_ffn_ref(x, wqkv, q_scale, k_scale, wo, ln_g, ln_b, w1, b1, w2, b2):
        import jax, jax.numpy as jnp
        import numpy as np
        DIM = 256
        DEPTH = 2
        HEADS = 8
        DIM_HEAD = 64
        WINDOW = 128
        INNER = HEADS * DIM_HEAD
        HID = int(DIM * 4 * 2 / 3)
        B, N = (2, 2048)
        QK_SCALE = 8.0

        def shift_token(t):
            t1, t2 = jnp.split(t, 2, axis=-1)
            t2 = jnp.pad(t2, ((0, 0), (1, 0), (0, 0)))[:, :-1]
            return jnp.concatenate([t1, t2], axis=-1)

        def l2norm(t):
            return t / jnp.clip(jnp.linalg.norm(t, axis=-1, keepdims=True), 1e-12)

        def rotate_half(x):
            x1, x2 = jnp.split(x, 2, axis=-1)
            return jnp.concatenate([-x2, x1], axis=-1)

        def rotary_xpos(q, k):
            n = q.shape[-2]
            half_idx = jnp.arange(0, DIM_HEAD, 2, dtype=jnp.float32)
            inv_freq = 1.0 / 10000.0 ** (half_idx / DIM_HEAD)
            t = jnp.arange(n, dtype=jnp.float32)
            freqs = t[:, None] * inv_freq[None, :]
            freqs = jnp.concatenate([freqs, freqs], axis=-1)
            base = (half_idx + 0.4 * DIM_HEAD) / (1.4 * DIM_HEAD)
            power = (t - n // 2) / float(WINDOW // 2)
            scale = base[None, :] ** power[:, None]
            scale = jnp.concatenate([scale, scale], axis=-1)
            cos, sin = (jnp.cos(freqs), jnp.sin(freqs))
            q = q * cos * scale + rotate_half(q) * sin * scale
            k = k * cos / scale + rotate_half(k) * sin / scale
            return (q, k)

        def local_attention(q, k, v):
            b, h, n, d = q.shape
            w = n // WINDOW
            bq = q.reshape(b, h, w, WINDOW, d) * QK_SCALE
            bk = k.reshape(b, h, w, WINDOW, d)
            bv = v.reshape(b, h, w, WINDOW, d)

            def look_around(t):
                p = jnp.pad(t, ((0, 0), (0, 0), (1, 0), (0, 0), (0, 0)))
                return jnp.concatenate([p[:, :, :w], p[:, :, 1:]], axis=3)
            bk, bv = (look_around(bk), look_around(bv))
            bt = jnp.arange(n).reshape(w, WINDOW)
            btp = jnp.pad(bt, ((1, 0), (0, 0)), constant_values=-1)
            btk = jnp.concatenate([btp[:w], btp[1:]], axis=1)
            sim = jnp.einsum('bhwid,bhwjd->bhwij', bq, bk)
            i = bt[:, :, None]
            j = btk[:, None, :]
            mask = (i < j) | (i > j + WINDOW) | (j == -1)
            sim = jnp.where(mask, -jnp.finfo(sim.dtype).max, sim)
            attn = jax.nn.softmax(sim, axis=-1)
            out = jnp.einsum('bhwij,bhwjd->bhwid', attn, bv)
            return out.reshape(b, h, n, d)

        def _layer(x, wqkv, qs, ksc, wo, lg, lb, w1, b1, w2, b2):
            b, n, _ = x.shape
            h = shift_token(x)
            qkv = h @ wqkv
            q, k, v = jnp.split(qkv, 3, axis=-1)
            to_heads = lambda t: t.reshape(b, n, HEADS, DIM_HEAD).transpose(0, 2, 1, 3)
            q, k, v = (to_heads(q), to_heads(k), to_heads(v))
            q = l2norm(q) * qs
            k = l2norm(k) * ksc
            q, k = rotary_xpos(q, k)
            o = local_attention(q, k, v)
            o = o.transpose(0, 2, 1, 3).reshape(b, n, INNER)
            x = x + o @ wo
            h = shift_token(x)
            mu = h.mean(-1, keepdims=True)
            var = h.var(-1, keepdims=True)
            h = (h - mu) / jnp.sqrt(var + 1e-05) * lg + lb
            h = h @ w1 + b1
            a, g = jnp.split(h, 2, axis=-1)
            h = a * jax.nn.gelu(g, approximate=False)
            x = x + h @ w2 + b2
            return x
        for l in range(DEPTH):
            x = _layer(x, wqkv[l], q_scale[l], k_scale[l], wo[l], ln_g[l], ln_b[l], w1[l], b1[l], w2[l], b2[l])
        return x

    def _L2_xattn_ref(query, key, value, Wq, bq, Wk, bk, Wv, bv, Wo, bo):
        import jax, jax.numpy as jnp
        import numpy as np
        EMBED_DIM = 256
        HEADS = 16
        HEAD_DIM = EMBED_DIM // HEADS
        B, Sq, E = query.shape
        Sk = key.shape[1]
        H, D = (HEADS, HEAD_DIM)
        Q = (query @ Wq + bq).reshape(B, Sq, H, D).transpose(0, 2, 1, 3)
        K = (key @ Wk + bk).reshape(B, Sk, H, D).transpose(0, 2, 1, 3)
        V = (value @ Wv + bv).reshape(B, Sk, H, D).transpose(0, 2, 1, 3)
        scores = jnp.einsum('bhqd,bhkd->bhqk', Q, K) / jnp.sqrt(jnp.float32(D))
        attn = jax.nn.softmax(scores, axis=-1)
        out = jnp.einsum('bhqk,bhkd->bhqd', attn, V)
        out = out.transpose(0, 2, 1, 3).reshape(B, Sq, E)
        return out @ Wo + bo

    def _L2_ffn_ref(x, Wg, W1, b1, W2, b2):
        import math
        import jax, jax.numpy as jnp
        import numpy as np
        B, S, D, H, E, K = (4, 512, 256, 1024, 8, 2)
        CAPACITY_RATIO = 1.05
        b, s, d = x.shape
        e = Wg.shape[1]
        n = b * s
        cap = int(math.ceil(n * K / e * CAPACITY_RATIO))
        xf = x.reshape(n, d)
        probs = jax.nn.softmax(xf @ Wg, axis=-1)
        topv, topi = jax.lax.top_k(probs, K)
        gates = topv / jnp.sum(topv, axis=-1, keepdims=True)
        eidx = topi.reshape(-1)
        oh = jax.nn.one_hot(eidx, e, dtype=jnp.int32)
        pos = jnp.sum(jnp.cumsum(oh, axis=0) * oh, axis=-1) - 1
        keep = pos < cap
        dest = jnp.where(keep, eidx * cap + pos, e * cap)
        xr = jnp.repeat(xf, K, axis=0)
        buf = jnp.zeros((e * cap + 1, d), x.dtype).at[dest].set(xr)
        expert_in = buf[:e * cap].reshape(e, cap, d)
        h = jax.nn.gelu(jnp.einsum('ecd,edh->ech', expert_in, W1) + b1[:, None, :])
        y = jnp.einsum('ech,ehd->ecd', h, W2) + b2[:, None, :]
        yf = jnp.concatenate([y.reshape(e * cap, d), jnp.zeros((1, d), y.dtype)], axis=0)
        gathered = yf[dest]
        w = (gates.reshape(-1) * keep.astype(gates.dtype))[:, None]
        out = (gathered * w).reshape(n, K, d).sum(axis=1).reshape(b, s, d)
        return out

    def _L3_xattn_ref(x1, x2, Wq, Wkv, Wo, bo):
        import jax, jax.numpy as jnp
        import numpy as np
        HEADS = 16
        DIM_HEAD = 64
        SCALE = DIM_HEAD ** (-0.5)

        def _split_heads(x):
            b, l, n = x.shape
            return x.reshape(b, l, HEADS, DIM_HEAD).transpose(0, 2, 1, 3)
        q = x1 @ Wq
        kv = x2 @ Wkv
        k, v = jnp.split(kv, 2, axis=-1)
        q, k, v = map(_split_heads, (q, k, v))
        attn = jnp.einsum('bhid,bhjd->bhij', q, k) * SCALE
        attn = jax.nn.softmax(attn, axis=-1)
        out = jnp.einsum('bhij,bhjd->bhid', attn, v)
        b, h, l, d = out.shape
        out = out.transpose(0, 2, 1, 3).reshape(b, l, h * d)
        return out @ Wo + bo

    def _L3_ffn_ref(x, Wg, bg, W1, b1, W2, b2):
        import jax, jax.numpy as jnp
        import numpy as np
        B, T, D, H, E, K = (2, 512, 256, 1024, 8, 2)
        EPS = 1e-12

        def moe_forward(x, Wg, bg, W1, b1, W2, b2):
            gates = jax.nn.softmax(x @ Wg + bg, axis=-1)
            _, top_idx = jax.lax.top_k(gates, K)
            mask = jax.nn.one_hot(top_idx, E, dtype=gates.dtype).sum(axis=-2)
            g = gates * mask
            g = g / jnp.maximum(jnp.sum(jnp.abs(g), axis=-1, keepdims=True), EPS)
            h = jnp.einsum('btd,edh->bteh', x, W1) + b1[None, None]
            h = jax.nn.gelu(h, approximate=False)
            eo = jnp.einsum('bteh,ehd->bted', h, W2) + b2[None, None]
            return jnp.einsum('bte,bted->btd', g, eo)
        return moe_forward(x, Wg, bg, W1, b1, W2, b2)
    x = x + _L0_xattn_ref(_layernorm(x, axis=-1), ctx_1024, ctx_1024, mask_BxSxS2_bk1, L0_xattn_Wq, L0_xattn_bq, L0_xattn_Wk, L0_xattn_bk, L0_xattn_Wv, L0_xattn_bv, L0_xattn_Wo, L0_xattn_bo)
    x = x + _L0_ffn_ref(_layernorm(x, axis=-1), L0_ffn_router_w, L0_ffn_w_gate, L0_ffn_w_up, L0_ffn_w_down, L0_ffn_ws_gate_up, L0_ffn_ws_down)
    x = x + _L1_xattn_ref(_layernorm(x, axis=-1), ctx_1024, mask_BxS2_bk0, L1_xattn_Wq, L1_xattn_bq, L1_xattn_Wk, L1_xattn_bk, L1_xattn_Wv, L1_xattn_bv, L1_xattn_Wo, L1_xattn_bo)
    x = x + _L1_ffn_ref(_layernorm(x, axis=-1), L1_ffn_wqkv, L1_ffn_q_scale, L1_ffn_k_scale, L1_ffn_wo, L1_ffn_ln_g, L1_ffn_ln_b, L1_ffn_w1, L1_ffn_b1, L1_ffn_w2, L1_ffn_b2)
    x = x + _L2_xattn_ref(_layernorm(x, axis=-1), ctx_1024, ctx_1024, L2_xattn_Wq, L2_xattn_bq, L2_xattn_Wk, L2_xattn_bk, L2_xattn_Wv, L2_xattn_bv, L2_xattn_Wo, L2_xattn_bo)
    x = x + _L2_ffn_ref(_layernorm(x, axis=-1), L2_ffn_Wg, L2_ffn_W1, L2_ffn_b1, L2_ffn_W2, L2_ffn_b2)
    x = x + _L3_xattn_ref(_layernorm(x, axis=-1), ctx_1024, L3_xattn_Wq, L3_xattn_Wkv, L3_xattn_Wo, L3_xattn_bo)
    x = x + _L3_ffn_ref(_layernorm(x, axis=-1), L3_ffn_Wg, L3_ffn_bg, L3_ffn_W1, L3_ffn_b1, L3_ffn_W2, L3_ffn_b2)
    return x

_drawn_inputs = setup_inputs


def setup_inputs(seed=0):
    import zlib

    import numpy as np

    out = dict(_drawn_inputs(seed))
    spreads = {'L1_ffn_q_scale': (1.0, 0.6),
     'L1_ffn_k_scale': (1.0, 0.6),
     'L1_ffn_ln_g': (1.0, 0.6),
     'L1_ffn_ln_b': (0.0, 0.8),
     'L1_ffn_b1': (0.0, 0.8),
     'L1_ffn_b2': (0.0, 0.516),
     'L2_xattn_bq': (0.0, 2.0),
     'L2_xattn_bk': (0.0, 2.0),
     'L2_xattn_bv': (0.0, 0.8),
     'L2_xattn_bo': (0.0, 0.8),
     'L2_ffn_b1': (0.0, 2.0),
     'L2_ffn_b2': (0.0, 1.569)}
    factors = {'L0_xattn_bk': 64.0,
     'L0_ffn_router_w': 8.0,
     'L0_ffn_w_gate': 8.0,
     'L0_ffn_w_up': 8.0,
     'L0_ffn_w_down': 8.0,
     'L0_ffn_ws_gate_up': 6.845,
     'L0_ffn_ws_down': 7.207,
     'L1_xattn_Wq': 3.999,
     'L1_xattn_bq': 64.0,
     'L1_xattn_Wk': 2.906,
     'L1_xattn_bk': 64.0,
     'L1_xattn_bv': 21.264,
     'L1_xattn_bo': 11.041,
     'L1_ffn_w1': 3.561,
     'L1_ffn_w2': 3.452,
     'L2_ffn_W1': 8.872,
     'L3_xattn_bo': 32.486,
     'L3_ffn_bg': 47.967,
     'L3_ffn_b1': 64.0,
     'L3_ffn_b2': 52.36,
     'L2_xattn_Wq': 2.68,
     'L3_xattn_Wq': 3.098,
     'L3_ffn_Wg': 4.413,
     'L3_ffn_W1': 4.785,
     'L3_ffn_W2': 4.185}
    for name, (base, spread) in spreads.items():
        noise = np.random.default_rng([zlib.crc32(name.encode()), seed]).standard_normal(out[name].shape)
        drawn = base * np.exp(spread * noise) if base else spread * noise
        out[name] = jnp.asarray(drawn.astype(out[name].dtype))
    for name, factor in factors.items():
        out[name] = (out[name] * factor).astype(out[name].dtype)
    return out
```

```python
from contextlib import ExitStack

import numpy as np
import concourse.bass as bass
from concourse import mybir

F32 = mybir.dt.float32
BF16 = mybir.dt.bfloat16
U8 = mybir.dt.uint8
U32 = mybir.dt.uint32
I32 = mybir.dt.int32
ALU = mybir.AluOpType
ACT = mybir.ActivationFunctionType
AX = mybir.AxisListType.X

P = 128
B, S, D = 2, 1024, 256
T = B * S // P
TB = S // P
J = 77
DC = D // P
LN_EPS = 1e-5
MASKED = -1e9


class Steps:

    def __init__(self, sem, *names):
        self.sem, self.names, self.n = sem, names, len(names)

    def at(self, t, name):
        return (t + 2) * self.n + self.names.index(name) + 1


def row(a, t):
    return a[:, bass.ts(t, 1), :].rearrange("p o m -> p (o m)")


def col(a, t):
    return a[:, bass.ts(t, 1)]


def stand_alone(eng, waited):
    eng.sem_inc(waited, 1)


def reuse(eng, sems, t, u, per=1):
    if not isinstance(t, int) or t >= 2:
        eng.wait_ge(sems[u], (t - u) * (8 * per))


def pipeline(eng, n, *phases, peel=0):
    lead = max(lag for lag, _ in phases) + peel
    lead += lead % 2

    def step(s, u):
        for lag, body in phases:
            if not isinstance(s, int) or 0 <= s - lag < n:
                body(s - lag, (u - lag) % 2)

    for s in range(lead):
        step(s, s % 2)
    pairs = max(n - lead, 0) // 2
    if pairs:
        with eng.Fori(0, pairs, 1) as i:
            for u in range(2):
                step(i * 2 + (lead + u), u)
    for s in range(lead + 2 * pairs, n + max(lag for lag, _ in phases)):
        step(s, s % 2)


class Shared:
    pass


class Scope:

    def __init__(self, k, ctx, name):
        self.k, self.nc, self.ctx, self.name = k, k.nc, ctx, name

    def sb(self, name, shape, dt=F32):
        return self.ctx.enter_context(self.nc.sbuf_tensor(f"{self.name}_{name}", shape, dt))

    def pair(self, name, shape, dt=F32):
        return [self.sb(f"{name}{u}", shape, dt) for u in range(2)]

    def bank(self, name, width=512):
        return self.ctx.enter_context(self.nc.psum_tensor(f"{self.name}_{name}_bank", [P, width], F32))

    def sem(self, name):
        handle = self.k.stage_sems.enter_context(self.nc.semaphore(f"{self.name}_{name}"))
        self.k.stage_sem_numbers.append(handle.num)
        return handle

    def lasting_sems(self, name, n=2):
        return [self.k.ctx.enter_context(self.nc.semaphore(f"{self.name}_{name}{u}")) for u in range(n)]

    def sems(self, name, n=2):
        return [self.sem(f"{name}{u}") for u in range(n)]

    def steps(self, name, *names):
        return Steps(self.sem(name), *(names or (name,)))



def norm_scales(nc, k):
    old, numbers = k.stage_sems, sorted(k.stage_sem_numbers)
    k.stage_sems, k.stage_sem_numbers = ExitStack(), []
    sc = Scope(k, k.ctx, f"n{k.stage}")
    k.stage += 1
    runs = [[n, n + 1] for n in numbers if n - 1 not in numbers]
    for r in runs:
        while r[1] in numbers:
            r[1] += 1
    aggregated, rooted = sc.sem("aggregated"), sc.sem("rooted")
    inverted = sc.sem("inverted")
    with nc.Block() as block:
        @block.sync
        def _(sp):
            for n0, n1 in runs:
                sp.sem_clear(range(n0, n1))

        @block.vector
        def _(dve):
            for t in range(T):
                nc.vector.bn_aggr(k.mv[:, t, :], k.stats[:, t, :]).then_inc(aggregated, 1)
            dve.wait_ge(aggregated, T)
            nc.vector.tensor_scalar(k.var[:, :], k.mv[:, :, 1], LN_EPS, None, ALU.add).then_inc(aggregated, 1)
            nc.vector.tensor_copy(k.mean[:, :], k.mv[:, :, 0]).then_inc(aggregated, 1)
            dve.wait_ge(rooted, 1)
            nc.vector.reciprocal(k.rstd[:, :], k.std[:, :]).then_inc(inverted, 1)
            dve.wait_ge(inverted, 1)

        @block.scalar
        def _(act):
            act.wait_ge(aggregated, T + 1)
            nc.scalar.activation(k.std[:, :], k.var[:, :], ACT.Sqrt).then_inc(rooted, 1)
    old.close()



class Attention:

    def __init__(self, name, heads, nslot, w, parts, scale, blocks=None, mask=None):
        self.name, self.heads, self.nslot, self.w, self.parts, self.scale = name, heads, nslot, w, parts, scale
        self.hj = heads * J
        self.blocks = blocks or [range(DC)] * heads
        self.mask = mask
        self.chunks = [(c, min(P, self.hj - c)) for c in range(0, self.hj, P)]
        self.groups = [(h, min(h + 6, heads)) for h in range(0, heads, 6)]


HALVES = [[(h // 2, 64 * (h % 2), 64 * (h % 2) + 64)] for h in range(16)]
ATTENTIONS = [
    Attention("a0", 16, 8, 128, HALVES, 1 / 8, blocks=[[h // 8] for h in range(16)], mask="tokens"),
    Attention("a1", 1, 2, 128, [[(0, 0, 128), (1, 0, 128)]], 1 / 16, mask="keys"),
    Attention("a2", 16, 16, 16, [[(h, 0, 16)] for h in range(16)], 1 / 4),
    Attention("a3", 16, 8, 128, HALVES, 1 / 8),
]


class Folded:

    def __init__(self, nc, a):
        self.nrow = B * a.hj + D
        self.fold = nc.dram_tensor(f"{a.name}_dram_fold", (P, a.heads, B, DC, J), F32, kind="Internal").ap()
        self.vw = nc.dram_tensor(f"{a.name}_dram_vw", (B, a.hj, D), F32, kind="Internal").ap()
        self.row = nc.dram_tensor(f"{a.name}_dram_row", (self.nrow,), F32, kind="Internal").ap()
        self.parts = nc.dram_tensor(f"{a.name}_dram_parts", (3, self.nrow), BF16, kind="Internal").ap()


def fold_contexts(nc, k, s, block, jobs, direct=None):
    tensors = []
    for a, d in jobs:
        n, w = a.nslot, a.w
        j = Shared()
        j.a, j.d, j.n, j.w, j.out = a, d, n, w, k.folded[a.name]
        j.wk, j.wv = s.sb(a.name + "wk", [P, DC, n * w]), s.sb(a.name + "wv", [P, DC, n * w])
        j.wq, j.wo = s.sb(a.name + "wq", [w, n, D]), s.sb(a.name + "wo", [w, n, D])
        j.bk, j.bv, j.bq, j.bks = (s.sb(a.name + x, [w, n]) for x in ("bk", "bv", "bq", "bks"))
        j.kt, j.vt = s.sb(a.name + "kt", [w, n, B * J]), s.sb(a.name + "vt", [w, n, B * J])
        rows = max(p for p in range(1, P + 1) if j.out.nrow % p == 0)
        cols = j.out.nrow // rows
        j.row, j.rest, j.rest2 = (s.sb(a.name + x, [rows, cols]) for x in ("row", "rest", "rest2"))
        j.parts = [s.sb(f"{a.name}part{i}", [rows, cols], BF16) for i in range(3)]
        j.loaded = s.sem(a.name + "loaded")
        tensors.append(j)
    fold_out, row_out, vw_out = s.pair("foldout", [P, B, DC, J]), s.pair("rowout", [1, B, J]), s.pair("vwout", [J, B, D])
    kv_ps = [s.bank(f"kv{i}") for i in range(2)]
    a_ps, v_ps = [s.bank(f"a{i}") for i in range(3)], [s.bank(f"v{i}") for i in range(3)]
    projected, kv_done, bias_scaled = s.sem("projected"), s.sem("kvdone"), s.sem("bscaled")
    folded, row_copied, vw_made, vw_copied = s.sem("folded"), s.sem("rowcopied"), s.sem("vwmade"), s.sem("vwcopied")
    stored = s.sems("stored")
    bo_in, row_in, split, parts_out = s.sem("boin"), s.sem("rowin"), s.sem("split"), s.sem("partsout")
    per = 2 if direct is not None else 3
    heads = [(j, h) for j in tensors for h in range(j.a.heads)]

    @block.sync
    def _(sp):
        for j in tensors:
            sp.dma_start(j.wk[:, :, :], j.d["wk"].rearrange("(c p) n -> p c n", p=P)).then_inc(j.loaded, 16)
            sp.dma_start(j.wv[:, :, :], j.d["wv"].rearrange("(c p) n -> p c n", p=P)).then_inc(j.loaded, 16)
            for t, src in ((j.bk, "bk"), (j.bv, "bv"), (j.bq, "bq")):
                sp.dma_start(t[:, :], j.d[src]).then_inc(j.loaded, 16)
            for t, src in ((j.wq, "wq"), (j.wo, "wo")):
                sp.dma_start(t[:, :, :], j.d[src]).then_inc(j.loaded, 16)
            sp.dma_start(j.out.row[B * j.a.hj:].unsqueeze(0), j.d["bo"]).then_inc(bo_in, 16)
        for i, (j, h) in enumerate(heads):
            sp.wait_ge(row_copied, i + 1)
            if direct is None:
                sp.dma_start(j.out.fold[:, h], fold_out[i % 2][:, :, :, :]).then_inc(stored[i % 2], 16)
            sp.dma_start(j.out.row[0:B * j.a.hj].unsqueeze(0).rearrange("o (b j) -> o b j", b=B)[:, :, h * J:(h + 1) * J],
                         row_out[i % 2][:, :, :]).then_inc(stored[i % 2], 16)
            sp.wait_ge(vw_copied, i + 1)
            sp.dma_start(j.out.vw[:, h * J:(h + 1) * J, :].rearrange("b j d -> j b d"),
                         vw_out[i % 2][:, :, :]).then_inc(stored[i % 2], 16)
        for u in range(2):
            if len(heads) > u:
                sp.wait_ge(stored[u], 16 * per * ((len(heads) - u + 1) // 2))
        sp.wait_ge(bo_in, 16 * len(tensors))
        for i, j in enumerate(tensors):
            rows = j.row.shape[0]
            sp.dma_start(j.row[:, :], j.out.row.rearrange("(p n) -> p n", p=rows)).then_inc(row_in, 16)
        for i, j in enumerate(tensors):
            sp.wait_ge(split, 5 * (i + 1))
            rows = j.row.shape[0]
            for x in range(3):
                sp.dma_start(j.out.parts[x].rearrange("(p n) -> p n", p=rows), j.parts[x][:, :]).then_inc(parts_out, 16)
        sp.wait_ge(parts_out, 48 * len(tensors))

    @block.tensor
    def _(pe):
        slots, n_heads = 0, 0
        for j in tensors:
            a, n, w = j.a, j.n, j.w
            pe.wait_ge(j.loaded, 16 * 7)
            first = slots
            for i in range(n):
                ps = kv_ps[slots % 2]
                if slots >= 2:
                    pe.wait_ge(kv_done, slots - 1)
                for half, wt in enumerate((j.wk, j.wv)):
                    for c in range(DC):
                        last = nc.tensor.matmul(ps[0:w, half * 256:half * 256 + B * J], wt[:, c, i * w:(i + 1) * w],
                                                k.ctx_t[:, c, :], start=c == 0, stop=c == DC - 1)
                last.then_inc(projected, 1)
                slots += 1
            for h in range(a.heads):
                ps, vps = a_ps[n_heads % 3], v_ps[n_heads % 3]
                pe.wait_ge(kv_done, first + a.parts[h][-1][0] + 1)
                if n_heads >= 3:
                    pe.wait_ge(row_copied, n_heads - 2)
                for c in [*a.blocks[h], DC]:
                    m = P if c < DC else 1
                    for i, (slot, p0, p1) in enumerate(a.parts[h]):
                        lhs = j.wq[p0:p1, slot, c * P:(c + 1) * P] if c < DC else j.bq[p0:p1, slot:slot + 1]
                        last = nc.tensor.matmul(ps[0:m, c * 160:c * 160 + B * J], lhs, j.kt[p0:p1, slot, :],
                                                start=i == 0, stop=i == len(a.parts[h]) - 1)
                last.then_inc(folded, 1)
                if n_heads >= 3:
                    pe.wait_ge(vw_copied, n_heads - 2)
                for b in range(B):
                    for i, (slot, p0, p1) in enumerate(a.parts[h]):
                        last = nc.tensor.matmul(vps[0:J, b * D:(b + 1) * D], j.vt[p0:p1, slot, b * J:(b + 1) * J],
                                                j.wo[p0:p1, slot, :], start=i == 0, stop=i == len(a.parts[h]) - 1)
                last.then_inc(vw_made, 1)
                n_heads += 1

    @block.scalar
    def _(act):
        slots, n_heads = 0, 0
        for i, j in enumerate(tensors):
            a = j.a
            act.wait_ge(j.loaded, 16 * 7)
            nc.scalar.mul(j.bks[:, :], j.bk[:, :], a.scale).then_inc(bias_scaled, 1)
            act.wait_ge(bias_scaled, i + 1)
            for slot in range(j.n):
                ps = kv_ps[slots % 2]
                act.wait_ge(projected, slots + 1)
                nc.scalar.activation(j.kt[:, slot, :], ps[0:j.w, 0:B * J], ACT.Identity, bias=j.bks[:, slot:slot + 1], scale=a.scale)
                nc.scalar.activation(j.vt[:, slot, :], ps[0:j.w, 256:256 + B * J], ACT.Identity,
                                     bias=j.bv[:, slot:slot + 1]).then_inc(kv_done, 1)
                slots += 1
            for h in range(a.heads):
                u, ps, vps = n_heads % 2, a_ps[n_heads % 3], v_ps[n_heads % 3]
                act.wait_ge(folded, n_heads + 1)
                if n_heads >= 2:
                    act.wait_ge(stored[u], 16 * per * (n_heads // 2))
                for c in a.blocks[h]:
                    to = direct[:, h, :, c, :] if direct is not None else fold_out[u][:, :, c, :]
                    nc.scalar.copy(to, ps[:, c * 160:c * 160 + B * J].rearrange("p (b j) -> p b j", b=B))
                nc.scalar.copy(row_out[u][:, :, :], ps[0:1, DC * 160:DC * 160 + B * J].rearrange("p (b j) -> p b j", b=B)).then_inc(row_copied, 1)
                act.wait_ge(vw_made, n_heads + 1)
                nc.scalar.copy(vw_out[u][:, :, :], vps[0:J, :].rearrange("p (b d) -> p b d", b=B)).then_inc(vw_copied, 1)
                n_heads += 1

    @block.vector
    def _(dve):
        dve.wait_ge(row_in, 16 * len(tensors))
        for i, j in enumerate(tensors):
            n = 5 * i
            nc.vector.tensor_copy(j.parts[0][:, :], j.row[:, :]).then_inc(split, 1)
            dve.wait_ge(split, n + 1)
            nc.vector.tensor_tensor(j.rest[:, :], j.row[:, :], j.parts[0][:, :], ALU.subtract).then_inc(split, 1)
            dve.wait_ge(split, n + 2)
            nc.vector.tensor_copy(j.parts[1][:, :], j.rest[:, :]).then_inc(split, 1)
            dve.wait_ge(split, n + 3)
            nc.vector.tensor_tensor(j.rest2[:, :], j.rest[:, :], j.parts[1][:, :], ALU.subtract).then_inc(split, 1)
            dve.wait_ge(split, n + 4)
            nc.vector.tensor_copy(j.parts[2][:, :], j.rest2[:, :]).then_inc(split, 1)


def zero_slot_buffers(nc, k, block):
    k.buffers_zeroed = True

    @block.gpsimd
    def _(pool):
        for xbuf, zeroed, n in k.slot_buffers.values():
            for i in range(n):
                pool.dma_start(xbuf[i * 512:(i + 1) * 512, :].rearrange("(p a) d -> p (a d)", p=P), k.zeros[:, :]).then_inc(zeroed, 16)


def attention(nc, k, a, d):
    norm_scales(nc, k)
    first = a.name not in k.folded
    with ExitStack() as ctx:
        s = Scope(k, ctx, a.name)
        nch, ngr = len(a.chunks), len(a.groups)
        fold = s.sb("fold", [P, a.heads, B, DC, J])
        vw = s.sb("vw", [P, B, nch, D])
        c3 = s.sb("c3", [3, B * a.hj + D], BF16)
        if first:
            k.folded[a.name] = Folded(nc, a)
            with ExitStack() as fold_ctx:
                with nc.Block() as block:
                    fold_contexts(nc, k, Scope(k, fold_ctx, a.name + "f"), block, [(a, d)], direct=fold)
        src = k.folded[a.name]
        fold_in, vw_in, c3_in = s.sem("foldin"), s.sem("vwin"), s.sem("c3in")

        xn, xn_t = s.pair("xn", [P, D]), s.pair("xnt", [P, DC, P])
        probs, probs_t = s.pair("probs", [P, a.hj]), s.pair("probst", [P, nch, P])
        mx, total, inv = s.pair("mx", [P, a.heads]), s.pair("total", [P, a.heads]), s.pair("inv", [P, a.heads])
        turned_ps, out_ps = s.bank("turned"), s.bank("out")
        score_ps = [s.bank(f"score{g}") for g in range(3)]
        pt_ps = [s.bank(f"pt{g}") for g in range(3)]
        quads = [range(q, min(q + 4, nch)) for q in range(0, nch, 4)]
        if a.mask:
            masked = s.sb("masked", [P, 6 * J])
            drop = s.pair("drop", [P, J], U8)
            mask_in = s.sems("maskin")
            keys = s.sb("keys", [P, B, J], U8)
            factor, addend = s.sb("factor", [P, B, J]), s.sb("addend", [P, B, J])
            ready = s.sem("maskready")
            waited = s.sem("waited")

        normed = s.steps("normed")
        turned = s.steps("turned")
        copied = s.steps("copied")
        scored = s.steps("scored", *(f"g{g}" for g in range(ngr)))
        masking = s.steps("masking", *(("mul", "add") if a.mask == "keys" else (f"g{g}" for g in range(ngr))))
        softmax = s.steps("softmax", *(f"{w}{g}" for g in range(ngr) for w in ("max", "sub")))
        exped = s.steps("exped", *(f"g{g}" for g in range(ngr)))
        scaled = s.steps("scaled", "sum", "inv", "probs")
        p_turned = s.steps("pturned", *(f"q{q}" for q in range(len(quads))))
        p_copied = s.steps("pcopied", *(f"q{q}" for q in range(len(quads))))
        mixed = s.steps("mixed")
        added = s.steps("added", "x", "stats")

        def heads3(ap, g):
            h0, h1 = a.groups[g]
            return ap[:, h0 * J:h1 * J].rearrange("p (h j) -> p h j", j=J)

        def over_keys(ap, h0, h1):
            return ap[:, h0:h1].unsqueeze(2).broadcast_to([P, h1 - h0, J])

        with nc.Block() as block:
            if not k.buffers_zeroed:
                zero_slot_buffers(nc, k, block)

            @block.sync
            def _(sp):
                sp.dma_start(c3[:, :], src.parts).then_inc(c3_in, 16)
                if not first:
                    sp.dma_start(fold[:, :, :, :, :], src.fold).then_inc(fold_in, 16)
                for c, (c0, rows) in enumerate(a.chunks):
                    sp.dma_start(vw[0:rows, :, c, :], src.vw[:, c0:c0 + rows, :].rearrange("b p d -> p b d")).then_inc(vw_in, 16)
                if a.mask == "tokens":
                    for u in range(2):
                        sp.sem_inc(mask_in[u], 16)

                    def load(t, u):
                        sp.wait_ge(masking.sem, masking.at(t - 2, masking.names[-1]))
                        sp.dma_start(drop[u][:, :], d["mask"][bass.ts(t, P), :]).then_inc(mask_in[u], 16)
                    pipeline(sp, T, (0, load))
                if a.mask == "keys":
                    sp.dma_start(keys[:, :, :], d["mask"].partition_broadcast(P)).then_inc(mask_in[0], 16)

            @block.vector
            def _(dve):
                for st in (normed, masking, softmax, scaled, added):
                    dve.sem_inc(st.sem, 2 * st.n)
                if a.mask:
                    nc.vector.memset(masked[:, :], MASKED).then_inc(ready, 1)
                    dve.wait_ge(ready, 1)
                if a.mask == "keys":
                    dve.wait_ge(mask_in[0], 16)
                    nc.vector.tensor_scalar(factor[:, :, :], keys[:, :, :], 0.0, None, ALU.not_equal).then_inc(ready, 1)
                    nc.vector.tensor_scalar(addend[:, :, :], keys[:, :, :], 0.0, MASKED, ALU.is_equal, ALU.mult).then_inc(ready, 1)
                    dve.wait_ge(ready, 3)

                def norm(t, u):
                    dve.wait_ge(turned.sem, turned.at(t - 2, "turned"))
                    nc.vector.tensor_scalar(xn[u][:, :], row(k.x, t), col(k.mean, t), col(k.rstd, t),
                                            ALU.subtract, ALU.mult).then_inc(normed.sem, 1)

                def maxima(t, u):
                    for g, (h0, h1) in enumerate(a.groups):
                        ps = score_ps[g][:, 0:(h1 - h0) * J].rearrange("p (h j) -> p h j", j=J)
                        dve.wait_ge(scored.sem, scored.at(t, f"g{g}"))
                        if a.mask == "tokens":
                            if g == 0:
                                dve.wait_ge(mask_in[u], (t - u) * 8 + 32)
                            stand_alone(dve, waited)
                            nc.vector.copy_predicated(
                                ps, drop[u][:, :].unsqueeze(1).broadcast_to([P, h1 - h0, J]),
                                masked[:, 0:(h1 - h0) * J].rearrange("p (h j) -> p h j", j=J)).then_inc(masking.sem, 1)
                            dve.wait_ge(masking.sem, masking.at(t, f"g{g}"))
                        if a.mask == "keys":
                            ps = score_ps[0][:, 0:J]
                            nc.vector.tensor_tensor(ps, ps, row(factor, t // TB), ALU.mult).then_inc(masking.sem, 1)
                            dve.wait_ge(masking.sem, masking.at(t, "mul"))
                            nc.vector.tensor_tensor(ps, ps, row(addend, t // TB), ALU.add).then_inc(masking.sem, 1)
                            dve.wait_ge(masking.sem, masking.at(t, "add"))
                            ps = ps.unsqueeze(1)
                        nc.vector.tensor_reduce(mx[u][:, h0:h1], ps, AX, ALU.max).then_inc(softmax.sem, 1)
                        dve.wait_ge(softmax.sem, softmax.at(t, f"max{g}"))
                        if g == 0:
                            dve.wait_ge(p_turned.sem, p_turned.at(t - 2, p_turned.names[-1]))
                        nc.vector.tensor_tensor(heads3(probs[u], g), ps, over_keys(mx[u], h0, h1),
                                                ALU.subtract).then_inc(softmax.sem, 1)

                def scale(t, u):
                    dve.wait_ge(exped.sem, exped.at(t, exped.names[-1]))
                    p3 = probs[u][:, :].rearrange("p (h j) -> p h j", j=J)
                    nc.vector.tensor_reduce(total[u][:, :], p3, AX, ALU.add).then_inc(scaled.sem, 1)
                    dve.wait_ge(scaled.sem, scaled.at(t, "sum"))
                    nc.vector.reciprocal(inv[u][:, :], total[u][:, :]).then_inc(scaled.sem, 1)
                    dve.wait_ge(scaled.sem, scaled.at(t, "inv"))
                    nc.vector.tensor_tensor(p3, p3, over_keys(inv[u], 0, a.heads), ALU.mult).then_inc(scaled.sem, 1)

                def add(t, u):
                    dve.wait_ge(mixed.sem, mixed.at(t, "mixed"))
                    nc.vector.tensor_tensor(row(k.x, t), row(k.x, t), out_ps[:, 0:D], ALU.add).then_inc(added.sem, 1)
                    dve.wait_ge(added.sem, added.at(t, "x"))
                    nc.vector.bn_stats(row(k.stats, t), row(k.x, t)).then_inc(added.sem, 1)

                pipeline(dve, T, (0, norm), (1, maxima), (2, add), (1, scale))

            @block.scalar
            def _(act):
                for st in (copied, exped, p_copied):
                    act.sem_inc(st.sem, 2 * st.n)

                def copy_x(t, u):
                    act.wait_ge(turned.sem, turned.at(t, "turned"))
                    act.wait_ge(scored.sem, scored.at(t - 2, scored.names[-1]))
                    nc.scalar.copy(xn_t[u][:, :, :], turned_ps[:, 0:D].rearrange("p (c n) -> p c n", c=DC)).then_inc(copied.sem, 1)

                def exp(t, u):
                    for g in range(ngr):
                        act.wait_ge(softmax.sem, softmax.at(t, f"sub{g}"))
                        h0, h1 = a.groups[g]
                        nc.scalar.activation(probs[u][:, h0 * J:h1 * J], probs[u][:, h0 * J:h1 * J], ACT.Exp).then_inc(exped.sem, 1)

                def copy_p(t, u):
                    for q, cs in enumerate(quads):
                        act.wait_ge(p_turned.sem, p_turned.at(t, f"q{q}"))
                        if q == 0:
                            act.wait_ge(mixed.sem, mixed.at(t - 2, "mixed"))
                        whole = [c for c in cs if a.chunks[c][1] == P]
                        last = None
                        if whole:
                            last = nc.scalar.copy(probs_t[u][:, whole[0]:whole[-1] + 1, :],
                                                  pt_ps[q][:, 0:len(whole) * P].rearrange("p (c n) -> p c n", n=P))
                        for c in cs:
                            if a.chunks[c][1] < P:
                                n = a.chunks[c][1]
                                last = nc.scalar.copy(probs_t[u][0:n, c, :], pt_ps[q][0:n, (c - cs[0]) * P:(c - cs[0] + 1) * P])
                        last.then_inc(p_copied.sem, 1)

                pipeline(act, T, (0, copy_x), (1, exp), (1, copy_p))

            @block.tensor
            def _(pe):
                for st in (turned, scored, p_turned, mixed):
                    pe.sem_inc(st.sem, 2 * st.n)

                def turn(t, u):
                    pe.wait_ge(normed.sem, normed.at(t, "normed"))
                    pe.wait_ge(copied.sem, copied.at(t - 1, "copied"))
                    for c in range(DC):
                        last = nc.tensor.transpose(turned_ps[:, c * P:(c + 1) * P], xn[u][:, c * P:(c + 1) * P], k.ident[:, :])
                    last.then_inc(turned.sem, 1)

                def score(t, u):
                    pe.wait_ge(copied.sem, copied.at(t, "copied"))
                    b = t // TB
                    if isinstance(t, int) and t == 0:
                        pe.wait_ge(c3_in, 16)
                        if not first:
                            pe.wait_ge(fold_in, 16)
                    for g, (h0, h1) in enumerate(a.groups):
                        width = (h1 - h0) * J
                        pe.wait_ge(softmax.sem, softmax.at(t - 1, f"sub{g}"))
                        nc.tensor.matmul(score_ps[g][:, 0:width], k.ones3[:, :], c3[:, bass.ds(b * a.hj + h0 * J, width)],
                                         start=True, stop=False, skip_group_check=True)
                        for c in range(DC):
                            hs = [h for h in range(h0, h1) if c in a.blocks[h]]
                            if hs:
                                last = nc.tensor.matmul(score_ps[g][:, (hs[0] - h0) * J:(hs[-1] + 1 - h0) * J].rearrange("p (h j) -> p h j", j=J),
                                                        xn_t[u][:, c, :], fold[:, hs[0]:hs[-1] + 1, bass.ds(b, 1), c, :].rearrange("p h o j -> p h (o j)"),
                                                        start=False, stop=True, skip_group_check=True)
                        last.then_inc(scored.sem, 1)

                def turn_p(t, u):
                    pe.wait_ge(scaled.sem, scaled.at(t, "probs"))
                    for q, cs in enumerate(quads):
                        pe.wait_ge(p_copied.sem, p_copied.at(t - 1, f"q{q}"))
                        for c in cs:
                            c0, n = a.chunks[c]
                            last = nc.tensor.transpose(pt_ps[q][0:n, (c - cs[0]) * P:(c - cs[0] + 1) * P],
                                                       probs[u][:, c0:c0 + n], k.ident[:, :])
                        last.then_inc(p_turned.sem, 1)

                def mix(t, u):
                    b = t // TB
                    if isinstance(t, int) and t == 0:
                        pe.wait_ge(vw_in, 16 * nch)
                    pe.wait_ge(added.sem, added.at(t - 1, "x"))
                    nc.tensor.matmul(out_ps[:, 0:D], k.ones3[:, :], c3[:, B * a.hj:], start=True, stop=False)
                    for q, cs in enumerate(quads):
                        pe.wait_ge(p_copied.sem, p_copied.at(t, f"q{q}"))
                        for c in cs:
                            n = a.chunks[c][1]
                            last = nc.tensor.matmul(out_ps[:, 0:D], probs_t[u][0:n, c, :],
                                                    vw[0:n, bass.ds(b, 1), c, :].rearrange("p o n -> p (o n)"),
                                                    start=False, stop=c == nch - 1)
                    last.then_inc(mixed.sem, 1)

                pipeline(pe, T, (0, turn), (0, score), (1, turn_p), (1, mix))



class Experts:

    def __init__(self, name, e, top, hidden, cap, stride, ntiles, act, group):
        self.name, self.e, self.top, self.hidden, self.cap, self.stride = name, e, top, hidden, cap, stride
        self.ntiles, self.act, self.group = ntiles, act, group
        self.rows = ntiles * P


M0 = Experts("m0", 64, 8, 192, 128, 128, 64, ACT.Silu, 4)
M2 = Experts("m2", 8, 2, 1024, 538, 640, 40, ACT.Gelu_apprx_tanh, 8)
M3 = Experts("m3", 8, 2, 1024, None, None, 2 * T + 8, ACT.Gelu, 8)
NOWHERE = 100000.0
TOP_EPS = 1e-12


def route(nc, k, m, d, r):
    shared = m is M0
    E, K, G = m.e, m.top, m.group
    groups = T // G
    F = m.hidden
    HC, HP = 2, F // 2
    N = G * P
    with ExitStack() as ctx:
        s = Scope(k, ctx, m.name + "r")
        xn, xn_t = s.pair("xn", [P, D]), s.pair("xnt", [P, DC, P])
        bias = s.sb("bias", [P, E])
        lg, pr = s.sb("lg", [P, T, E]), s.sb("pr", [P, G, E])
        mx, tot, inv = s.sb("mx", [P, G]), s.sb("tot", [P, G]), s.sb("inv", [P, G])
        top, idx, idxf = s.sb("top", [P, G, 8]), s.sb("idx", [P, G, 8], U32), s.sb("idxf", [P, G, K])
        onehot, picked = s.sb("onehot", [P, G, K, E]), s.sb("picked", [P, G, K, E])
        mask, cum = s.pair("mask", [P, G, E]), s.pair("cum", [P, G + 1, E])
        pos, over, kept, slotf = (s.sb(n, [P, G, K]) for n in ("pos", "over", "kept", "slotf"))
        tsum, tmax, tinv, wk = s.sb("tsum", [P, G]), s.sb("tmax", [P, G]), s.sb("tinv", [P, G]), s.sb("wk", [P, G, K])
        y_ps, pos_ps = [s.bank("y0"), s.bank("y1")], s.bank("pos")
        gu_ps = s.bank("gu", 2048)
        turned_ps, logit_ps = [gu_ps[:, u * 512:(u + 1) * 512] for u in range(2)], y_ps
        if shared:
            wgu, wd = s.sb("wgu", [P, DC, 2 * F]), s.sb("wd", [HP, HC, D])
            xn_all = s.sb("xnall", [P, DC, T * P])
            gate, h_t = s.sb("gate", [HP, HC, N]), s.pair("ht", [HP, HC, N])
        if m.cap is not None:
            xs, slot = s.pair("xs", [P, G, D]), s.pair("slot", [P, G, K], U32)
        loaded, cleared, waited, pool_waited = s.sem("loaded"), s.sem("cleared"), s.sem("waited"), s.sem("poolwaited")
        scattered = s.lasting_sems("scattered")
        nload = 2 * shared + (m.cap is None)

        normed, turned, copied, scored, logged = (s.steps(n) for n in ("normed", "turned", "copied", "scored", "logged"))
        shifted, exped = s.steps("shifted", "max", "sub"), s.steps("exped")
        ranked = s.steps("ranked", "sum", "inv", "prob", "top", "idx", "idxf", "onehot", "mask", *(f"cum{j}" for j in range(G)))
        counted = s.steps("counted")
        placed = s.steps("placed", "picked", "pos", "tsum", "tmax", "tinv", "wk", "kept", "over", "slotf", "slot", "rows", "slots", "weights")
        gu_made, gated, hidden, y_made, added = (s.steps(n) for n in ("gumade", "gated", "hidden", "ymade", "added"))

        def per_e(ap):
            return ap.rearrange("p g k -> p (g k)").unsqueeze(2).broadcast_to([P, G * K, E])

        with nc.Block() as block:
            @block.sync
            def _(sp):
                if m.cap is None:
                    sp.dma_start(bias[:, :], d["bg"].partition_broadcast(P)).then_inc(loaded, 16)
                if shared:
                    sp.dma_start(wgu[:, :, :], d["sgu"].rearrange("(c p) f -> p c f", p=P)).then_inc(loaded, 16)
                    sp.dma_start(wd[:, :, :], d["sd"].rearrange("(c p) f -> p c f", p=HP)).then_inc(loaded, 16)
                if m is not M0:
                    sp.dma_start(r.b1[:, :], d["b1"]).then_inc(r.w_in, 16)
                    sp.dma_start(r.b2[:, :, :].rearrange("p e f -> p (e f)"), d["b2"].partition_broadcast(P)).then_inc(r.w_in, 16)
                    for e in range(E):
                        sp.dma_start(r.w1[:, e, :, :], d["w1"][e].rearrange("(c p) f -> p c f", p=P)).then_inc(r.w_in, 16)
                        sp.dma_start(r.w2[:, e, :, :], d["w2"][e].rearrange("(c p) f -> p c f", p=P)).then_inc(r.w_in, 16)

            @block.gpsimd
            def _(pool):
                if m.cap is None:
                    return
                pool.wait_ge(r.zeroed, 16 * r.nzero)

                def scatter(c, u):
                    pool.wait_ge(placed.sem, placed.at(c, "rows"))
                    stand_alone(pool, pool_waited)
                    for j in range(G):
                        for i in range(K):
                            nc.gpsimd.indirect_dma_start(r.xbuf[:, :], bass.IndirectOffsetOnAxis(slot[u][:, j, i:i + 1], 0), xs[u][:, j, :], None,
                                                         bounds_check=m.rows - 1, oob_is_err=False).then_inc(scattered[u], 16)
                pipeline(pool, groups, (0, scatter))
                for u in range(2):
                    pool.wait_ge(scattered[u], 16 * G * K * (groups // 2))

            @block.vector
            def _(dve):
                for st in (normed, logged, shifted, ranked, placed, hidden, added):
                    dve.sem_inc(st.sem, 2 * st.n)
                nc.vector.memset(cum[0][:, 0, :], 0.0).then_inc(cleared, 1)
                if nload:
                    dve.wait_ge(loaded, 16 * nload)
                dve.wait_ge(cleared, 1)

                def norm(t, u):
                    dve.wait_ge(turned.sem, turned.at(t - 2, "turned"))
                    nc.vector.tensor_scalar(xn[u][:, :], row(k.x, t), col(k.mean, t), col(k.rstd, t),
                                            ALU.subtract, ALU.mult).then_inc(normed.sem, 1)

                def log(t, u):
                    dve.wait_ge(scored.sem, scored.at(t, "scored"))
                    if m.cap is None:
                        nc.vector.tensor_tensor(row(lg, t), logit_ps[u][:, 0:E], bias[:, :], ALU.add).then_inc(logged.sem, 1)
                    else:
                        nc.vector.tensor_copy(row(lg, t), logit_ps[u][:, 0:E]).then_inc(logged.sem, 1)
                pipeline(dve, T, (0, norm), (2, log))
                dve.wait_ge(logged.sem, logged.at(T - 1, "logged"))

                def rank(c, u):
                    def done(name):
                        dve.wait_ge(ranked.sem, ranked.at(c, name))
                    lgc = lg[:, bass.ts(c, G), :]
                    nc.vector.tensor_reduce(mx[:, :], lgc, AX, ALU.max).then_inc(shifted.sem, 1)
                    dve.wait_ge(shifted.sem, shifted.at(c, "max"))
                    nc.vector.tensor_tensor(lgc, lgc, mx[:, :].unsqueeze(2).broadcast_to([P, G, E]), ALU.subtract).then_inc(shifted.sem, 1)
                    dve.wait_ge(exped.sem, exped.at(c, "exped"))
                    nc.vector.tensor_reduce(tot[:, :], pr[:, :, :], AX, ALU.add).then_inc(ranked.sem, 1)
                    done("sum")
                    nc.vector.reciprocal(inv[:, :], tot[:, :]).then_inc(ranked.sem, 1)
                    done("inv")
                    nc.vector.tensor_tensor(pr[:, :, :], pr[:, :, :], inv[:, :].unsqueeze(2).broadcast_to([P, G, E]), ALU.mult).then_inc(ranked.sem, 1)
                    done("prob")
                    stand_alone(dve, waited)
                    for j in range(G):
                        last = nc.vector.max(top[:, j, :], pr[:, j, :])
                    last.then_inc(ranked.sem, 1)
                    done("top")
                    stand_alone(dve, waited)
                    for j in range(G):
                        last = nc.vector.max_index(idx[:, j, :], top[:, j, :], pr[:, j, :])
                    last.then_inc(ranked.sem, 1)
                    done("idx")
                    nc.vector.tensor_copy(idxf[:, :, :], idx[:, :, 0:K]).then_inc(ranked.sem, 1)
                    done("idxf")
                    nc.vector.tensor_tensor(onehot[:, :, :, :].rearrange("p g k e -> p (g k) e"),
                                            r.iota[:, 0:E].unsqueeze(1).broadcast_to([P, G * K, E]), per_e(idxf[:, :, :]), ALU.is_equal).then_inc(ranked.sem, 1)
                    done("onehot")
                    nc.vector.tensor_reduce(mask[u][:, :, :], onehot[:, :, :, :].rearrange("p g k e -> p g e k"), AX, ALU.add).then_inc(ranked.sem, 1)
                    done("mask")
                    dve.wait_ge(counted.sem, counted.at(c - 1, "counted"))
                    for j in range(G):
                        after = cum[u][:, j + 1, :] if j < G - 1 else cum[1 - u][:, 0, :]
                        nc.vector.tensor_tensor(after, cum[u][:, j, :], mask[u][:, j, :], ALU.add).then_inc(ranked.sem, 1)
                        done(f"cum{j}")

                def place(c, u):
                    def done(name):
                        dve.wait_ge(placed.sem, placed.at(c, name))
                    dve.wait_ge(counted.sem, counted.at(c, "counted"))
                    for j in range(G):
                        last = nc.vector.tensor_tensor(picked[:, j, :, :], onehot[:, j, :, :],
                                                       pos_ps[:, j * E:(j + 1) * E].unsqueeze(1).broadcast_to([P, K, E]), ALU.mult)
                    last.then_inc(placed.sem, 1)
                    done("picked")
                    nc.vector.tensor_reduce(pos[:, :, :].rearrange("p g k -> p (g k)"), picked[:, :, :, :].rearrange("p g k e -> p (g k) e"),
                                            AX, ALU.add).then_inc(placed.sem, 1)
                    nc.vector.tensor_reduce(tsum[:, :], top[:, :, 0:K], AX, ALU.add).then_inc(placed.sem, 1)
                    done("tsum")
                    nc.vector.tensor_scalar(tmax[:, :], tsum[:, :], TOP_EPS, None, ALU.max).then_inc(placed.sem, 1)
                    done("tmax")
                    nc.vector.reciprocal(tinv[:, :], tmax[:, :]).then_inc(placed.sem, 1)
                    done("tinv")
                    nc.vector.tensor_tensor(wk[:, :, :], top[:, :, 0:K], tinv[:, :].unsqueeze(2).broadcast_to([P, G, K]), ALU.mult).then_inc(placed.sem, 1)
                    cap = float(m.cap or B * S + 1)
                    nc.vector.tensor_scalar(kept[:, :, :], pos[:, :, :], cap, None, ALU.is_lt).then_inc(placed.sem, 1)
                    nc.vector.tensor_scalar(over[:, :, :], pos[:, :, :], cap, NOWHERE, ALU.is_ge, ALU.mult).then_inc(placed.sem, 1)
                    done("over")
                    nc.vector.scalar_tensor_tensor(slotf[:, :, :], idxf[:, :, :], float(m.stride or 0), pos[:, :, :],
                                                   ALU.mult, ALU.add).then_inc(placed.sem, 1)
                    done("slotf")
                    if m.cap is None:
                        nc.vector.tensor_copy(r.idxf[:, bass.ts(c, G), :], idxf[:, :, :]).then_inc(placed.sem, 1)
                        nc.vector.tensor_copy(r.pos[:, bass.ts(c, G), :], pos[:, :, :]).then_inc(placed.sem, 2)
                    else:
                        reuse(dve, scattered, c, u, G * K)
                        nc.vector.tensor_tensor(slot[u][:, :, :], slotf[:, :, :], over[:, :, :], ALU.add).then_inc(placed.sem, 1)
                        for j in range(G):
                            last = nc.vector.tensor_scalar(xs[u][:, j, :], row(k.x, c * G + j), col(k.mean, c * G + j), col(k.rstd, c * G + j),
                                                           ALU.subtract, ALU.mult)
                        last.then_inc(placed.sem, 1)
                        done("slot")
                        nc.vector.tensor_copy(r.slots[:, bass.ts(c, G), :], slot[u][:, :, :]).then_inc(placed.sem, 1)
                    nc.vector.tensor_tensor(r.weights[:, bass.ts(c, G), :], wk[:, :, :], kept[:, :, :], ALU.mult).then_inc(placed.sem, 1)

                def hide(c, u):
                    dve.wait_ge(gated.sem, gated.at(c, "gated"))
                    dve.wait_ge(y_made.sem, y_made.at(c - 2, "ymade"))
                    nc.vector.tensor_tensor(h_t[u][:, :, :].rearrange("p h n -> p (h n)"), gate[:, :, :].rearrange("p h n -> p (h n)"),
                                            gu_ps[0:HP, 1024:2048], ALU.mult).then_inc(hidden.sem, 1)

                def add(c, u):
                    dve.wait_ge(y_made.sem, y_made.at(c, "ymade"))
                    for i in range(2):
                        xi = k.x[:, bass.ts(c * 2 + i, G // 2), :].rearrange("p t d -> p (t d)")
                        last = nc.vector.tensor_tensor(xi, xi, y_ps[i][:, 0:G // 2 * D], ALU.add)
                    last.then_inc(added.sem, 1)

                if shared:
                    pipeline(dve, groups, (0, rank), (0, place), (1, hide), (1, add), peel=2)
                else:
                    pipeline(dve, groups, (0, rank), (0, place), peel=2)
                dve.wait_ge(placed.sem, placed.at(groups - 1, "weights"))

            @block.scalar
            def _(act):
                for st in (copied, exped, gated):
                    act.sem_inc(st.sem, 2 * st.n)

                def copy_x(t, u):
                    act.wait_ge(turned.sem, turned.at(t, "turned"))
                    act.wait_ge(scored.sem, scored.at(t - 2, "scored"))
                    x_t = turned_ps[u][:, 0:D].rearrange("p (c n) -> p c n", c=DC)
                    if shared:
                        nc.scalar.copy(xn_all[:, :, bass.ts(t, P)], x_t)
                    nc.scalar.copy(xn_t[u][:, :, :], x_t).then_inc(copied.sem, 1)
                pipeline(act, T, (0, copy_x))

                def exp(c, u):
                    act.wait_ge(shifted.sem, shifted.at(c, "sub"))
                    act.wait_ge(ranked.sem, ranked.at(c - 1, "idx"))
                    nc.scalar.activation(pr[:, :, :], lg[:, bass.ts(c, G), :], ACT.Exp).then_inc(exped.sem, 1)

                def silu(c, u):
                    act.wait_ge(gu_made.sem, gu_made.at(c, "gumade"))
                    act.wait_ge(hidden.sem, hidden.at(c - 1, "hidden"))
                    nc.scalar.activation(gate[:, :, :].rearrange("p h n -> p (h n)"), gu_ps[0:HP, 0:1024], ACT.Silu).then_inc(gated.sem, 1)

                pipeline(act, groups, *([(0, exp)] + [(0, silu)] * shared))

            @block.tensor
            def _(pe):
                for st in (turned, scored, counted, gu_made, y_made):
                    pe.sem_inc(st.sem, 2 * st.n)
                pe.wait_ge(cleared, 1)

                def turn(t, u):
                    pe.wait_ge(normed.sem, normed.at(t, "normed"))
                    pe.wait_ge(copied.sem, copied.at(t - 2, "copied"))
                    for c in range(DC):
                        last = nc.tensor.transpose(turned_ps[u][:, c * P:(c + 1) * P], xn[u][:, c * P:(c + 1) * P], k.ident[:, :])
                    last.then_inc(turned.sem, 1)

                def score(t, u):
                    pe.wait_ge(copied.sem, copied.at(t, "copied"))
                    pe.wait_ge(logged.sem, logged.at(t - 2, "logged"))
                    for c in range(DC):
                        last = nc.tensor.matmul(logit_ps[u][:, 0:E], xn_t[u][:, c, :], r.wr[:, c, :], start=c == 0, stop=c == DC - 1)
                    last.then_inc(scored.sem, 1)
                pipeline(pe, T, (0, turn), (1, score))

                def gate_up(c, u):
                    pe.wait_ge(copied.sem, copied.at(T - 1, "copied"))
                    pe.wait_ge(hidden.sem, hidden.at(c - 1, "hidden"))
                    for i in range(2 * HC):
                        for dc in range(DC):
                            last = nc.tensor.matmul(gu_ps[0:HP, i * 512:(i + 1) * 512], wgu[:, dc, i * HP:(i + 1) * HP], xn_all[:, dc, bass.ts(c, N)],
                                                    start=dc == 0, stop=dc == DC - 1)
                    last.then_inc(gu_made.sem, 1)

                def count(c, u):
                    pe.wait_ge(ranked.sem, ranked.at(c, f"cum{G - 1}"))
                    pe.wait_ge(placed.sem, placed.at(c - 1, "picked"))
                    nc.tensor.matmul(pos_ps[:, 0:G * E], r.before[:, :], mask[u][:, :, :].rearrange("p g e -> p (g e)"), start=True, stop=False)
                    nc.tensor.matmul(pos_ps[:, 0:G * E], r.ones[:, :], cum[u][:, 0:G, :].rearrange("p g e -> p (g e)"), start=False, stop=True).then_inc(counted.sem, 1)

                def down(c, u):
                    pe.wait_ge(hidden.sem, hidden.at(c, "hidden"))
                    pe.wait_ge(added.sem, added.at(c - 1, "added"))
                    for j in range(G):
                        for h in range(HC):
                            last = nc.tensor.matmul(y_ps[j // 2][:, j % 2 * D:(j % 2 + 1) * D], h_t[u][:, h, j * P:(j + 1) * P], wd[:, h, :],
                                                    start=h == 0, stop=h == HC - 1)
                    last.then_inc(y_made.sem, 1)

                if nload:
                    pe.wait_ge(loaded, 16 * nload)
                if shared:
                    pipeline(pe, groups, (0, count), (0, gate_up), (1, down))
                else:
                    pipeline(pe, groups, (0, count))
                    if m.cap is None:
                        pe.wait_ge(placed.sem, placed.at(groups - 1, "picked"))
                        nc.tensor.matmul(pos_ps[:, 0:E], r.ones[:, :], cum[groups % 2][:, 0, :], start=True, stop=True).then_inc(r.totals, 1)

        if m.cap is None:
            lay_out_slots(nc, k, m, r, pos_ps, scattered)


def lay_out_slots(nc, k, m, r, pos_ps, scattered):
    E, K = m.e, m.top
    with ExitStack() as ctx:
        s = Scope(k, ctx, m.name + "s")
        up, whole = s.sb("up", [P, E], I32), s.sb("whole", [P, E], I32)
        size, start = s.sb("size", [P, E]), s.sb("start", [P, E + 1])
        owner, owned, ownerf = s.sb("owner", [1, m.ntiles, E - 1]), s.sb("owned", [1, m.ntiles]), s.sb("ownerf", [1, m.ntiles])
        onehot = s.sb("onehot", [P, T * K, E])
        base, slotf = s.sb("base", [P, T * K]), s.sb("slotf", [P, T * K])
        xs, slot = s.pair("xs", [P, D]), s.pair("slot", [P, K], U32)
        pool_waited = s.sem("poolwaited")
        chain, normed, copied = s.sem("chain"), s.steps("normed"), s.steps("copied")
        with nc.Block() as block:
            @block.vector
            def _(dve):
                for st in (normed, copied):
                    dve.sem_inc(st.sem, 2 * st.n)
                step = 0

                def then(ins):
                    nonlocal step
                    step += 1
                    ins.then_inc(chain, 1)
                    dve.wait_ge(chain, step)

                dve.wait_ge(r.totals, 1)
                then(nc.vector.tensor_scalar(up[:, :], pos_ps[:, 0:E], float(P - 1), None, ALU.add))
                then(nc.vector.tensor_scalar(whole[:, :], up[:, :], P.bit_length() - 1, None, ALU.arith_shift_right))
                then(nc.vector.tensor_copy(size[:, :], whole[:, :]))
                then(nc.vector.memset(start[:, 0:1], 0.0))
                for e in range(E):
                    then(nc.vector.tensor_tensor(start[:, e + 1:e + 2], start[:, e:e + 1], size[:, e:e + 1], ALU.add))
                then(nc.vector.tensor_tensor(owner[:, :, :], r.iota[0:1, 0:m.ntiles].unsqueeze(2).broadcast_to([1, m.ntiles, E - 1]),
                                             start[0:1, 1:E].unsqueeze(1).broadcast_to([1, m.ntiles, E - 1]), ALU.is_ge))
                then(nc.vector.tensor_reduce(ownerf[:, :], owner[:, :, :], AX, ALU.add))
                then(nc.vector.tensor_copy(r.owner[:, :], ownerf[:, :]))
                idxs = r.idxf[:, :, :].rearrange("p t k -> p (t k)")
                then(nc.vector.tensor_tensor(onehot[:, :, :], r.iota[:, 0:E].unsqueeze(1).broadcast_to([P, T * K, E]),
                                             idxs.unsqueeze(2).broadcast_to([P, T * K, E]), ALU.is_equal))
                then(nc.vector.tensor_tensor(onehot[:, :, :], onehot[:, :, :],
                                             start[:, 0:E].unsqueeze(1).broadcast_to([P, T * K, E]), ALU.mult))
                then(nc.vector.tensor_reduce(base[:, :], onehot[:, :, :], AX, ALU.add))
                then(nc.vector.scalar_tensor_tensor(slotf[:, :], base[:, :], float(P), r.pos[:, :, :].rearrange("p t k -> p (t k)"),
                                                    ALU.mult, ALU.add))
                then(nc.vector.tensor_copy(r.slots[:, :, :].rearrange("p t k -> p (t k)"), slotf[:, :]))

                def prepare(t, u):
                    reuse(dve, scattered, t, u, K)
                    nc.vector.tensor_scalar(xs[u][:, :], row(k.x, t), col(k.mean, t), col(k.rstd, t),
                                            ALU.subtract, ALU.mult).then_inc(normed.sem, 1)
                    nc.vector.tensor_copy(slot[u][:, :], row(r.slots, t)).then_inc(copied.sem, 1)
                pipeline(dve, T, (0, prepare), peel=2)

            @block.gpsimd
            def _(pool):
                pool.wait_ge(r.zeroed, 16 * r.nzero)

                def scatter(t, u):
                    pool.wait_ge(normed.sem, normed.at(t, "normed"))
                    pool.wait_ge(copied.sem, copied.at(t, "copied"))
                    stand_alone(pool, pool_waited)
                    for i in range(K):
                        nc.gpsimd.indirect_dma_start(r.xbuf[:, :], bass.IndirectOffsetOnAxis(slot[u][:, i:i + 1], 0), xs[u][:, :], None,
                                                     bounds_check=m.rows - 1, oob_is_err=False).then_inc(scattered[u], 16)
                pipeline(pool, T, (0, scatter))
                for u in range(2):
                    pool.wait_ge(scattered[u], 16 * K * (T // 2))


def narrow_experts(nc, k, m, d, r):
    F, HC = m.hidden, 2
    HP = F // HC
    npair = m.ntiles // 2
    with ExitStack() as ctx:
        s = Scope(k, ctx, m.name + "e")
        xb, xt = s.pair("xb", [P, 2, D]), s.pair("xt", [P, DC, 2, P])
        wgu, wd = s.pair("wgu", [P, 2 * DC, 2 * F]), s.pair("wd", [HP, 2 * HC, D])
        gate, h_t, y = s.pair("gate", [HP, 2, HC * P]), s.pair("ht", [HP, 2, HC * P]), s.pair("y", [P, 2, D])
        turned_ps, y_ps = [s.bank("turned0"), s.bank("turned1")], [s.bank("y0"), s.bank("y1")]
        gu_ps = [s.bank(f"gu{u}", 1024) for u in range(2)]
        x_in, wgu_in, wd_in, stored = s.sems("xin"), s.sems("wguin"), s.sems("wdin"), s.lasting_sems("stored")
        turned, copied, gu_made, gated, hidden = (s.steps(n) for n in ("turned", "copied", "gumade", "gated", "hidden"))
        y_made, y_copied = s.steps("ymade"), s.steps("ycopied")

        def nth(q, u):
            return (q - u) * 8 + 32

        with nc.Block() as block:
            @block.sync
            def _(sp):
                for u in range(2):
                    for sem in (x_in[u], wgu_in[u], wd_in[u]):
                        sp.sem_inc(sem, 16)

                def load_x(q, u):
                    sp.wait_ge(turned.sem, turned.at(q - 2, "turned"))
                    sp.dma_start(xb[u][:, :, :], r.xbuf[bass.ts(q, 2 * P), :].rearrange("(i p) d -> p i d", p=P)).then_inc(x_in[u], 16)

                def load_w(q, u):
                    sp.wait_ge(gu_made.sem, gu_made.at(q - 2, "gumade"))
                    sp.dma_start(wgu[u][:, :, :], d["gu"][bass.ts(q, 2 * D), :].rearrange("(c p) f -> p c f", p=P)).then_inc(wgu_in[u], 16)
                    sp.wait_ge(y_made.sem, y_made.at(q - 2, "ymade"))
                    sp.dma_start(wd[u][:, :, :], d["down"][bass.ts(q, 2 * F), :].rearrange("(c p) f -> p c f", p=HP)).then_inc(wd_in[u], 16)
                pipeline(sp, npair, (0, load_x), (1, load_w))

            @block.gpsimd
            def _(pool):
                def store(q, u):
                    pool.wait_ge(y_copied.sem, y_copied.at(q, "ycopied"))
                    pool.dma_start(r.ybuf[bass.ts(q, 2 * P), :].rearrange("(i p) d -> p i d", p=P), y[u][:, :, :]).then_inc(stored[u], 16)
                pipeline(pool, npair, (0, store))
                for u in range(2):
                    pool.wait_ge(stored[u], 16 * (npair // 2))

            @block.tensor
            def _(pe):
                for st in (turned, gu_made, y_made):
                    pe.sem_inc(st.sem, 2 * st.n)

                def turn(q, u):
                    pe.wait_ge(x_in[u], nth(q, u))
                    pe.wait_ge(copied.sem, copied.at(q - 2, "copied"))
                    for c in range(DC):
                        for i in range(2):
                            o = (2 * c + i) * P
                            last = nc.tensor.transpose(turned_ps[u][:, o:o + P], xb[u][:, i, c * P:(c + 1) * P], k.ident[:, :])
                    last.then_inc(turned.sem, 1)

                def gate_up(q, u):
                    pe.wait_ge(wgu_in[u], nth(q, u))
                    pe.wait_ge(copied.sem, copied.at(q, "copied"))
                    pe.wait_ge(hidden.sem, hidden.at(q - 2, "hidden"))
                    for i in range(2):
                        for j in range(2 * HC):
                            for c in range(DC):
                                last = nc.tensor.matmul(gu_ps[u][0:HP, i * 512 + j * P:i * 512 + (j + 1) * P],
                                                        wgu[u][:, i * DC + c, j * HP:(j + 1) * HP], xt[u][:, c, i, :],
                                                        start=c == 0, stop=c == DC - 1)
                    last.then_inc(gu_made.sem, 1)

                def down(q, u):
                    pe.wait_ge(wd_in[u], nth(q, u))
                    pe.wait_ge(hidden.sem, hidden.at(q, "hidden"))
                    pe.wait_ge(y_copied.sem, y_copied.at(q - 2, "ycopied"))
                    for i in range(2):
                        for c in range(HC):
                            last = nc.tensor.matmul(y_ps[u][:, i * D:(i + 1) * D], h_t[u][:, i, c * P:(c + 1) * P], wd[u][:, i * HC + c, :],
                                                    start=c == 0, stop=c == HC - 1)
                    last.then_inc(y_made.sem, 1)

                pipeline(pe, npair, (0, turn), (3, down), (1, gate_up))

            @block.scalar
            def _(act):
                for st in (gated, copied):
                    act.sem_inc(st.sem, 2 * st.n)

                def copy_x(q, u):
                    act.wait_ge(turned.sem, turned.at(q, "turned"))
                    act.wait_ge(gu_made.sem, gu_made.at(q - 2, "gumade"))
                    nc.scalar.copy(xt[u][:, :, :, :].rearrange("p c i n -> p (c i n)"), turned_ps[u][:, :]).then_inc(copied.sem, 1)

                def silu(q, u):
                    act.wait_ge(gu_made.sem, gu_made.at(q, "gumade"))
                    act.wait_ge(hidden.sem, hidden.at(q - 2, "hidden"))
                    nc.scalar.activation(gate[u][:, :, :], gu_ps[u][0:HP, :].rearrange("p (i f) -> p i f", i=2)[:, :, 0:HC * P],
                                         m.act).then_inc(gated.sem, 1)
                pipeline(act, npair, (0, copy_x), (1, silu))

            @block.vector
            def _(dve):
                for st in (hidden, y_copied):
                    dve.sem_inc(st.sem, 2 * st.n)

                def hide(q, u):
                    dve.wait_ge(gated.sem, gated.at(q, "gated"))
                    dve.wait_ge(y_made.sem, y_made.at(q - 2, "ymade"))
                    nc.vector.tensor_tensor(h_t[u][:, :, :], gate[u][:, :, :],
                                            gu_ps[u][0:HP, :].rearrange("p (i f) -> p i f", i=2)[:, :, HC * P:], ALU.mult).then_inc(hidden.sem, 1)

                def copy_y(q, u):
                    dve.wait_ge(y_made.sem, y_made.at(q, "ymade"))
                    reuse(dve, stored, q, u)
                    nc.vector.tensor_copy(y[u][:, :, :].rearrange("p i d -> p (i d)"), y_ps[u][:, :]).then_inc(y_copied.sem, 1)
                pipeline(dve, npair, (3, copy_y), (1, hide), peel=2)


def wide_experts(nc, k, m, d, r):
    HC = m.hidden // P
    with ExitStack() as ctx:
        s = Scope(k, ctx, m.name + "e")
        xb, xt = s.pair("xb", [P, D]), s.pair("xt", [P, DC, P])
        w1 = s.pair("w1e", [P, DC, m.hidden])
        h_t, y = s.pair("ht", [P, HC, P]), s.pair("y", [P, D])
        turned_ps, y_ps = [s.bank("turned0"), s.bank("turned1")], [s.bank("y0"), s.bank("y1")]
        h_ps = [[s.bank(f"h{u}{half}") for half in range(2)] for u in range(2)]
        x_in, stored = s.sems("xin"), s.sems("stored")
        turned, copied, w1_copied = s.steps("turned"), s.steps("copied"), s.steps("w1copied")
        made, acted = s.steps("made", "0", "1"), s.steps("acted", "0", "1")
        y_made, y_added = s.steps("ymade"), s.steps("yadded")

        def nth(t, u):
            return (t - u) * 8 + 32

        def owner(eng, t):
            return eng.value_load(r.owner[0:1, bass.ts(t, 1)], min_val=0, max_val=m.e - 1)

        with nc.Block() as block:
            @block.sync
            def _(sp):
                for u in range(2):
                    for sem in (x_in[u], stored[u]):
                        sp.sem_inc(sem, 16)

                def load(t, u):
                    sp.wait_ge(turned.sem, turned.at(t - 2, "turned"))
                    sp.dma_start(xb[u][:, :], r.xbuf[bass.ts(t, P), :]).then_inc(x_in[u], 16)

                def store(t, u):
                    sp.wait_ge(y_added.sem, y_added.at(t, "yadded"))
                    sp.dma_start(r.ybuf[bass.ts(t, P), :], y[u][:, :]).then_inc(stored[u], 16)
                pipeline(sp, m.ntiles, (0, load), (3, store))
                for u in range(2):
                    sp.wait_ge(stored[u], 16 * (m.ntiles // 2 + 1))

            @block.tensor
            def _(pe):
                for st in (turned, made, y_made):
                    pe.sem_inc(st.sem, 2 * st.n)
                pe.wait_ge(r.w_in, 16 * r.nw)

                def turn(t, u):
                    pe.wait_ge(x_in[u], nth(t, u))
                    pe.wait_ge(copied.sem, copied.at(t - 2, "copied"))
                    for c in range(DC):
                        last = nc.tensor.transpose(turned_ps[u][:, c * P:(c + 1) * P], xb[u][:, c * P:(c + 1) * P], k.ident[:, :])
                    last.then_inc(turned.sem, 1)

                def up(t, u):
                    pe.wait_ge(copied.sem, copied.at(t, "copied"))
                    pe.wait_ge(w1_copied.sem, w1_copied.at(t, "w1copied"))
                    for half in range(2):
                        pe.wait_ge(acted.sem, acted.at(t - 2, f"{half}"))
                        for i in range(4):
                            f0 = (4 * half + i) * P
                            for c in range(DC):
                                last = nc.tensor.matmul(h_ps[u][half][:, i * P:(i + 1) * P], w1[u][:, c, f0:f0 + P], xt[u][:, c, :],
                                                        start=c == 0, stop=c == DC - 1)
                        last.then_inc(made.sem, 1)

                def down(t, u):
                    e = owner(pe, t)
                    pe.wait_ge(y_added.sem, y_added.at(t - 2, "yadded"))
                    for c in range(HC):
                        if c % 4 == 0:
                            pe.wait_ge(acted.sem, acted.at(t, f"{c // 4}"))
                        last = nc.tensor.matmul(y_ps[u][:, 0:D], h_t[u][:, c, :], r.w2[:, bass.ts(e, 1), c, :].rearrange("p o f -> p (o f)"),
                                                start=c == 0, stop=c == HC - 1)
                    last.then_inc(y_made.sem, 1)

                pipeline(pe, m.ntiles, (0, turn), (1, up), (2, down))

            @block.scalar
            def _(act):
                act.sem_inc(acted.sem, 2 * acted.n)
                act.wait_ge(r.w_in, 16 * r.nw)

                def activate(t, u):
                    e = owner(act, t)
                    act.wait_ge(y_made.sem, y_made.at(t - 2, "ymade"))
                    for half in range(2):
                        act.wait_ge(made.sem, made.at(t, f"{half}"))
                        for i in range(4):
                            last = nc.scalar.activation(h_t[u][:, 4 * half + i, :], h_ps[u][half][:, i * P:(i + 1) * P], m.act,
                                                        bias=r.b1[:, bass.ds(e * HC + (4 * half + i), 1)])
                        last.then_inc(acted.sem, 1)
                pipeline(act, m.ntiles, (0, activate))

            @block.vector
            def _(dve):
                for st in (copied, w1_copied, y_added):
                    dve.sem_inc(st.sem, 2 * st.n)
                dve.wait_ge(r.w_in, 16 * r.nw)

                def copy_x(t, u):
                    dve.wait_ge(turned.sem, turned.at(t, "turned"))
                    dve.wait_ge(made.sem, made.at(t - 2, "1"))
                    nc.vector.tensor_copy(xt[u][:, :, :], turned_ps[u][:, 0:D].rearrange("p (c n) -> p c n", c=DC)).then_inc(copied.sem, 1)

                def copy_w1(t, u):
                    e = owner(dve, t)
                    dve.wait_ge(made.sem, made.at(t - 2, "1"))
                    nc.vector.tensor_copy(w1[u][:, :, :].rearrange("p c f -> p (c f)"),
                                          r.w1[:, bass.ts(e, 1), :, :].rearrange("p o c f -> p (o c f)")).then_inc(w1_copied.sem, 1)

                def add_b2(t, u):
                    e = owner(dve, t)
                    dve.wait_ge(y_made.sem, y_made.at(t, "ymade"))
                    dve.wait_ge(stored[u], (t - u) * 8 + 16)
                    nc.vector.tensor_tensor(y[u][:, :], y_ps[u][:, 0:D], row(r.b2, e), ALU.add).then_inc(y_added.sem, 1)
                pipeline(dve, m.ntiles, (0, copy_w1), (0, copy_x), (3, add_b2))


def combine(nc, k, m, r, jobs):
    K = m.top
    G = 8 // K
    with ExitStack() as ctx:
        s = Scope(k, ctx, m.name + "c")
        got = s.pair("got", [P, G, K, D])
        slot = s.pair("slot", [P, G, K], U32)
        pool_waited = s.sem("poolwaited")
        cleared, gathered = s.sem("cleared"), s.lasting_sems("gathered")
        copied = s.steps("copied")
        added = s.steps("added", *(f"{i}" for i in range(K)), "stats")
        with nc.Block() as block:
            @block.gpsimd
            def _(pool):
                def gather(g, u):
                    pool.wait_ge(copied.sem, copied.at(g, "copied"))
                    stand_alone(pool, pool_waited)
                    pool.wait_ge(added.sem, added.at(g - 2, f"{K - 1}"))
                    stand_alone(pool, pool_waited)
                    for j in range(G):
                        for i in range(K):
                            nc.gpsimd.indirect_dma_start(got[u][:, j, i, :], None, r.ybuf[:, :], bass.IndirectOffsetOnAxis(slot[u][:, j, i:i + 1], 0),
                                                         bounds_check=m.rows - 1, oob_is_err=False).then_inc(gathered[u], 16)
                pool.wait_ge(cleared, 2)
                pipeline(pool, T // G, (0, gather))

            @block.vector
            def _(dve):
                for st in (copied, added):
                    dve.sem_inc(st.sem, 2 * st.n)
                for u in range(2):
                    nc.vector.memset(got[u][:, :, :, :], 0.0).then_inc(cleared, 1)

                def index(g, u):
                    reuse(dve, gathered, g, u, G * K)
                    nc.vector.tensor_copy(slot[u][:, :, :], r.slots[:, bass.ts(g, G), :]).then_inc(copied.sem, 1)

                def add(g, u):
                    dve.wait_ge(gathered[u], (g - u) * (8 * G * K) + 16 * G * K)
                    for i in range(K):
                        if i:
                            dve.wait_ge(added.sem, added.at(g, f"{i - 1}"))
                        for j in range(G):
                            t = g * G + j
                            last = nc.vector.scalar_tensor_tensor(row(k.x, t), got[u][:, j, i, :], r.weights[:, bass.ts(t, 1), i], row(k.x, t),
                                                                  ALU.mult, ALU.add)
                        last.then_inc(added.sem, 1)
                    dve.wait_ge(added.sem, added.at(g, f"{K - 1}"))
                    for j in range(G):
                        last = nc.vector.bn_stats(row(k.stats, g * G + j), row(k.x, g * G + j))
                    last.then_inc(added.sem, 1)
                pipeline(dve, T // G, (0, index), (1, add), peel=2)

            if jobs:
                fold_contexts(nc, k, s, block, jobs)


def experts(nc, k, m, d):
    norm_scales(nc, k)
    with ExitStack() as ctx:
        s = Scope(k, ctx, m.name)
        r = Shared()
        r.xbuf, r.zeroed, r.nzero = k.slot_buffers[m.name]
        r.ybuf = nc.dram_tensor(f"{m.name}_ybuf", (m.rows, D), F32, kind="Internal").ap()
        r.iota, r.before, r.ones = s.sb("iota", [P, 64]), s.sb("before", [P, P]), s.sb("ones", [P, P])
        r.slots, r.weights = s.sb("slots", [P, T, m.top], U32), s.sb("weights", [P, T, m.top])
        r.pos, r.idxf = s.sb("pos", [P, T, m.top]), s.sb("idxf", [P, T, m.top])
        r.wr = s.sb("wr", [P, DC, m.e])
        loaded, ready = s.sem("loaded"), s.sem("ready")
        r.totals, r.w_in = s.sem("totals"), s.sem("win")
        wide = m is not M0
        if wide:
            hc = m.hidden // P
            r.w1, r.w2 = s.sb("w1", [P, m.e, DC, m.hidden]), s.sb("w2", [P, m.e, hc, D])
            r.b1, r.b2 = s.sb("b1", [P, m.e * hc]), s.sb("b2", [P, m.e, D])
            r.owner = s.sb("owner", [1, m.ntiles], I32)
            r.nw = 2 * m.e + 2
        with nc.Block() as block:
            if not k.buffers_zeroed:
                zero_slot_buffers(nc, k, block)

            @block.sync
            def _(sp):
                sp.dma_start(r.wr[:, :, :], d["wr"].rearrange("(c p) e -> p c e", p=P)).then_inc(loaded, 16)
                sp.dma_start(r.iota[:, :], k.iota).then_inc(loaded, 16)
                sp.dma_start(r.before[:, :], k.before).then_inc(loaded, 16)
                if wide and m.cap is not None:
                    sp.dma_start(r.owner[:, :], d["owner"]).then_inc(loaded, 16)
                sp.wait_ge(loaded, 64 if wide and m.cap is not None else 48)

            @block.vector
            def _(dve):
                nc.vector.memset(r.ones[:, :], 1.0).then_inc(ready, 1)
                dve.wait_ge(ready, 1)
        route(nc, k, m, d, r)
        if wide:
            wide_experts(nc, k, m, d, r)
        else:
            narrow_experts(nc, k, m, d, r)
        jobs = k.fold_jobs if m is M0 else []
        for a, _ in jobs:
            k.folded[a.name] = Folded(nc, a)
        combine(nc, k, m, r, jobs)



LH, LD = 8, 64
INNER = LH * LD
HID = 682
QUARTER = HID // 2
HID_CHUNKS = [(c, min(P, HID - c)) for c in range(0, HID, P)]
NORM_EPS2 = 1e-24
SHUT = -1e24
SCORE_BANKS = [(0, 2), (1, 3), (4, 6), (5, 7)]


def y_row(a, t):
    return row(a, t + (t // TB + 1))


def y_shift(sp, h, y, t, sem):
    half = D // 2
    here, before = t + (t // TB + 1), t + t // TB
    sp.dma_start(h[:, 0:half], y[:, bass.ts(here, 1), 0:half].rearrange("p o d -> p (o d)")).then_inc(sem, 16)
    sp.dma_start(h[1:P, half:D], y[0:P - 1, bass.ts(here, 1), half:D].rearrange("p o d -> p (o d)")).then_inc(sem, 16)
    sp.dma_start(h[0:1, half:D], y[P - 1:P, bass.ts(before, 1), half:D].rearrange("p o d -> p (o d)")).then_inc(sem, 16)


def local_attention(nc, k, d, l, y_in, y_out, lo):
    with ExitStack() as ctx:
        s = Scope(k, ctx, f"la{l}")
        wqkv, wo = s.sb("wqkv", [P, DC, 3 * INNER]), s.sb("wo", [P, INNER // P, D])
        tables = [s.sb(n, [P, TB, LD]) for n in ("cosq", "sinq", "cosk", "sink")]
        scales = s.sb("scales", [P, 4, LD])
        h, h_t = s.pair("h", [P, D]), s.pair("ht", [P, DC, P])
        squares, ss, clamped, inv_norm = s.pair("squares", [P, 2, INNER]), s.pair("ss", [P, 16]), s.pair("clamped", [P, 16]), s.pair("invnorm", [P, 16])
        cosed, sined = s.sb("cosed", [P, 2, LH, LD]), s.sb("sined", [P, 2, LH, LD])
        qk = s.pair("qk", [P, 2, INNER])
        q_t, k_t, v = s.pair("qt", [P, 4, P]), s.pair("kt", [P, 4, P]), s.pair("v", [P, INNER])
        mx, nb, total, inv = s.pair("mx", [P, LH]), s.pair("nb", [P, LH]), s.pair("total", [P, LH]), s.pair("inv", [P, LH])
        probs, probs_t = s.pair("probs", [P, LH, 2 * P]), s.pair("probst", [P, LH, 2, P])
        o, o_t = s.pair("o", [P, INNER]), s.pair("ot", [P, 4, P])
        score_ps = [s.bank(f"score{j}") for j in range(4)]
        q_ps, k_ps, v_ps, c_ps = s.bank("q"), s.bank("k"), s.bank("v"), s.bank("c")
        loaded, ready, h_in = s.sem("loaded"), s.sem("ready"), s.sems("hin")

        turned, copied = s.steps("turned"), s.steps("copied")
        projected = s.steps("projected", "q", "k", "v")
        squared = s.steps("squared", "q", "k")
        roped = s.steps("roped", "ssq", "ssk", "clamp", "qcos", "qsin0", "qsin1", "q", "kcos", "ksin0", "ksin1", "k", "knorm")
        powered = s.steps("powered")
        qk_turned, qk_copied, v_copied = s.steps("qkturned", "q", "k"), s.steps("qkcopied", "q", "k"), s.steps("vcopied")
        scored = s.steps("scored", *"0123")
        maxed = s.steps("maxed", *(f"{w}{j}" for j in range(4) for w in ("max", "bias")))
        exped = s.steps("exped", *"0123")
        p_turned, p_copied = s.steps("pturned", *"0123"), s.steps("pcopied", *"0123")
        mixed, o_scaled = s.steps("mixed"), s.steps("oscaled", "inv", "o")
        o_turned, o_copied, made, added = s.steps("oturned"), s.steps("ocopied"), s.steps("made"), s.steps("added")
        nload = 2 + 4 + 4

        with nc.Block() as block:
            @block.sync
            def _(sp):
                sp.dma_start(wqkv[:, :, :], d["wqkv"][l].rearrange("(c p) n -> p c n", p=P)).then_inc(loaded, 16)
                sp.dma_start(wo[:, :, :], d["wo"][l].rearrange("(c p) n -> p c n", p=P)).then_inc(loaded, 16)
                for i, n in enumerate(("cosq", "sinq", "cosk", "sink")):
                    sp.dma_start(tables[i][:, :, :], d[n].rearrange("(w p) e -> p w e", p=P)).then_inc(loaded, 16)
                for i, n in enumerate(("qs", "qs_turned", "ks", "ks_turned")):
                    sp.dma_start(scales[:, i, :], d[n][l].partition_broadcast(P)).then_inc(loaded, 16)
                for u in range(2):
                    sp.sem_inc(h_in[u], 16)

                def load(t, u):
                    sp.wait_ge(turned.sem, turned.at(t - 2, "turned"))
                    y_shift(sp, h[u], y_in, t, h_in[u])
                pipeline(sp, T, (0, load))

            @block.gpsimd
            def _(pool):
                pool.sem_inc(powered.sem, 2)
                pool.wait_ge(ready, 2)

                def power(t, u):
                    pool.wait_ge(roped.sem, roped.at(t, "clamp"))
                    nc.gpsimd.tensor_tensor(inv_norm[u][:, :], clamped[u][:, :], lo.minus_half[:, :], ALU.pow).then_inc(powered.sem, 1)
                pipeline(pool, T, (0, power))

            @block.vector
            def _(dve):
                for st in (roped, maxed, o_scaled, added):
                    dve.sem_inc(st.sem, 2 * st.n)
                nc.vector.memset(k_t[1][:, :, :], 0.0).then_inc(ready, 1)
                nc.vector.memset(v[1][:, :], 0.0).then_inc(ready, 1)
                dve.wait_ge(loaded, 16 * nload)
                for i in range(4):
                    nc.vector.tensor_tensor(tables[i][:, :, :], tables[i][:, :, :],
                                            scales[:, i, :].unsqueeze(1).broadcast_to([P, TB, LD]), ALU.mult).then_inc(ready, 1)
                dve.wait_ge(ready, 6)

                def table(i, t, half=None):
                    e0, e1 = (0, LD) if half is None else (half * 32, half * 32 + 32)
                    return tables[i][:, bass.ts(t % TB, 1), e0:e1].broadcast_to([P, LH, e1 - e0])

                def rope(t, u):
                    def done(name):
                        dve.wait_ge(roped.sem, roped.at(t, name))
                    for i, n in enumerate("qk"):
                        dve.wait_ge(squared.sem, squared.at(t, n))
                        nc.vector.tensor_reduce(ss[u][:, i * LH:(i + 1) * LH], squares[u][:, i, :].rearrange("p (h e) -> p h e", h=LH),
                                                AX, ALU.add).then_inc(roped.sem, 1)
                    done("ssk")
                    nc.vector.tensor_scalar(clamped[u][:, :], ss[u][:, :], NORM_EPS2, None, ALU.max).then_inc(roped.sem, 1)
                    for i, (n, ps) in enumerate((("q", q_ps), ("k", k_ps))):
                        src = ps[:, :].rearrange("p (h e) -> p h e", h=LH)
                        nc.vector.tensor_tensor(cosed[:, i, :, :], src, table(2 * i, t), ALU.mult).then_inc(roped.sem, 1)
                        for half in range(2):
                            nc.vector.tensor_tensor(sined[:, i, :, half * 32:half * 32 + 32], src[:, :, 32 - half * 32:64 - half * 32],
                                                    table(2 * i + 1, t, half), ALU.mult).then_inc(roped.sem, 1)
                        done(f"{n}sin1")
                        if i == 0:
                            dve.wait_ge(qk_turned.sem, qk_turned.at(t - 2, "k"))
                        nc.vector.tensor_tensor(qk[u][:, i, :].rearrange("p (h e) -> p h e", h=LH), cosed[:, i, :, :], sined[:, i, :, :],
                                                ALU.add).then_inc(roped.sem, 1)
                    done("k")
                    dve.wait_ge(powered.sem, powered.at(t, "powered"))
                    keys = qk[u][:, 1, :].rearrange("p (h e) -> p h e", h=LH)
                    nc.vector.tensor_tensor(keys, keys, inv_norm[u][:, LH:2 * LH].unsqueeze(2).broadcast_to([P, LH, LD]),
                                            ALU.mult).then_inc(roped.sem, 1)

                def maxima(t, u):
                    dve.wait_ge(exped.sem, exped.at(t - 2, "3"))
                    for j, (h0, h1) in enumerate(SCORE_BANKS):
                        dve.wait_ge(scored.sem, scored.at(t, f"{j}"))
                        nc.vector.tensor_reduce(mx[u][:, h0:h1 + 1:2], score_ps[j][:, :].rearrange("p (h e) -> p h e", h=2), AX, ALU.max).then_inc(maxed.sem, 1)
                        dve.wait_ge(maxed.sem, maxed.at(t, f"max{j}"))
                        nc.vector.scalar_tensor_tensor(nb[u][:, h0:h1 + 1:2], mx[u][:, h0:h1 + 1:2], -1.0, inv_norm[u][:, h0:h1 + 1:2],
                                                       ALU.mult, ALU.mult).then_inc(maxed.sem, 1)

                def scale_o(t, u):
                    dve.wait_ge(exped.sem, exped.at(t, "3"))
                    nc.vector.reciprocal(inv[u][:, :], total[u][:, :]).then_inc(o_scaled.sem, 1)
                    dve.wait_ge(o_scaled.sem, o_scaled.at(t, "inv"))
                    dve.wait_ge(mixed.sem, mixed.at(t, "mixed"))
                    dve.wait_ge(o_turned.sem, o_turned.at(t - 2, "oturned"))
                    nc.vector.tensor_tensor(o[u][:, :].rearrange("p (h e) -> p h e", h=LH), c_ps[:, :].rearrange("p (h e) -> p h e", h=LH),
                                            inv[u][:, :].unsqueeze(2).broadcast_to([P, LH, LD]), ALU.mult).then_inc(o_scaled.sem, 1)

                def add(t, u):
                    dve.wait_ge(made.sem, made.at(t, "made"))
                    nc.vector.tensor_tensor(y_row(y_out, t), y_row(y_in, t), v_ps[:, 0:D], ALU.add).then_inc(added.sem, 1)

                pipeline(dve, T, (2, add), (1, maxima), (0, rope), (1, scale_o))

            @block.scalar
            def _(act):
                for st in (copied, squared, qk_copied, v_copied, exped, p_copied, o_copied):
                    act.sem_inc(st.sem, 2 * st.n)

                def copy_h(t, u):
                    act.wait_ge(turned.sem, turned.at(t, "turned"))
                    act.wait_ge(projected.sem, projected.at(t - 2, "v"))
                    nc.scalar.copy(h_t[u][:, :, :], c_ps[:, 0:D].rearrange("p (c n) -> p c n", c=DC)).then_inc(copied.sem, 1)

                def copy_o(t, u):
                    act.wait_ge(o_turned.sem, o_turned.at(t, "oturned"))
                    act.wait_ge(made.sem, made.at(t - 2, "made"))
                    nc.scalar.copy(o_t[u][:, :, :], v_ps[:, :].rearrange("p (c n) -> p c n", c=4)).then_inc(o_copied.sem, 1)

                def copy_qk(t, u):
                    act.wait_ge(qk_turned.sem, qk_turned.at(t, "q"))
                    act.wait_ge(scored.sem, scored.at(t - 1, "3"))
                    nc.scalar.copy(q_t[u][:, :, :], q_ps[:, :].rearrange("p (c n) -> p c n", c=4)).then_inc(qk_copied.sem, 1)
                    act.wait_ge(qk_turned.sem, qk_turned.at(t, "k"))
                    nc.scalar.copy(k_t[u][:, :, :], k_ps[:, :].rearrange("p (c n) -> p c n", c=4)).then_inc(qk_copied.sem, 1)

                def exp(t, u):
                    act.wait_ge(p_turned.sem, p_turned.at(t - 2, "3"))
                    act.wait_ge(o_scaled.sem, o_scaled.at(t - 2, "inv"))
                    for j, pair in enumerate(SCORE_BANKS):
                        act.wait_ge(maxed.sem, maxed.at(t, f"bias{j}"))
                        for i, hh in enumerate(pair):
                            last = nc.scalar.activation(probs[u][:, hh, :], score_ps[j][:, i * 2 * P:(i + 1) * 2 * P], ACT.Exp,
                                                        bias=nb[u][:, hh:hh + 1], scale=inv_norm[u][:, hh:hh + 1],
                                                        accum_out=total[u][:, hh:hh + 1])
                        last.then_inc(exped.sem, 1)

                def square(t, u):
                    for i, (n, ps) in enumerate((("q", q_ps), ("k", k_ps))):
                        act.wait_ge(projected.sem, projected.at(t, n))
                        act.wait_ge(roped.sem, roped.at(t - 2, "ssk"))
                        nc.scalar.activation(squares[u][:, i, :], ps[:, :], ACT.Square).then_inc(squared.sem, 1)

                def copy_p(t, u):
                    act.wait_ge(mixed.sem, mixed.at(t - 2, "mixed"))
                    for j, (h0, h1) in enumerate(SCORE_BANKS):
                        act.wait_ge(p_turned.sem, p_turned.at(t, f"{j}"))
                        nc.scalar.copy(probs_t[u][:, h0:h1 + 1:2, :, :].rearrange("p h w n -> p h (w n)"),
                                       score_ps[j][:, :].rearrange("p (h n) -> p h n", h=2)).then_inc(p_copied.sem, 1)

                def copy_v(t, u):
                    act.wait_ge(projected.sem, projected.at(t, "v"))
                    act.wait_ge(mixed.sem, mixed.at(t - 1, "mixed"))
                    nc.scalar.copy(v[u][:, :], v_ps[:, :]).then_inc(v_copied.sem, 1)

                pipeline(act, T, (0, copy_h), (2, copy_o), (1, copy_qk), (1, exp), (0, square), (1, copy_p), (0, copy_v))

            @block.tensor
            def _(pe):
                for st in (turned, projected, qk_turned, scored, p_turned, mixed, o_turned, made):
                    pe.sem_inc(st.sem, 2 * st.n)
                pe.wait_ge(loaded, 16 * nload)
                pe.wait_ge(ready, 2)

                def turn(t, u):
                    pe.wait_ge(h_in[u], (t - u) * 24 + 64)
                    pe.wait_ge(o_scaled.sem, o_scaled.at(t - 2, "o"))
                    for c in range(DC):
                        last = nc.tensor.transpose(c_ps[:, c * P:(c + 1) * P], h[u][:, c * P:(c + 1) * P], k.ident[:, :])
                    last.then_inc(turned.sem, 1)

                def project(t, u):
                    pe.wait_ge(copied.sem, copied.at(t, "copied"))
                    for i, ps in enumerate((q_ps, k_ps, v_ps)):
                        if i < 2:
                            pe.wait_ge(qk_copied.sem, qk_copied.at(t - 1, "qk"[i]))
                        else:
                            pe.wait_ge(added.sem, added.at(t - 2, "added"))
                        for c in range(DC):
                            last = nc.tensor.matmul(ps[:, :], h_t[u][:, c, :], wqkv[:, c, i * INNER:(i + 1) * INNER],
                                                    start=c == 0, stop=c == DC - 1)
                        last.then_inc(projected.sem, 1)

                def turn_qk(t, u):
                    pe.wait_ge(roped.sem, roped.at(t, "k"))
                    for i, ps in enumerate((q_ps, k_ps)):
                        if i == 1:
                            pe.wait_ge(roped.sem, roped.at(t, "knorm"))
                        for c in range(4):
                            last = nc.tensor.transpose(ps[:, c * P:(c + 1) * P], qk[u][:, i, c * P:(c + 1) * P], k.ident[:, :])
                        last.then_inc(qk_turned.sem, 1)

                def score(t, u):
                    pe.wait_ge(qk_copied.sem, qk_copied.at(t, "k"))
                    first = 1 - (t % TB + (TB - 1)) // TB
                    for j in range(4):
                        pe.wait_ge(p_copied.sem, p_copied.at(t - 1, f"{j}"))
                        nc.tensor.matmul(score_ps[j][:, :], lo.ident16[:, :], lo.shut[:, bass.ts(first, 1), :].rearrange("p o n -> p (o n)"),
                                         start=True, stop=False, skip_group_check=True)
                    for j0 in (0, 2):
                        for i in range(2):
                            for j in (j0, j0 + 1):
                                hh = SCORE_BANKS[j][i]
                                p0 = LD * (hh % 2)
                                for w, kt in enumerate((k_t[1 - u], k_t[u])):
                                    c0 = i * 2 * P + w * P
                                    last = nc.tensor.matmul(score_ps[j][:, c0:c0 + P], q_t[u][p0:p0 + LD, hh // 2, :], kt[p0:p0 + LD, hh // 2, :],
                                                            start=False, stop=True, skip_group_check=True)
                                if i == 1:
                                    last.then_inc(scored.sem, 1)

                def turn_p(t, u):
                    for j, pair in enumerate(SCORE_BANKS):
                        pe.wait_ge(exped.sem, exped.at(t, f"{j}"))
                        for i, hh in enumerate(pair):
                            for w in range(2):
                                c0 = i * 2 * P + w * P
                                last = nc.tensor.transpose(score_ps[j][:, c0:c0 + P], probs[u][:, hh, w * P:(w + 1) * P], k.ident[:, :])
                        last.then_inc(p_turned.sem, 1)

                def mix(t, u):
                    pe.wait_ge(v_copied.sem, v_copied.at(t, "vcopied"))
                    pe.wait_ge(copied.sem, copied.at(t + 1, "copied") if not isinstance(t, int) or t + 1 < T else copied.at(t, "copied"))
                    for j, pair in enumerate(SCORE_BANKS):
                        pe.wait_ge(p_copied.sem, p_copied.at(t, f"{j}"))
                        for hh in pair:
                            for w, vw in enumerate((v[1 - u], v[u])):
                                last = nc.tensor.matmul(c_ps[:, hh * LD:(hh + 1) * LD], probs_t[u][:, hh, w, :], vw[:, hh * LD:(hh + 1) * LD],
                                                        start=w == 0, stop=w == 1)
                    last.then_inc(mixed.sem, 1)

                def turn_o(t, u):
                    pe.wait_ge(o_scaled.sem, o_scaled.at(t, "o"))
                    pe.wait_ge(v_copied.sem, v_copied.at(t + 1, "vcopied") if not isinstance(t, int) or t + 1 < T else v_copied.at(t, "vcopied"))
                    for c in range(4):
                        last = nc.tensor.transpose(v_ps[:, c * P:(c + 1) * P], o[u][:, c * P:(c + 1) * P], k.ident[:, :])
                    last.then_inc(o_turned.sem, 1)

                def output(t, u):
                    pe.wait_ge(o_copied.sem, o_copied.at(t, "ocopied"))
                    for c in range(4):
                        last = nc.tensor.matmul(v_ps[:, 0:D], o_t[u][:, c, :], wo[:, c, :], start=c == 0, stop=c == 3)
                    last.then_inc(made.sem, 1)

                pipeline(pe, T, (0, turn), (2, turn_o), (1, turn_qk), (2, output), (1, score), (0, project), (1, turn_p), (1, mix))


def local_feed_forward(nc, k, d, l, y_in, y_out, lo):
    with ExitStack() as ctx:
        s = Scope(k, ctx, f"lf{l}")
        nrow = 2 * HID + D
        nch = len(HID_CHUNKS)
        w1, w2 = s.sb("w1", [P, DC, 2 * HID]), s.sb("w2", [P, nch, D])
        w1g = s.sb("w1g", [P, DC, 2 * HID])
        gain, offset = s.sb("gain", [P, DC]), s.sb("offset", [P, DC])
        brow, rest, rest2 = s.sb("brow", [1, nrow]), s.sb("rest", [1, nrow]), s.sb("rest2", [1, nrow])
        parts = [s.sb(f"part{i}", [1, nrow], BF16) for i in range(3)]
        b3 = s.sb("b3", [3, nrow], BF16)
        h, z, z_t = s.pair("h", [P, D]), s.pair("z", [P, D]), s.pair("zt", [P, DC, P])
        st6, mv, ve, rstd = s.pair("st", [P, 6]), s.pair("mv", [P, 2]), s.pair("ve", [P, 1]), s.pair("rstd", [P, 1])
        gelu, hid, hid_t = s.pair("gelu", [P, HID]), s.pair("hid", [P, HID]), s.pair("hidt", [P, nch, P])
        banks = [s.bank(f"m{i}") for i in range(4)]
        ht_ps = [s.bank("ht0"), s.bank("ht1")]
        t_ps, y_ps = s.bank("t"), s.bank("y")
        loaded, folded, biased, split, h_in, dve_waited = s.sem("loaded"), s.sem("folded"), s.sem("biased"), s.sem("split"), s.sems("hin"), s.sem("dvewaited")
        b3_in = s.sem("b3in")

        normed = s.steps("normed", "stats", "aggr", "eps", "z")
        powered, turned, copied = s.steps("powered"), s.steps("turned"), s.steps("copied")
        made = s.steps("made", "g0", "g1", "a0", "a1")
        gated, hidden = s.steps("gated", "0", "1"), s.steps("hidden", "0", "1")
        h_turned, h_copied = s.steps("hturned", "0", "1"), s.steps("hcopied", "0", "1")
        y_made, added = s.steps("ymade"), s.steps("added", *(["y"] if l == 0 else ["y", "x", "stats"]))
        nload = 3 + 4 + 1

        with nc.Block() as block:
            @block.sync
            def _(sp):
                sp.dma_start(w1[:, :, :], d["w1"][l].rearrange("(c p) n -> p c n", p=P)).then_inc(loaded, 16)
                whole = nch - 1
                sp.dma_start(w2[:, 0:whole, :], d["w2"][l, 0:whole * P].rearrange("(c p) n -> p c n", p=P)).then_inc(loaded, 16)
                sp.dma_start(w2[0:HID - whole * P, whole, :], d["w2"][l, whole * P:HID]).then_inc(loaded, 16)
                sp.dma_start(gain[:, :], d["gain"][l]).then_inc(loaded, 16)
                sp.dma_start(offset[:, :], d["offset"][l]).then_inc(loaded, 16)
                sp.dma_start(brow[:, 0:2 * HID], d["b1"][l:l + 1]).then_inc(loaded, 16)
                sp.dma_start(brow[:, 2 * HID:], d["b2"][l:l + 1]).then_inc(loaded, 16)
                sp.wait_ge(split, 5)
                for i in range(3):
                    sp.dma_start(b3[i:i + 1, :], parts[i][:, :]).then_inc(b3_in, 16)
                sp.wait_ge(b3_in, 48)
                for u in range(2):
                    sp.sem_inc(h_in[u], 16)

                def load(t, u):
                    sp.wait_ge(normed.sem, normed.at(t - 2, "z"))
                    y_shift(sp, h[u], y_in, t, h_in[u])
                pipeline(sp, T, (0, load))

            @block.gpsimd
            def _(pool):
                pool.sem_inc(powered.sem, 2)

                def power(t, u):
                    pool.wait_ge(normed.sem, normed.at(t, "eps"))
                    nc.gpsimd.tensor_tensor(rstd[u][:, :], ve[u][:, :], lo.minus_half[:, 0:1], ALU.pow).then_inc(powered.sem, 1)
                pipeline(pool, T, (0, power))

            @block.vector
            def _(dve):
                for st in (normed, hidden, h_copied, added):
                    dve.sem_inc(st.sem, 2 * st.n)
                dve.wait_ge(loaded, 16 * (nload - 1))
                for c in range(DC):
                    nc.vector.tensor_scalar(w1g[:, c, :], w1[:, c, :], gain[:, c:c + 1], None, ALU.mult).then_inc(folded, 1)
                dve.wait_ge(biased, 4)
                for i in range(4):
                    cols = slice(i * QUARTER, (i + 1) * QUARTER)
                    nc.vector.tensor_tensor(brow[:, cols], brow[:, cols], banks[i][0:1, 0:QUARTER], ALU.add).then_inc(folded, 1)
                dve.wait_ge(folded, 6)
                nc.vector.tensor_copy(parts[0][:, :], brow[:, :]).then_inc(split, 1)
                dve.wait_ge(split, 1)
                nc.vector.tensor_tensor(rest[:, :], brow[:, :], parts[0][:, :], ALU.subtract).then_inc(split, 1)
                dve.wait_ge(split, 2)
                nc.vector.tensor_copy(parts[1][:, :], rest[:, :]).then_inc(split, 1)
                dve.wait_ge(split, 3)
                nc.vector.tensor_tensor(rest2[:, :], rest[:, :], parts[1][:, :], ALU.subtract).then_inc(split, 1)
                dve.wait_ge(split, 4)
                nc.vector.tensor_copy(parts[2][:, :], rest2[:, :]).then_inc(split, 1)

                def stats(t, u):
                    def done(name):
                        dve.wait_ge(normed.sem, normed.at(t, name))
                    dve.wait_ge(h_in[u], (t - u) * 24 + 64)
                    nc.vector.bn_stats(st6[u][:, :], h[u][:, :]).then_inc(normed.sem, 1)
                    done("stats")
                    stand_alone(dve, dve_waited)
                    nc.vector.bn_aggr(mv[u][:, :], st6[u][:, :]).then_inc(normed.sem, 1)
                    done("aggr")
                    nc.vector.tensor_scalar(ve[u][:, :], mv[u][:, 1:2], LN_EPS, None, ALU.add).then_inc(normed.sem, 1)

                def norm(t, u):
                    dve.wait_ge(powered.sem, powered.at(t, "powered"))
                    dve.wait_ge(turned.sem, turned.at(t - 2, "turned"))
                    nc.vector.tensor_scalar(z[u][:, :], h[u][:, :], mv[u][:, 0:1], rstd[u][:, 0:1], ALU.subtract, ALU.mult).then_inc(normed.sem, 1)

                def hide(t, u):
                    dve.wait_ge(h_turned.sem, h_turned.at(t - 2, "1"))
                    for i in range(2):
                        dve.wait_ge(gated.sem, gated.at(t, f"{i}"))
                        dve.wait_ge(made.sem, made.at(t, f"a{i}"))
                        cols = slice(i * QUARTER, (i + 1) * QUARTER)
                        nc.vector.tensor_tensor(hid[u][:, cols], gelu[u][:, cols], banks[i][:, 0:QUARTER], ALU.mult).then_inc(hidden.sem, 1)

                def copy_h(t, u):
                    dve.wait_ge(y_made.sem, y_made.at(t - 2, "ymade"))
                    dve.wait_ge(h_turned.sem, h_turned.at(t, "0"))
                    nc.vector.tensor_copy(hid_t[u][:, 0:4, :], ht_ps[0][:, :].rearrange("p (c n) -> p c n", c=4)).then_inc(h_copied.sem, 1)
                    dve.wait_ge(h_turned.sem, h_turned.at(t, "1"))
                    rows = HID_CHUNKS[5][1]
                    nc.vector.tensor_copy(hid_t[u][:, 4, :], ht_ps[1][:, 0:P])
                    nc.vector.tensor_copy(hid_t[u][0:rows, 5, :], ht_ps[1][0:rows, P:2 * P]).then_inc(h_copied.sem, 1)

                def add(t, u):
                    dve.wait_ge(y_made.sem, y_made.at(t, "ymade"))
                    nc.vector.tensor_tensor(y_row(y_out, t), y_row(y_in, t), y_ps[:, 0:D], ALU.add).then_inc(added.sem, 1)
                    if l == 1:
                        dve.wait_ge(added.sem, added.at(t, "y"))
                        nc.vector.tensor_tensor(row(k.x, t), row(k.x, t), y_row(y_out, t), ALU.add).then_inc(added.sem, 1)
                        dve.wait_ge(added.sem, added.at(t, "x"))
                        nc.vector.bn_stats(row(k.stats, t), row(k.x, t)).then_inc(added.sem, 1)

                pipeline(dve, T, (0, stats), (1, hide), (0, norm), (2, add), (1, copy_h))

            @block.scalar
            def _(act):
                for st in (copied, gated):
                    act.sem_inc(st.sem, 2 * st.n)

                def copy_z(t, u):
                    act.wait_ge(turned.sem, turned.at(t, "turned"))
                    act.wait_ge(made.sem, made.at(t - 2, "a1"))
                    nc.scalar.copy(z_t[u][:, :, :], t_ps[:, 0:D].rearrange("p (c n) -> p c n", c=DC)).then_inc(copied.sem, 1)

                def gate(t, u):
                    act.wait_ge(hidden.sem, hidden.at(t - 2, "1"))
                    for i in range(2):
                        act.wait_ge(made.sem, made.at(t, f"g{i}"))
                        nc.scalar.activation(gelu[u][:, i * QUARTER:(i + 1) * QUARTER], banks[2 + i][:, 0:QUARTER], ACT.Gelu).then_inc(gated.sem, 1)
                pipeline(act, T, (1, gate), (0, copy_z))

            @block.tensor
            def _(pe):
                for st in (turned, made, h_turned, y_made):
                    pe.sem_inc(st.sem, 2 * st.n)
                pe.wait_ge(loaded, 16 * (nload - 1))
                for i in range(4):
                    for c in range(DC):
                        last = nc.tensor.matmul(banks[i][0:1, 0:QUARTER], offset[:, c:c + 1], w1[:, c, i * QUARTER:(i + 1) * QUARTER],
                                                start=c == 0, stop=c == DC - 1)
                    last.then_inc(biased, 1)
                pe.wait_ge(folded, 6)
                pe.wait_ge(b3_in, 48)

                def turn(t, u):
                    pe.wait_ge(normed.sem, normed.at(t, "z"))
                    pe.wait_ge(copied.sem, copied.at(t - 1, "copied"))
                    for c in range(DC):
                        last = nc.tensor.transpose(t_ps[:, c * P:(c + 1) * P], z[u][:, c * P:(c + 1) * P], k.ident[:, :])
                    last.then_inc(turned.sem, 1)

                def up(t, u):
                    pe.wait_ge(copied.sem, copied.at(t, "copied"))
                    for i in (2, 3, 0, 1):
                        if i >= 2:
                            pe.wait_ge(gated.sem, gated.at(t - 1, f"{i - 2}"))
                        else:
                            pe.wait_ge(hidden.sem, hidden.at(t - 1, f"{i}"))
                        cols = slice(i * QUARTER, (i + 1) * QUARTER)
                        nc.tensor.matmul(banks[i][:, 0:QUARTER], k.ones3[:, :], b3[:, cols], start=True, stop=False)
                        for c in range(DC):
                            last = nc.tensor.matmul(banks[i][:, 0:QUARTER], z_t[u][:, c, :], w1g[:, c, cols], start=False, stop=c == DC - 1)
                        last.then_inc(made.sem, 1)

                def turn_h(t, u):
                    for q, cs in enumerate((range(4), range(4, nch))):
                        pe.wait_ge(hidden.sem, hidden.at(t, "1"))
                        pe.wait_ge(h_copied.sem, h_copied.at(t - 1, f"{q}"))
                        for c in cs:
                            c0, n = HID_CHUNKS[c]
                            last = nc.tensor.transpose(ht_ps[q][0:n, (c - cs[0]) * P:(c - cs[0] + 1) * P], hid[u][:, c0:c0 + n], k.ident[:, :])
                        last.then_inc(h_turned.sem, 1)

                def down(t, u):
                    pe.wait_ge(added.sem, added.at(t - 1, "y"))
                    nc.tensor.matmul(y_ps[:, 0:D], k.ones3[:, :], b3[:, 2 * HID:], start=True, stop=False)
                    for c, (c0, n) in enumerate(HID_CHUNKS):
                        if c in (0, 4):
                            pe.wait_ge(h_copied.sem, h_copied.at(t, f"{c // 4}"))
                        last = nc.tensor.matmul(y_ps[:, 0:D], hid_t[u][0:n, c, :], w2[0:n, c, :], start=False, stop=c == nch - 1)
                    last.then_inc(y_made.sem, 1)

                pipeline(pe, T, (1, up), (0, turn), (2, down), (1, turn_h))


def local_layers(nc, k, d):
    norm_scales(nc, k)
    with ExitStack() as ctx:
        s = Scope(k, ctx, "lo")
        lo = Shared()
        y = s.pair("y", [P, T + B, D])
        lo.shut, lo.ident16 = s.sb("shut", [P, 2, 4 * P], BF16), s.sb("ident16", [P, P], BF16)
        lo.minus_half = s.sb("minushalf", [P, 16])
        loaded, ready = s.sem("loaded"), s.sem("ready")
        shut_f, ident_f = s.sb("shutf", [P, 2, 4 * P]), None
        with nc.Block() as block:
            @block.sync
            def _(sp):
                sp.dma_start(shut_f[:, :, :], d["shut"]).then_inc(loaded, 16)

            @block.vector
            def _(dve):
                nc.vector.memset(lo.minus_half[:, :], -0.5).then_inc(ready, 1)
                for u in range(2):
                    for b in range(B):
                        nc.vector.memset(y[u][:, b * (TB + 1), :], 0.0).then_inc(ready, 1)
                nc.vector.tensor_copy(lo.ident16[:, :], k.ident[:, :]).then_inc(ready, 1)
                dve.wait_ge(loaded, 16)
                nc.vector.tensor_copy(lo.shut[:, :, :], shut_f[:, :, :]).then_inc(ready, 1)
                for t in range(T):
                    nc.vector.tensor_scalar(y[0][:, t + t // TB + 1, :], k.x[:, t, :], k.mean[:, t:t + 1], k.rstd[:, t:t + 1],
                                            ALU.subtract, ALU.mult).then_inc(ready, 1)
                dve.wait_ge(ready, 7 + T)
        for l in range(2):
            local_attention(nc, k, d, l, y[0], y[1], lo)
            local_feed_forward(nc, k, d, l, y[1], y[0], lo)


def local_tables():
    f = np.float32
    half = np.arange(0, LD, 2, dtype=f)
    inv_freq = (f(1.0) / f(10000.0) ** (half / f(LD))).astype(f)
    t = np.arange(S, dtype=f)
    freqs = (t[:, None] * inv_freq[None, :]).astype(f)
    freqs = np.concatenate([freqs, freqs], axis=-1)
    base = ((half + f(0.4 * LD)) / f(1.4 * LD)).astype(f)
    power = ((t - f(S // 2)) / f(P // 2)).astype(f)
    scale = (base[None, :] ** power[:, None]).astype(f)
    scale = np.concatenate([scale, scale], axis=-1)
    sign = np.where(np.arange(LD) < LD // 2, f(-1), f(1))[None, :]
    cos, sin = np.cos(freqs), np.sin(freqs)
    i, j = np.arange(P)[:, None], np.arange(P)[None, :]
    before, here = np.where(i > j, SHUT, 0.0), np.where(i < j, SHUT, 0.0)
    usual, first = np.concatenate([before, here], axis=1), np.concatenate([np.full((P, P), SHUT), here], axis=1)
    shut = np.stack([np.tile(usual, 2), np.tile(first, 2)], axis=1)
    return {"cosq": f(8) * cos * scale, "sinq": f(8) * sin * scale * sign, "cosk": cos / scale, "sink": sin / scale * sign,
            "shut": shut.astype(f)}



def program(nc, d, out, stages=None):
    with ExitStack() as ctx:
        k = Shared()
        k.nc, k.ctx, k.stage = nc, ctx, 0
        k.stage_sems, k.stage_sem_numbers = ExitStack(), []
        s = Scope(k, ctx, "all")
        k.x = s.sb("x", [P, T, D])
        k.stats = s.sb("stats", [P, T, 6])
        k.mv, k.mean, k.var = s.sb("mv", [P, T, 2]), s.sb("mean", [P, T]), s.sb("var", [P, T])
        k.std, k.rstd = s.sb("std", [P, T]), s.sb("rstd", [P, T])
        k.ident = s.sb("ident", [P, P])
        k.ones3 = s.sb("ones3", [3, P], BF16)
        k.ctx_t = s.sb("ctxt", [P, DC, B * J])
        k.folded = {}
        k.iota, k.before = d["iota"], d["before"]
        k.zeros = s.sb("zeros", [P, 1024])
        loaded, ready = s.sem("loaded"), s.sem("ready")
        stored, = s.lasting_sems("stored", 1)
        k.slot_buffers, zeroed = {}, s.lasting_sems("zeroed", 3)
        for m, sem in zip((M0, M2, M3), zeroed):
            if stages is None or m.name in stages:
                k.slot_buffers[m.name] = (nc.dram_tensor(f"{m.name}_xbuf", (m.rows, D), F32, kind="Internal").ap(),
                                          sem, m.rows // 512)
        with nc.Block() as block:
            @block.sync
            def _(sp):
                sp.dma_start(k.x[:, :, :], d["x"].rearrange("(t p) d -> p t d", p=P)).then_inc(loaded, 16)
                sp.dma_start(k.ident[:, :], d["ident"]).then_inc(loaded, 16)
                sp.dma_start(k.ctx_t[:, :, :], d["ctx_t"].rearrange("(c p) n -> p c n", p=P)).then_inc(loaded, 16)
                sp.wait_ge(loaded, 48)

            @block.vector
            def _(dve):
                nc.vector.memset(k.zeros[:, :], 0.0)
                nc.vector.memset(k.ones3[:, :], 1.0)
                dve.wait_ge(loaded, 48)
                for t in range(T):
                    nc.vector.bn_stats(k.stats[:, t, :], k.x[:, t, :]).then_inc(ready, 1)
                dve.wait_ge(ready, T)
        k.buffers_zeroed = False
        k.fold_jobs = [(a, d[a.name]) for a in ATTENTIONS[1:] if a.name in d]
        for name, stage in STAGES:
            if stages is None or name in stages:
                stage(nc, k, d.get(name, d))
        with nc.Block() as block:
            @block.sync
            def _(sp):
                sp.dma_start(out.rearrange("(t p) d -> p t d", p=P), k.x[:, :, :]).then_inc(stored, 16)
                sp.wait_ge(stored, 16)


STAGES = []


def att_stage(a):
    STAGES.append((a.name, lambda nc, k, d: attention(nc, k, a, d)))


att_stage(ATTENTIONS[0])
STAGES.append(("m0", lambda nc, k, d: experts(nc, k, M0, d)))
att_stage(ATTENTIONS[1])
STAGES.append(("local", local_layers))
att_stage(ATTENTIONS[2])
STAGES.append(("m2", lambda nc, k, d: experts(nc, k, M2, d)))
att_stage(ATTENTIONS[3])
STAGES.append(("m3", lambda nc, k, d: experts(nc, k, M3, d)))



def block_diagonal(w, heads, a, b):
    out = np.zeros((heads, a, heads, b), w.dtype)
    for h in range(heads):
        out[h, :, h, :] = w[h]
    return out.reshape(heads * a, heads * b)


def by_slot(m, n):
    return m.reshape(n, m.shape[0] // n, -1).transpose(1, 0, 2)


def lay_out(i):
    a0, a1, a2, a3 = ATTENTIONS
    o = {
        "x": i["x"].reshape(B * S, D),
        "ctx_t": i["ctx_1024"].reshape(B * J, D).T,
        "ident": np.eye(P, dtype=np.float32),
        "iota": np.tile(np.arange(64, dtype=np.float32), (P, 1)),
        "before": np.triu(np.ones((P, P), np.float32), 1),
    }

    def att(a, wq, wk, wv, wo, bq, bk, bv, bo, mask=None):
        n = a.nslot
        o[a.name] = {
            "wq": by_slot(wq.T, n), "wk": wk, "wv": wv, "wo": by_slot(wo, n),
            "bq": bq.reshape(n, -1).T, "bk": bk.reshape(n, -1).T, "bv": bv.reshape(n, -1).T, "bo": bo.reshape(1, D),
        }
        if mask is not None:
            o[a.name]["mask"] = mask

    def diag(n):
        return block_diagonal(i[f"L0_xattn_{n}"], 16, 16, 64)

    att(a0, diag("Wq"), diag("Wk"), diag("Wv"), i["L0_xattn_Wo"].T, i["L0_xattn_bq"], i["L0_xattn_bk"],
        i["L0_xattn_bv"], i["L0_xattn_bo"], i["mask_BxSxS2_bk1"].reshape(B * S, J))
    for a, n, mask in ((a1, "L1", i["mask_BxS2_bk0"]), (a2, "L2", None)):
        att(a, *(i[f"{n}_xattn_{w}"] for w in ("Wq", "Wk", "Wv", "Wo", "bq", "bk", "bv", "bo")), mask)
    zero = np.zeros(1024, np.float32)
    wkv = i["L3_xattn_Wkv"]
    att(a3, i["L3_xattn_Wq"], wkv[:, :1024], wkv[:, 1024:], i["L3_xattn_Wo"], zero, zero, zero, i["L3_xattn_bo"])

    o["m0"] = {
        "wr": i["L0_ffn_router_w"].T, "sgu": i["L0_ffn_ws_gate_up"], "sd": i["L0_ffn_ws_down"],
        "gu": np.concatenate([i["L0_ffn_w_gate"], i["L0_ffn_w_up"]], axis=2).reshape(M0.e * D, -1),
        "down": i["L0_ffn_w_down"].reshape(-1, D),
    }
    for m, n in ((M2, "L2"), (M3, "L3")):
        o[m.name] = {
            "wr": i[f"{n}_ffn_Wg"], "w1": i[f"{n}_ffn_W1"], "w2": i[f"{n}_ffn_W2"],
            "b1": i[f"{n}_ffn_b1"].reshape(-1, P).T, "b2": i[f"{n}_ffn_b2"].reshape(-1),
        }
    o["m2"]["owner"] = (np.arange(M2.ntiles, dtype=np.int32) // (M2.stride // P))[None, :]
    o["m3"]["bg"] = i["L3_ffn_bg"]
    lf = {n: i[f"L1_ffn_{n}"] for n in ("wqkv", "q_scale", "k_scale", "wo", "ln_g", "ln_b", "w1", "b1", "w2", "b2")}
    o["local"] = {
        **{n: lf[n] for n in ("wqkv", "wo", "w1", "b1", "w2", "b2")},
        "qs": lf["q_scale"], "qs_turned": np.roll(lf["q_scale"], LD // 2, axis=1),
        "ks": lf["k_scale"], "ks_turned": np.roll(lf["k_scale"], LD // 2, axis=1),
        "gain": lf["ln_g"].reshape(2, DC, P).transpose(0, 2, 1), "offset": lf["ln_b"].reshape(2, DC, P).transpose(0, 2, 1),
        **local_tables(),
    }
    return o


def declare(nc, o, arrays, prefix="in"):
    d = {}
    for name, a in o.items():
        if isinstance(a, dict):
            d[name] = declare(nc, a, arrays, f"{prefix}_{name}")
        else:
            a = np.ascontiguousarray(a)
            arrays[f"{prefix}_{name}"] = a
            d[name] = nc.dram_tensor(f"{prefix}_{name}", a.shape, mybir.dt.from_np(a.dtype), kind="ExternalInput").ap()
    return d


def kernel(**inputs):
    import concourse.bacc as bacc
    from concourse.bass_utils import run_bass_kernel_spmd

    nc = bacc.Bacc("TRN2", target_bir_lowering=False, num_devices=1)
    arrays = {}
    d = declare(nc, lay_out({n: np.asarray(a) for n, a in inputs.items()}), arrays)
    out = nc.dram_tensor("out", (B * S, D), F32, kind="ExternalOutput").ap()
    program(nc, d, out)
    r = run_bass_kernel_spmd(nc, [arrays], core_ids=[0])
    return r.results[0]["out"].reshape(B, S, D)
```

```python
from contextlib import ExitStack

import numpy as np
import concourse.bass as bass
from concourse import mybir

F32 = mybir.dt.float32
BF16 = mybir.dt.bfloat16
U8 = mybir.dt.uint8
U32 = mybir.dt.uint32
I32 = mybir.dt.int32
ALU = mybir.AluOpType
ACT = mybir.ActivationFunctionType
AX = mybir.AxisListType.X

P = 128
B, S, D = 2, 1024, 256
T = B * S // P
TB = S // P
J = 77
DC = D // P
LN_EPS = 1e-5
MASKED = -1e9


class Steps:

    def __init__(self, sem, *names):
        self.sem, self.names, self.n = sem, names, len(names)

    def at(self, t, name):
        return (t + 2) * self.n + self.names.index(name) + 1


def row(a, t):
    return a[:, bass.ts(t, 1), :].rearrange("p o m -> p (o m)")


def col(a, t):
    return a[:, bass.ts(t, 1)]


def stand_alone(eng, waited):
    eng.sem_inc(waited, 1)


def reuse(eng, sems, t, u, per=1):
    if not isinstance(t, int) or t >= 2:
        eng.wait_ge(sems[u], (t - u) * (8 * per))


def pipeline(eng, n, *phases, peel=0):
    lead = max(lag for lag, _ in phases) + peel
    lead += lead % 2

    def step(s, u):
        for lag, body in phases:
            if not isinstance(s, int) or 0 <= s - lag < n:
                body(s - lag, (u - lag) % 2)

    for s in range(lead):
        step(s, s % 2)
    pairs = max(n - lead, 0) // 2
    if pairs:
        with eng.Fori(0, pairs, 1) as i:
            for u in range(2):
                step(i * 2 + (lead + u), u)
    for s in range(lead + 2 * pairs, n + max(lag for lag, _ in phases)):
        step(s, s % 2)


class Shared:
    pass


class Scope:

    def __init__(self, k, ctx, name):
        self.k, self.nc, self.ctx, self.name = k, k.nc, ctx, name

    def sb(self, name, shape, dt=F32):
        return self.ctx.enter_context(self.nc.sbuf_tensor(f"{self.name}_{name}", shape, dt))

    def pair(self, name, shape, dt=F32):
        return [self.sb(f"{name}{u}", shape, dt) for u in range(2)]

    def bank(self, name, width=512):
        return self.ctx.enter_context(self.nc.psum_tensor(f"{self.name}_{name}_bank", [P, width], F32))

    def sem(self, name):
        handle = self.k.stage_sems.enter_context(self.nc.semaphore(f"{self.name}_{name}"))
        self.k.stage_sem_numbers.append(handle.num)
        return handle

    def lasting_sems(self, name, n=2):
        return [self.k.ctx.enter_context(self.nc.semaphore(f"{self.name}_{name}{u}")) for u in range(n)]

    def sems(self, name, n=2):
        return [self.sem(f"{name}{u}") for u in range(n)]

    def steps(self, name, *names):
        return Steps(self.sem(name), *(names or (name,)))



def begin_stage(k):
    old, numbers = k.stage_sems, sorted(k.stage_sem_numbers)
    k.stage_sems, k.stage_sem_numbers = ExitStack(), []
    k.stage += 1
    runs = [[n, n + 1] for n in numbers if n - 1 not in numbers]
    for r in runs:
        while r[1] in numbers:
            r[1] += 1
    return old, runs


def norm_scales(nc, k):
    old, runs = begin_stage(k)
    sc = Scope(k, k.ctx, f"n{k.stage}")
    aggregated, rooted = sc.sem("aggregated"), sc.sem("rooted")
    inverted = sc.sem("inverted")
    with nc.Block() as block:
        @block.sync
        def _(sp):
            for n0, n1 in runs:
                sp.sem_clear(range(n0, n1))

        @block.vector
        def _(dve):
            for t in range(T):
                nc.vector.bn_aggr(k.mv[:, t, :], k.stats[:, t, :]).then_inc(aggregated, 1)
            dve.wait_ge(aggregated, T)
            nc.vector.tensor_scalar(k.var[:, :], k.mv[:, :, 1], LN_EPS, None, ALU.add).then_inc(aggregated, 1)
            nc.vector.tensor_copy(k.mean[:, :], k.mv[:, :, 0]).then_inc(aggregated, 1)
            dve.wait_ge(rooted, 1)
            nc.vector.reciprocal(k.rstd[:, :], k.std[:, :]).then_inc(inverted, 1)
            dve.wait_ge(inverted, 1)

        @block.scalar
        def _(act):
            act.wait_ge(aggregated, T + 1)
            nc.scalar.activation(k.std[:, :], k.var[:, :], ACT.Sqrt).then_inc(rooted, 1)
    old.close()



class Attention:

    def __init__(self, name, heads, nslot, w, parts, scale, blocks=None, mask=None):
        self.name, self.heads, self.nslot, self.w, self.parts, self.scale = name, heads, nslot, w, parts, scale
        self.hj = heads * J
        self.blocks = blocks or [range(DC)] * heads
        self.mask = mask
        self.chunks = [(c, min(P, self.hj - c)) for c in range(0, self.hj, P)]
        self.groups = [(h, min(h + 6, heads)) for h in range(0, heads, 6)]


HALVES = [[(h // 2, 64 * (h % 2), 64 * (h % 2) + 64)] for h in range(16)]
ATTENTIONS = [
    Attention("a0", 16, 8, 128, HALVES, 1 / 8, blocks=[[h // 8] for h in range(16)], mask="tokens"),
    Attention("a1", 1, 2, 128, [[(0, 0, 128), (1, 0, 128)]], 1 / 16, mask="keys"),
    Attention("a2", 16, 16, 16, [[(h, 0, 16)] for h in range(16)], 1 / 4),
    Attention("a3", 16, 8, 128, HALVES, 1 / 8),
]


class Folded:

    def __init__(self, nc, a):
        self.nrow = B * a.hj + D
        self.fold = nc.dram_tensor(f"{a.name}_dram_fold", (P, a.heads, B, DC, J), F32, kind="Internal").ap()
        self.vw = nc.dram_tensor(f"{a.name}_dram_vw", (B, a.hj, D), F32, kind="Internal").ap()
        self.row = nc.dram_tensor(f"{a.name}_dram_row", (self.nrow,), F32, kind="Internal").ap()
        self.parts = nc.dram_tensor(f"{a.name}_dram_parts", (3, self.nrow), BF16, kind="Internal").ap()


def fold_contexts(nc, k, s, block, jobs, direct=None):
    tensors = []
    for a, d in jobs:
        n, w = a.nslot, a.w
        j = Shared()
        j.a, j.d, j.n, j.w, j.out = a, d, n, w, k.folded[a.name]
        j.wk, j.wv = s.sb(a.name + "wk", [P, DC, n * w]), s.sb(a.name + "wv", [P, DC, n * w])
        j.wq, j.wo = s.sb(a.name + "wq", [w, n, D]), s.sb(a.name + "wo", [w, n, D])
        j.bk, j.bv, j.bq, j.bks = (s.sb(a.name + x, [w, n]) for x in ("bk", "bv", "bq", "bks"))
        j.kt, j.vt = s.sb(a.name + "kt", [w, n, B * J]), s.sb(a.name + "vt", [w, n, B * J])
        rows = max(p for p in range(1, P + 1) if j.out.nrow % p == 0)
        cols = j.out.nrow // rows
        j.row, j.rest, j.rest2 = (s.sb(a.name + x, [rows, cols]) for x in ("row", "rest", "rest2"))
        j.parts = [s.sb(f"{a.name}part{i}", [rows, cols], BF16) for i in range(3)]
        j.loaded = s.sem(a.name + "loaded")
        tensors.append(j)
    fold_out, row_out, vw_out = s.pair("foldout", [P, B, DC, J]), s.pair("rowout", [1, B, J]), s.pair("vwout", [J, B, D])
    kv_ps = [s.bank(f"kv{i}") for i in range(2)]
    a_ps, v_ps = [s.bank(f"a{i}") for i in range(3)], [s.bank(f"v{i}") for i in range(3)]
    projected, kv_done, bias_scaled = s.sem("projected"), s.sem("kvdone"), s.sem("bscaled")
    folded, row_copied, vw_made, vw_copied = s.sem("folded"), s.sem("rowcopied"), s.sem("vwmade"), s.sem("vwcopied")
    stored = s.sems("stored")
    bo_in, row_in, split, parts_out = s.sem("boin"), s.sem("rowin"), s.sem("split"), s.sem("partsout")
    per = 2 if direct is not None else 3
    heads = [(j, h) for j in tensors for h in range(j.a.heads)]

    @block.sync
    def _(sp):
        for j in tensors:
            sp.dma_start(j.wk[:, :, :], j.d["wk"].rearrange("(c p) n -> p c n", p=P)).then_inc(j.loaded, 16)
            sp.dma_start(j.wv[:, :, :], j.d["wv"].rearrange("(c p) n -> p c n", p=P)).then_inc(j.loaded, 16)
            for t, src in ((j.bk, "bk"), (j.bv, "bv"), (j.bq, "bq")):
                sp.dma_start(t[:, :], j.d[src]).then_inc(j.loaded, 16)
            for t, src in ((j.wq, "wq"), (j.wo, "wo")):
                sp.dma_start(t[:, :, :], j.d[src]).then_inc(j.loaded, 16)
            sp.dma_start(j.out.row[B * j.a.hj:].unsqueeze(0), j.d["bo"]).then_inc(bo_in, 16)
        for i, (j, h) in enumerate(heads):
            sp.wait_ge(row_copied, i + 1)
            if direct is None:
                sp.dma_start(j.out.fold[:, h], fold_out[i % 2][:, :, :, :]).then_inc(stored[i % 2], 16)
            sp.dma_start(j.out.row[0:B * j.a.hj].unsqueeze(0).rearrange("o (b j) -> o b j", b=B)[:, :, h * J:(h + 1) * J],
                         row_out[i % 2][:, :, :]).then_inc(stored[i % 2], 16)
            sp.wait_ge(vw_copied, i + 1)
            sp.dma_start(j.out.vw[:, h * J:(h + 1) * J, :].rearrange("b j d -> j b d"),
                         vw_out[i % 2][:, :, :]).then_inc(stored[i % 2], 16)
        for u in range(2):
            if len(heads) > u:
                sp.wait_ge(stored[u], 16 * per * ((len(heads) - u + 1) // 2))
        sp.wait_ge(bo_in, 16 * len(tensors))
        for i, j in enumerate(tensors):
            rows = j.row.shape[0]
            sp.dma_start(j.row[:, :], j.out.row.rearrange("(p n) -> p n", p=rows)).then_inc(row_in, 16)
        for i, j in enumerate(tensors):
            sp.wait_ge(split, 5 * (i + 1))
            rows = j.row.shape[0]
            for x in range(3):
                sp.dma_start(j.out.parts[x].rearrange("(p n) -> p n", p=rows), j.parts[x][:, :]).then_inc(parts_out, 16)
        sp.wait_ge(parts_out, 48 * len(tensors))

    @block.tensor
    def _(pe):
        slots, n_heads = 0, 0
        for j in tensors:
            a, n, w = j.a, j.n, j.w
            pe.wait_ge(j.loaded, 16 * 7)
            first = slots
            for i in range(n):
                ps = kv_ps[slots % 2]
                if slots >= 2:
                    pe.wait_ge(kv_done, slots - 1)
                for half, wt in enumerate((j.wk, j.wv)):
                    for c in range(DC):
                        last = nc.tensor.matmul(ps[0:w, half * 256:half * 256 + B * J], wt[:, c, i * w:(i + 1) * w],
                                                k.ctx_t[:, c, :], start=c == 0, stop=c == DC - 1)
                last.then_inc(projected, 1)
                slots += 1
            for h in range(a.heads):
                ps, vps = a_ps[n_heads % 3], v_ps[n_heads % 3]
                pe.wait_ge(kv_done, first + a.parts[h][-1][0] + 1)
                if n_heads >= 3:
                    pe.wait_ge(row_copied, n_heads - 2)
                for c in [*a.blocks[h], DC]:
                    m = P if c < DC else 1
                    for i, (slot, p0, p1) in enumerate(a.parts[h]):
                        lhs = j.wq[p0:p1, slot, c * P:(c + 1) * P] if c < DC else j.bq[p0:p1, slot:slot + 1]
                        last = nc.tensor.matmul(ps[0:m, c * 160:c * 160 + B * J], lhs, j.kt[p0:p1, slot, :],
                                                start=i == 0, stop=i == len(a.parts[h]) - 1)
                last.then_inc(folded, 1)
                if n_heads >= 3:
                    pe.wait_ge(vw_copied, n_heads - 2)
                for b in range(B):
                    for i, (slot, p0, p1) in enumerate(a.parts[h]):
                        last = nc.tensor.matmul(vps[0:J, b * D:(b + 1) * D], j.vt[p0:p1, slot, b * J:(b + 1) * J],
                                                j.wo[p0:p1, slot, :], start=i == 0, stop=i == len(a.parts[h]) - 1)
                last.then_inc(vw_made, 1)
                n_heads += 1

    @block.scalar
    def _(act):
        slots, n_heads = 0, 0
        for i, j in enumerate(tensors):
            a = j.a
            act.wait_ge(j.loaded, 16 * 7)
            nc.scalar.mul(j.bks[:, :], j.bk[:, :], a.scale).then_inc(bias_scaled, 1)
            act.wait_ge(bias_scaled, i + 1)
            for slot in range(j.n):
                ps = kv_ps[slots % 2]
                act.wait_ge(projected, slots + 1)
                nc.scalar.activation(j.kt[:, slot, :], ps[0:j.w, 0:B * J], ACT.Identity, bias=j.bks[:, slot:slot + 1], scale=a.scale)
                nc.scalar.activation(j.vt[:, slot, :], ps[0:j.w, 256:256 + B * J], ACT.Identity,
                                     bias=j.bv[:, slot:slot + 1]).then_inc(kv_done, 1)
                slots += 1
            for h in range(a.heads):
                u, ps, vps = n_heads % 2, a_ps[n_heads % 3], v_ps[n_heads % 3]
                act.wait_ge(folded, n_heads + 1)
                if n_heads >= 2:
                    act.wait_ge(stored[u], 16 * per * (n_heads // 2))
                for c in a.blocks[h]:
                    to = direct[:, h, :, c, :] if direct is not None else fold_out[u][:, :, c, :]
                    nc.scalar.copy(to, ps[:, c * 160:c * 160 + B * J].rearrange("p (b j) -> p b j", b=B))
                nc.scalar.copy(row_out[u][:, :, :], ps[0:1, DC * 160:DC * 160 + B * J].rearrange("p (b j) -> p b j", b=B)).then_inc(row_copied, 1)
                act.wait_ge(vw_made, n_heads + 1)
                nc.scalar.copy(vw_out[u][:, :, :], vps[0:J, :].rearrange("p (b d) -> p b d", b=B)).then_inc(vw_copied, 1)
                n_heads += 1

    @block.vector
    def _(dve):
        dve.wait_ge(row_in, 16 * len(tensors))
        for i, j in enumerate(tensors):
            n = 5 * i
            nc.vector.tensor_copy(j.parts[0][:, :], j.row[:, :]).then_inc(split, 1)
            dve.wait_ge(split, n + 1)
            nc.vector.tensor_tensor(j.rest[:, :], j.row[:, :], j.parts[0][:, :], ALU.subtract).then_inc(split, 1)
            dve.wait_ge(split, n + 2)
            nc.vector.tensor_copy(j.parts[1][:, :], j.rest[:, :]).then_inc(split, 1)
            dve.wait_ge(split, n + 3)
            nc.vector.tensor_tensor(j.rest2[:, :], j.rest[:, :], j.parts[1][:, :], ALU.subtract).then_inc(split, 1)
            dve.wait_ge(split, n + 4)
            nc.vector.tensor_copy(j.parts[2][:, :], j.rest2[:, :]).then_inc(split, 1)


def zero_slot_buffers(nc, k, block):
    k.buffers_zeroed = True

    @block.gpsimd
    def _(pool):
        for xbuf, zeroed, n in k.slot_buffers.values():
            for i in range(n):
                pool.dma_start(xbuf[i * 512:(i + 1) * 512, :].rearrange("(p a) d -> p (a d)", p=P), k.zeros[:, :]).then_inc(zeroed, 16)


class Ahead:

    def __init__(self, k, m, d):
        self.m, self.d = m, d
        self.ctx = ExitStack()
        s = Scope(k, self.ctx, m.name + "w")
        self.wr, self.logits = s.sb("wr", [P, DC, m.e]), s.sb("logits", [P, T, m.e])
        self.router_in, self.weights_in = s.lasting_sems("in")
        self.router_n = 1
        if m.cap is None:
            self.bias = s.sb("bias", [P, m.e])
            self.router_n += 1
        if m is M0:
            self.xn_t = s.sb("xnall", [P, DC, T * P])
        else:
            hc = m.hidden // P
            self.w1 = s.sb("w1", [P, m.e, DC, m.hidden])
            self.b1, self.b2 = s.sb("b1", [P, m.e * hc]), s.sb("b2", [P, m.e, D])
            self.owner = s.sb("owner", [1, m.ntiles], I32)
            self.weights_n = m.e + 2 + (m.cap is not None)

    def load_router(self, sp):
        m, d = self.m, self.d
        sp.dma_start(self.wr[:, :, :], d["wr"].rearrange("(c p) e -> p c e", p=P)).then_inc(self.router_in, 16)
        if m.cap is None:
            sp.dma_start(self.bias[:, :], d["bg"].partition_broadcast(P)).then_inc(self.router_in, 16)

    def load_weights(self, sp):
        m, d = self.m, self.d
        if m is not M0:
            if m.cap is not None:
                sp.dma_start(self.owner[:, :], d["owner"]).then_inc(self.weights_in, 16)
            sp.dma_start(self.b1[:, :], d["b1"]).then_inc(self.weights_in, 16)
            sp.dma_start(self.b2[:, :, :].rearrange("p e f -> p (e f)"), d["b2"].partition_broadcast(P)).then_inc(self.weights_in, 16)
            for e in range(m.e):
                sp.dma_start(self.w1[:, e, :, :], d["w1"][e].rearrange("(c p) f -> p c f", p=P)).then_inc(self.weights_in, 16)


def attention(nc, k, a, d):
    norm_scales(nc, k)
    ahead = None
    if a.name in k.experts_after:
        ahead = k.ahead = Ahead(k, *k.experts_after[a.name])
    first = a.name not in k.folded
    with ExitStack() as ctx:
        s = Scope(k, ctx, a.name)
        nch, ngr = len(a.chunks), len(a.groups)
        fold = s.sb("fold", [P, a.heads, B, DC, J])
        vw = s.sb("vw", [P, B, nch, D])
        c3 = s.sb("c3", [3, B * a.hj + D], BF16)
        if first:
            k.folded[a.name] = Folded(nc, a)
            with ExitStack() as fold_ctx:
                with nc.Block() as block:
                    fold_contexts(nc, k, Scope(k, fold_ctx, a.name + "f"), block, [(a, d)], direct=fold)
        src = k.folded[a.name]
        fold_in, vw_in, c3_in = s.sem("foldin"), s.sem("vwin"), s.sem("c3in")

        xn, xn_t = s.pair("xn", [P, D]), s.pair("xnt", [P, DC, P])
        probs, probs_t = s.pair("probs", [P, a.hj]), s.pair("probst", [P, nch, P])
        mx, total, inv = s.pair("mx", [P, a.heads]), s.pair("total", [P, a.heads]), s.pair("inv", [P, a.heads])
        turned_ps, out_ps = s.bank("turned"), s.bank("out")
        score_ps = [s.bank(f"score{g}") for g in range(3)]
        pt_ps = [s.bank(f"pt{g}") for g in range(3)]
        quads = [range(q, min(q + 4, nch)) for q in range(0, nch, 4)]
        if a.mask:
            masked = s.sb("masked", [P, 6 * J])
            drop = s.pair("drop", [P, J], U8)
            mask_in = s.sems("maskin")
            keys = s.sb("keys", [P, B, J], U8)
            factor, addend = s.sb("factor", [P, B, J]), s.sb("addend", [P, B, J])
            ready = s.sem("maskready")
            waited = s.sem("waited")

        normed = s.steps("normed")
        turned = s.steps("turned")
        copied = s.steps("copied")
        scored = s.steps("scored", *(f"g{g}" for g in range(ngr)))
        masking = s.steps("masking", *(("mul", "add") if a.mask == "keys" else (f"g{g}" for g in range(ngr))))
        maxed = s.steps("maxed", *(f"g{g}" for g in range(ngr)))
        exped = s.steps("exped", *(f"g{g}" for g in range(ngr)))
        scaled = s.steps("scaled", "inv", "probs")
        p_turned = s.steps("pturned", *(f"q{q}" for q in range(len(quads))))
        p_copied = s.steps("pcopied", *(f"q{q}" for q in range(len(quads))))
        mixed = s.steps("mixed")
        added = s.steps("added", "x", "stats")
        if ahead:
            xm, xm_t = s.pair("xm", [P, D]), s.pair("xmt", [P, DC, P])
            st6, mv = s.pair("st", [P, 6]), s.pair("mv", [P, 2])
            dve_waited = s.sem("dvewaited")
            renormed = s.steps("renormed", "copy", "aggr", "mean", "eps", "xm")
            powered, returned, recopied = s.steps("powered"), s.steps("returned"), s.steps("recopied")
            routed, logged = s.steps("routed"), s.steps("logged")

        def last_but(st, t, n, name):
            return st.at(t + n if not isinstance(t, int) else min(t + n, T - 1), name)

        with nc.Block() as block:
            if not k.buffers_zeroed:
                zero_slot_buffers(nc, k, block)

            @block.sync
            def _(sp):
                if ahead:
                    ahead.load_router(sp)
                sp.dma_start(c3[:, :], src.parts).then_inc(c3_in, 16)
                if not first:
                    sp.dma_start(fold[:, :, :, :, :], src.fold).then_inc(fold_in, 16)
                for c, (c0, rows) in enumerate(a.chunks):
                    sp.dma_start(vw[0:rows, :, c, :], src.vw[:, c0:c0 + rows, :].rearrange("b p d -> p b d")).then_inc(vw_in, 16)
                if ahead:
                    ahead.load_weights(sp)
                if a.mask == "tokens":
                    for u in range(2):
                        sp.sem_inc(mask_in[u], 16)

                    def load(t, u):
                        sp.wait_ge(masking.sem, masking.at(t - 2, masking.names[-1]))
                        sp.dma_start(drop[u][:, :], d["mask"][bass.ts(t, P), :]).then_inc(mask_in[u], 16)
                    pipeline(sp, T, (0, load))
                if a.mask == "keys":
                    sp.dma_start(keys[:, :, :], d["mask"].partition_broadcast(P)).then_inc(mask_in[0], 16)

            @block.vector
            def _(dve):
                for st in (normed, masking, maxed, scaled, added):
                    dve.sem_inc(st.sem, 2 * st.n)
                if a.mask:
                    nc.vector.memset(masked[:, :], MASKED).then_inc(ready, 1)
                    dve.wait_ge(ready, 1)
                if a.mask == "keys":
                    dve.wait_ge(mask_in[0], 16)
                    nc.vector.tensor_scalar(factor[:, :, :], keys[:, :, :], 0.0, None, ALU.not_equal).then_inc(ready, 1)
                    nc.vector.tensor_scalar(addend[:, :, :], keys[:, :, :], 0.0, MASKED, ALU.is_equal, ALU.mult).then_inc(ready, 1)
                    dve.wait_ge(ready, 3)

                def norm(t, u):
                    dve.wait_ge(turned.sem, turned.at(t - 2, "turned"))
                    nc.vector.tensor_scalar(xn[u][:, :], row(k.x, t), col(k.mean, t), col(k.rstd, t),
                                            ALU.subtract, ALU.mult).then_inc(normed.sem, 1)

                def mask_scores(t, u):
                    for g, (h0, h1) in enumerate(a.groups):
                        dve.wait_ge(scored.sem, scored.at(t, f"g{g}"))
                        if g == 0:
                            dve.wait_ge(mask_in[u], (t - u) * 8 + 32)
                        stand_alone(dve, waited)
                        nc.vector.copy_predicated(
                            score_ps[g][:, 0:(h1 - h0) * J].rearrange("p (h j) -> p h j", j=J),
                            drop[u][:, :].unsqueeze(1).broadcast_to([P, h1 - h0, J]),
                            masked[:, 0:(h1 - h0) * J].rearrange("p (h j) -> p h j", j=J)).then_inc(masking.sem, 1)

                def mask_keys(t, u):
                    ps = score_ps[0][:, 0:J]
                    dve.wait_ge(scored.sem, scored.at(t, "g0"))
                    nc.vector.tensor_tensor(ps, ps, row(factor, t // TB), ALU.mult).then_inc(masking.sem, 1)
                    dve.wait_ge(masking.sem, masking.at(t, "mul"))
                    nc.vector.tensor_tensor(ps, ps, row(addend, t // TB), ALU.add).then_inc(masking.sem, 1)

                def maxima(t, u):
                    dve.wait_ge(exped.sem, exped.at(t - 2, exped.names[-1]))
                    for g, (h0, h1) in enumerate(a.groups):
                        if a.mask:
                            dve.wait_ge(masking.sem, masking.at(t, f"g{g}" if a.mask == "tokens" else "add"))
                        else:
                            dve.wait_ge(scored.sem, scored.at(t, f"g{g}"))
                        nc.vector.tensor_reduce(mx[u][:, h0:h1], score_ps[g][:, 0:(h1 - h0) * J].rearrange("p (h j) -> p h j", j=J),
                                                AX, ALU.max, negate=True).then_inc(maxed.sem, 1)

                def scale(t, u):
                    dve.wait_ge(exped.sem, exped.at(t, exped.names[-1]))
                    p3 = probs[u][:, :].rearrange("p (h j) -> p h j", j=J)
                    nc.vector.reciprocal(inv[u][:, :], total[u][:, :]).then_inc(scaled.sem, 1)
                    dve.wait_ge(scaled.sem, scaled.at(t, "inv"))
                    nc.vector.tensor_tensor(p3, p3, inv[u][:, :].unsqueeze(2).broadcast_to([P, a.heads, J]), ALU.mult).then_inc(scaled.sem, 1)

                def add(t, u):
                    dve.wait_ge(mixed.sem, mixed.at(t, "mixed"))
                    nc.vector.tensor_tensor(row(k.x, t), row(k.x, t), out_ps[:, 0:D], ALU.add).then_inc(added.sem, 1)
                    dve.wait_ge(added.sem, added.at(t, "x"))
                    nc.vector.bn_stats(row(k.stats, t), row(k.x, t)).then_inc(added.sem, 1)

                def restat(t, u):
                    def done(name):
                        dve.wait_ge(renormed.sem, renormed.at(t, name))
                    dve.wait_ge(added.sem, added.at(t, "stats"))
                    stand_alone(dve, dve_waited)
                    nc.vector.tensor_copy(st6[u][:, :], row(k.stats, t)).then_inc(renormed.sem, 1)
                    done("copy")
                    stand_alone(dve, dve_waited)
                    nc.vector.bn_aggr(mv[u][:, :], st6[u][:, :]).then_inc(renormed.sem, 1)
                    done("aggr")
                    stand_alone(dve, dve_waited)
                    nc.vector.tensor_copy(col(k.mean, t), mv[u][:, 0:1]).then_inc(renormed.sem, 1)
                    nc.vector.tensor_scalar(col(k.var, t), mv[u][:, 1:2], LN_EPS, None, ALU.add).then_inc(renormed.sem, 1)

                def renorm(t, u):
                    dve.wait_ge(powered.sem, powered.at(t, "powered"))
                    dve.wait_ge(returned.sem, returned.at(t - 2, "returned"))
                    nc.vector.tensor_scalar(xm[u][:, :], row(k.x, t), col(k.mean, t), col(k.rstd, t),
                                            ALU.subtract, ALU.mult).then_inc(renormed.sem, 1)

                def log(t, u):
                    e = ahead.m.e
                    if isinstance(t, int) and t == 0:
                        dve.wait_ge(ahead.router_in, 16 * ahead.router_n)
                    dve.wait_ge(routed.sem, routed.at(t, "routed"))
                    if ahead.m.cap is None:
                        nc.vector.tensor_tensor(row(ahead.logits, t), out_ps[:, D:D + e], ahead.bias[:, :], ALU.add).then_inc(logged.sem, 1)
                    else:
                        stand_alone(dve, dve_waited)
                        nc.vector.tensor_copy(row(ahead.logits, t), out_ps[:, D:D + e]).then_inc(logged.sem, 1)

                masks = [(2, mask_scores if a.mask == "tokens" else mask_keys)] if a.mask else []
                if ahead:
                    for st in (renormed, logged):
                        dve.sem_inc(st.sem, 2 * st.n)
                    pipeline(dve, T, (0, norm), (5, renorm), (4, restat), (7, log), *masks, (2, maxima), (2, scale), (3, add))
                else:
                    pipeline(dve, T, (0, norm), *masks, (2, maxima), (2, scale), (3, add))

            if ahead:
                @block.gpsimd
                def _(pool):
                    pool.sem_inc(powered.sem, 2)

                    def power(t, u):
                        pool.wait_ge(renormed.sem, renormed.at(t, "eps"))
                        nc.gpsimd.tensor_tensor(col(k.rstd, t), col(k.var, t), k.minus_half[:, 0:1], ALU.pow).then_inc(powered.sem, 1)
                    pipeline(pool, T, (0, power))

            @block.scalar
            def _(act):
                for st in (copied, exped, p_copied):
                    act.sem_inc(st.sem, 2 * st.n)

                def copy_x(t, u):
                    act.wait_ge(turned.sem, turned.at(t, "turned"))
                    act.wait_ge(scored.sem, scored.at(t - 2, scored.names[-1]))
                    nc.scalar.copy(xn_t[u][:, :, :], turned_ps[:, 0:D].rearrange("p (c n) -> p c n", c=DC)).then_inc(copied.sem, 1)

                def exp(t, u):
                    act.wait_ge(p_turned.sem, p_turned.at(t - 2, p_turned.names[-1]))
                    for g, (h0, h1) in enumerate(a.groups):
                        act.wait_ge(maxed.sem, maxed.at(t, f"g{g}"))
                        for h in range(h0, h1):
                            last = nc.scalar.activation(probs[u][:, h * J:(h + 1) * J], score_ps[g][:, (h - h0) * J:(h - h0 + 1) * J], ACT.Exp,
                                                        bias=mx[u][:, h:h + 1], accum_out=total[u][:, h:h + 1])
                        last.then_inc(exped.sem, 1)

                def copy_p(t, u):
                    for q, cs in enumerate(quads):
                        act.wait_ge(p_turned.sem, p_turned.at(t, f"q{q}"))
                        if q == 0:
                            act.wait_ge(mixed.sem, mixed.at(t - 2, "mixed"))
                        whole = [c for c in cs if a.chunks[c][1] == P]
                        last = None
                        if whole:
                            last = nc.scalar.copy(probs_t[u][:, whole[0]:whole[-1] + 1, :],
                                                  pt_ps[q][:, 0:len(whole) * P].rearrange("p (c n) -> p c n", n=P))
                        for c in cs:
                            if a.chunks[c][1] < P:
                                n = a.chunks[c][1]
                                last = nc.scalar.copy(probs_t[u][0:n, c, :], pt_ps[q][0:n, (c - cs[0]) * P:(c - cs[0] + 1) * P])
                        last.then_inc(p_copied.sem, 1)

                def recopy(t, u):
                    act.wait_ge(returned.sem, returned.at(t, "returned"))
                    act.wait_ge(routed.sem, routed.at(t - 2, "routed"))
                    x_t = turned_ps[:, 0:D].rearrange("p (c n) -> p c n", c=DC)
                    if ahead.m is M0:
                        nc.scalar.copy(ahead.xn_t[:, :, bass.ts(t, P)], x_t)
                    nc.scalar.copy(xm_t[u][:, :, :], x_t).then_inc(recopied.sem, 1)

                if ahead:
                    act.sem_inc(recopied.sem, 2)
                    pipeline(act, T, (3, copy_p), (2, exp), (0, copy_x), (5, recopy))
                else:
                    pipeline(act, T, (3, copy_p), (2, exp), (0, copy_x))

            @block.tensor
            def _(pe):
                for st in (turned, scored, p_turned, mixed):
                    pe.sem_inc(st.sem, 2 * st.n)

                def turn(t, u):
                    pe.wait_ge(normed.sem, normed.at(t, "normed"))
                    pe.wait_ge(copied.sem, copied.at(t - 1, "copied"))
                    if ahead and (not isinstance(t, int) or t >= 6):
                        pe.wait_ge(recopied.sem, recopied.at(t - 6, "recopied"))
                    for c in range(DC):
                        last = nc.tensor.transpose(turned_ps[:, c * P:(c + 1) * P], xn[u][:, c * P:(c + 1) * P], k.ident[:, :])
                    last.then_inc(turned.sem, 1)

                def return_x(t, u):
                    pe.wait_ge(renormed.sem, renormed.at(t, "xm"))
                    pe.wait_ge(copied.sem, last_but(copied, t, 5, "copied"))
                    pe.wait_ge(recopied.sem, recopied.at(t - 1, "recopied"))
                    for c in range(DC):
                        last = nc.tensor.transpose(turned_ps[:, c * P:(c + 1) * P], xm[u][:, c * P:(c + 1) * P], k.ident[:, :])
                    last.then_inc(returned.sem, 1)

                def route_x(t, u):
                    if isinstance(t, int) and t == 0:
                        pe.wait_ge(ahead.router_in, 16 * ahead.router_n)
                    pe.wait_ge(recopied.sem, recopied.at(t, "recopied"))
                    pe.wait_ge(added.sem, last_but(added, t, 3, "x"))
                    pe.wait_ge(logged.sem, logged.at(t - 1, "logged"))
                    for c in range(DC):
                        last = nc.tensor.matmul(out_ps[:, D:D + ahead.m.e], xm_t[u][:, c, :], ahead.wr[:, c, :], start=c == 0, stop=c == DC - 1)
                    last.then_inc(routed.sem, 1)

                def score(t, u):
                    pe.wait_ge(copied.sem, copied.at(t, "copied"))
                    b = t // TB
                    if isinstance(t, int) and t == 0:
                        pe.wait_ge(c3_in, 16)
                        if not first:
                            pe.wait_ge(fold_in, 16)
                    for g, (h0, h1) in enumerate(a.groups):
                        width = (h1 - h0) * J
                        pe.wait_ge(exped.sem, exped.at(t - 1, f"g{g}"))
                        nc.tensor.matmul(score_ps[g][:, 0:width], k.ones3[:, :], c3[:, bass.ds(b * a.hj + h0 * J, width)],
                                         start=True, stop=False, skip_group_check=True)
                        for c in range(DC):
                            hs = [h for h in range(h0, h1) if c in a.blocks[h]]
                            if hs:
                                last = nc.tensor.matmul(score_ps[g][:, (hs[0] - h0) * J:(hs[-1] + 1 - h0) * J].rearrange("p (h j) -> p h j", j=J),
                                                        xn_t[u][:, c, :], fold[:, hs[0]:hs[-1] + 1, bass.ds(b, 1), c, :].rearrange("p h o j -> p h (o j)"),
                                                        start=False, stop=True, skip_group_check=True)
                        last.then_inc(scored.sem, 1)

                def turn_p(t, u):
                    pe.wait_ge(scaled.sem, scaled.at(t, "probs"))
                    for q, cs in enumerate(quads):
                        pe.wait_ge(p_copied.sem, p_copied.at(t - 1, f"q{q}"))
                        for c in cs:
                            c0, n = a.chunks[c]
                            last = nc.tensor.transpose(pt_ps[q][0:n, (c - cs[0]) * P:(c - cs[0] + 1) * P],
                                                       probs[u][:, c0:c0 + n], k.ident[:, :])
                        last.then_inc(p_turned.sem, 1)

                def mix(t, u):
                    b = t // TB
                    if isinstance(t, int) and t == 0:
                        pe.wait_ge(vw_in, 16 * nch)
                    pe.wait_ge(added.sem, added.at(t - 1, "x"))
                    if ahead and (not isinstance(t, int) or t >= 4):
                        pe.wait_ge(logged.sem, logged.at(t - 4, "logged"))
                    nc.tensor.matmul(out_ps[:, 0:D], k.ones3[:, :], c3[:, B * a.hj:], start=True, stop=False)
                    for q, cs in enumerate(quads):
                        pe.wait_ge(p_copied.sem, p_copied.at(t, f"q{q}"))
                        for c in cs:
                            n = a.chunks[c][1]
                            last = nc.tensor.matmul(out_ps[:, 0:D], probs_t[u][0:n, c, :],
                                                    vw[0:n, bass.ds(b, 1), c, :].rearrange("p o n -> p (o n)"),
                                                    start=False, stop=c == nch - 1)
                    last.then_inc(mixed.sem, 1)

                if ahead:
                    for st in (returned, routed):
                        pe.sem_inc(st.sem, 2 * st.n)
                    pipeline(pe, T, (3, turn_p), (3, mix), (1, score), (0, turn), (5, return_x), (6, route_x))
                else:
                    pipeline(pe, T, (3, turn_p), (3, mix), (1, score), (0, turn))



class Experts:

    def __init__(self, name, e, top, hidden, cap, stride, ntiles, act, group):
        self.name, self.e, self.top, self.hidden, self.cap, self.stride = name, e, top, hidden, cap, stride
        self.ntiles, self.act, self.group = ntiles, act, group
        self.rows = ntiles * P


M0 = Experts("m0", 64, 8, 192, 128, 128, 64, ACT.Silu, 4)
M2 = Experts("m2", 8, 2, 1024, 538, 640, 40, ACT.Gelu_apprx_tanh, 8)
M3 = Experts("m3", 8, 2, 1024, None, None, 2 * T + 8, ACT.Gelu, 8)
NOWHERE = 100000.0
TOP_EPS = 1e-12


def route(nc, k, m, d, r):
    shared = m is M0
    E, K, G = m.e, m.top, m.group
    groups = T // G
    F = m.hidden
    HC, HP = 2, F // 2
    N = G * P
    with ExitStack() as ctx:
        s = Scope(k, ctx, m.name + "r")
        lg, pr = r.ahead.logits, s.sb("pr", [P, G, E])
        mx, tot, inv = s.sb("mx", [P, G]), s.sb("tot", [P, G]), s.sb("inv", [P, G])
        top, idx, idxf = s.sb("top", [P, G, 8]), s.sb("idx", [P, G, 8], U32), s.sb("idxf", [P, G, K])
        onehot, picked = s.sb("onehot", [P, G, K, E]), s.sb("picked", [P, G, K, E])
        mask, cum = s.pair("mask", [P, G, E]), s.pair("cum", [P, G + 1, E])
        pos, over, kept, slotf = (s.sb(n, [P, G, K]) for n in ("pos", "over", "kept", "slotf"))
        tsum, tmax, tinv, wk = s.sb("tsum", [P, G]), s.sb("tmax", [P, G]), s.sb("tinv", [P, G]), s.sb("wk", [P, G, K])
        y_ps, pos_ps = [s.bank("y0"), s.bank("y1")], s.bank("pos")
        gu_ps = s.bank("gu", 2048)
        if shared:
            wgu, wd = s.sb("wgu", [P, DC, 2 * F]), s.sb("wd", [HP, HC, D])
            gate, h_t = s.sb("gate", [HP, HC, N]), s.pair("ht", [HP, HC, N])
        if m.cap is not None:
            xs, slot = s.pair("xs", [P, G, D]), s.pair("slot", [P, G, K], U32)
        loaded, cleared, waited, pool_waited = s.sem("loaded"), s.sem("cleared"), s.sem("waited"), s.sem("poolwaited")
        scattered = s.lasting_sems("scattered")
        nload = 2 * shared
        shifted, exped = s.steps("shifted", "max", "sub"), s.steps("exped")
        ranked = s.steps("ranked", "sum", "inv", "prob", "top", "idx", "idxf", "onehot", "mask", *(f"cum{j}" for j in range(G)))
        counted = s.steps("counted")
        placed = s.steps("placed", "picked", "pos", "tsum", "tmax", "tinv", "wk", "kept", "over", "slotf", "slot", "rows", "slots", "weights")
        gu_made, gated, hidden, y_made, added = (s.steps(n) for n in ("gumade", "gated", "hidden", "ymade", "added"))

        def per_e(ap):
            return ap.rearrange("p g k -> p (g k)").unsqueeze(2).broadcast_to([P, G * K, E])

        with nc.Block() as block:
            @block.sync
            def _(sp):
                for n0, n1 in r.old_runs:
                    sp.sem_clear(range(n0, n1))
                if shared:
                    sp.dma_start(wgu[:, :, :], d["sgu"].rearrange("(c p) f -> p c f", p=P)).then_inc(loaded, 16)
                    sp.dma_start(wd[:, :, :], d["sd"].rearrange("(c p) f -> p c f", p=HP)).then_inc(loaded, 16)
                if m is not M0:
                    for e in range(E):
                        sp.dma_start(r.w2[:, e, :, :], d["w2"][e].rearrange("(c p) f -> p c f", p=P)).then_inc(r.w_in, 16)

            @block.gpsimd
            def _(pool):
                if m.cap is None:
                    return
                pool.wait_ge(r.zeroed, 16 * r.nzero)

                def scatter(c, u):
                    pool.wait_ge(placed.sem, placed.at(c, "rows"))
                    stand_alone(pool, pool_waited)
                    for j in range(G):
                        for i in range(K):
                            nc.gpsimd.indirect_dma_start(r.xbuf[:, :], bass.IndirectOffsetOnAxis(slot[u][:, j, i:i + 1], 0), xs[u][:, j, :], None,
                                                         bounds_check=m.rows - 1, oob_is_err=False).then_inc(scattered[u], 16)
                pipeline(pool, groups, (0, scatter))
                for u in range(2):
                    pool.wait_ge(scattered[u], 16 * G * K * (groups // 2))

            @block.vector
            def _(dve):
                for st in (shifted, ranked, placed, hidden, added):
                    dve.sem_inc(st.sem, 2 * st.n)
                nc.vector.memset(cum[0][:, 0, :], 0.0).then_inc(cleared, 1)
                dve.wait_ge(cleared, 1)

                def rank(c, u):
                    def done(name):
                        dve.wait_ge(ranked.sem, ranked.at(c, name))
                    lgc = lg[:, bass.ts(c, G), :]
                    nc.vector.tensor_reduce(mx[:, :], lgc, AX, ALU.max).then_inc(shifted.sem, 1)
                    dve.wait_ge(shifted.sem, shifted.at(c, "max"))
                    nc.vector.tensor_tensor(lgc, lgc, mx[:, :].unsqueeze(2).broadcast_to([P, G, E]), ALU.subtract).then_inc(shifted.sem, 1)
                    dve.wait_ge(exped.sem, exped.at(c, "exped"))
                    nc.vector.tensor_reduce(tot[:, :], pr[:, :, :], AX, ALU.add).then_inc(ranked.sem, 1)
                    done("sum")
                    nc.vector.reciprocal(inv[:, :], tot[:, :]).then_inc(ranked.sem, 1)
                    done("inv")
                    nc.vector.tensor_tensor(pr[:, :, :], pr[:, :, :], inv[:, :].unsqueeze(2).broadcast_to([P, G, E]), ALU.mult).then_inc(ranked.sem, 1)
                    done("prob")
                    stand_alone(dve, waited)
                    for j in range(G):
                        last = nc.vector.max(top[:, j, :], pr[:, j, :])
                    last.then_inc(ranked.sem, 1)
                    done("top")
                    stand_alone(dve, waited)
                    for j in range(G):
                        last = nc.vector.max_index(idx[:, j, :], top[:, j, :], pr[:, j, :])
                    last.then_inc(ranked.sem, 1)
                    done("idx")
                    nc.vector.tensor_copy(idxf[:, :, :], idx[:, :, 0:K]).then_inc(ranked.sem, 1)
                    done("idxf")
                    nc.vector.tensor_tensor(onehot[:, :, :, :].rearrange("p g k e -> p (g k) e"),
                                            r.iota[:, 0:E].unsqueeze(1).broadcast_to([P, G * K, E]), per_e(idxf[:, :, :]), ALU.is_equal).then_inc(ranked.sem, 1)
                    done("onehot")
                    nc.vector.tensor_reduce(mask[u][:, :, :], onehot[:, :, :, :].rearrange("p g k e -> p g e k"), AX, ALU.add).then_inc(ranked.sem, 1)
                    done("mask")
                    dve.wait_ge(counted.sem, counted.at(c - 1, "counted"))
                    for j in range(G):
                        after = cum[u][:, j + 1, :] if j < G - 1 else cum[1 - u][:, 0, :]
                        nc.vector.tensor_tensor(after, cum[u][:, j, :], mask[u][:, j, :], ALU.add).then_inc(ranked.sem, 1)
                        done(f"cum{j}")

                def place(c, u):
                    def done(name):
                        dve.wait_ge(placed.sem, placed.at(c, name))
                    dve.wait_ge(counted.sem, counted.at(c, "counted"))
                    for j in range(G):
                        last = nc.vector.tensor_tensor(picked[:, j, :, :], onehot[:, j, :, :],
                                                       pos_ps[:, j * E:(j + 1) * E].unsqueeze(1).broadcast_to([P, K, E]), ALU.mult)
                    last.then_inc(placed.sem, 1)
                    done("picked")
                    nc.vector.tensor_reduce(pos[:, :, :].rearrange("p g k -> p (g k)"), picked[:, :, :, :].rearrange("p g k e -> p (g k) e"),
                                            AX, ALU.add).then_inc(placed.sem, 1)
                    nc.vector.tensor_reduce(tsum[:, :], top[:, :, 0:K], AX, ALU.add).then_inc(placed.sem, 1)
                    done("tsum")
                    nc.vector.tensor_scalar(tmax[:, :], tsum[:, :], TOP_EPS, None, ALU.max).then_inc(placed.sem, 1)
                    done("tmax")
                    nc.vector.reciprocal(tinv[:, :], tmax[:, :]).then_inc(placed.sem, 1)
                    done("tinv")
                    nc.vector.tensor_tensor(wk[:, :, :], top[:, :, 0:K], tinv[:, :].unsqueeze(2).broadcast_to([P, G, K]), ALU.mult).then_inc(placed.sem, 1)
                    cap = float(m.cap or B * S + 1)
                    nc.vector.tensor_scalar(kept[:, :, :], pos[:, :, :], cap, None, ALU.is_lt).then_inc(placed.sem, 1)
                    nc.vector.tensor_scalar(over[:, :, :], pos[:, :, :], cap, NOWHERE, ALU.is_ge, ALU.mult).then_inc(placed.sem, 1)
                    done("over")
                    nc.vector.scalar_tensor_tensor(slotf[:, :, :], idxf[:, :, :], float(m.stride or 0), pos[:, :, :],
                                                   ALU.mult, ALU.add).then_inc(placed.sem, 1)
                    done("slotf")
                    if m.cap is None:
                        nc.vector.tensor_copy(r.idxf[:, bass.ts(c, G), :], idxf[:, :, :]).then_inc(placed.sem, 1)
                        nc.vector.tensor_copy(r.pos[:, bass.ts(c, G), :], pos[:, :, :]).then_inc(placed.sem, 2)
                    else:
                        reuse(dve, scattered, c, u, G * K)
                        nc.vector.tensor_tensor(slot[u][:, :, :], slotf[:, :, :], over[:, :, :], ALU.add).then_inc(placed.sem, 1)
                        for j in range(G):
                            last = nc.vector.tensor_scalar(xs[u][:, j, :], row(k.x, c * G + j), col(k.mean, c * G + j), col(k.rstd, c * G + j),
                                                           ALU.subtract, ALU.mult)
                        last.then_inc(placed.sem, 1)
                        done("slot")
                        nc.vector.tensor_copy(r.slots[:, bass.ts(c, G), :], slot[u][:, :, :]).then_inc(placed.sem, 1)
                    nc.vector.tensor_tensor(r.weights[:, bass.ts(c, G), :], wk[:, :, :], kept[:, :, :], ALU.mult).then_inc(placed.sem, 1)

                def hide(c, u):
                    dve.wait_ge(gated.sem, gated.at(c, "gated"))
                    dve.wait_ge(y_made.sem, y_made.at(c - 2, "ymade"))
                    nc.vector.tensor_tensor(h_t[u][:, :, :].rearrange("p h n -> p (h n)"), gate[:, :, :].rearrange("p h n -> p (h n)"),
                                            gu_ps[0:HP, 1024:2048], ALU.mult).then_inc(hidden.sem, 1)

                def add(c, u):
                    dve.wait_ge(y_made.sem, y_made.at(c, "ymade"))
                    for i in range(2):
                        xi = k.x[:, bass.ts(c * 2 + i, G // 2), :].rearrange("p t d -> p (t d)")
                        last = nc.vector.tensor_tensor(xi, xi, y_ps[i][:, 0:G // 2 * D], ALU.add)
                    last.then_inc(added.sem, 1)

                if shared:
                    pipeline(dve, groups, (0, rank), (0, place), (1, hide), (1, add), peel=2)
                else:
                    pipeline(dve, groups, (0, rank), (0, place), peel=2)
                dve.wait_ge(placed.sem, placed.at(groups - 1, "weights"))

            @block.scalar
            def _(act):
                for st in (exped, gated):
                    act.sem_inc(st.sem, 2 * st.n)

                def exp(c, u):
                    act.wait_ge(shifted.sem, shifted.at(c, "sub"))
                    act.wait_ge(ranked.sem, ranked.at(c - 1, "idx"))
                    nc.scalar.activation(pr[:, :, :], lg[:, bass.ts(c, G), :], ACT.Exp).then_inc(exped.sem, 1)

                def silu(c, u):
                    act.wait_ge(gu_made.sem, gu_made.at(c, "gumade"))
                    act.wait_ge(hidden.sem, hidden.at(c - 1, "hidden"))
                    nc.scalar.activation(gate[:, :, :].rearrange("p h n -> p (h n)"), gu_ps[0:HP, 0:1024], ACT.Silu).then_inc(gated.sem, 1)

                pipeline(act, groups, *([(0, exp)] + [(0, silu)] * shared))

            @block.tensor
            def _(pe):
                for st in (counted, gu_made, y_made):
                    pe.sem_inc(st.sem, 2 * st.n)
                pe.wait_ge(cleared, 1)

                def gate_up(c, u):
                    pe.wait_ge(hidden.sem, hidden.at(c - 1, "hidden"))
                    for i in range(2 * HC):
                        for dc in range(DC):
                            last = nc.tensor.matmul(gu_ps[0:HP, i * 512:(i + 1) * 512], wgu[:, dc, i * HP:(i + 1) * HP], r.ahead.xn_t[:, dc, bass.ts(c, N)],
                                                    start=dc == 0, stop=dc == DC - 1)
                    last.then_inc(gu_made.sem, 1)

                def count(c, u):
                    pe.wait_ge(ranked.sem, ranked.at(c, f"cum{G - 1}"))
                    pe.wait_ge(placed.sem, placed.at(c - 1, "picked"))
                    nc.tensor.matmul(pos_ps[:, 0:G * E], r.before[:, :], mask[u][:, :, :].rearrange("p g e -> p (g e)"), start=True, stop=False)
                    nc.tensor.matmul(pos_ps[:, 0:G * E], r.ones[:, :], cum[u][:, 0:G, :].rearrange("p g e -> p (g e)"), start=False, stop=True).then_inc(counted.sem, 1)

                def down(c, u):
                    pe.wait_ge(hidden.sem, hidden.at(c, "hidden"))
                    pe.wait_ge(added.sem, added.at(c - 1, "added"))
                    for j in range(G):
                        for h in range(HC):
                            last = nc.tensor.matmul(y_ps[j // 2][:, j % 2 * D:(j % 2 + 1) * D], h_t[u][:, h, j * P:(j + 1) * P], wd[:, h, :],
                                                    start=h == 0, stop=h == HC - 1)
                    last.then_inc(y_made.sem, 1)

                if nload:
                    pe.wait_ge(loaded, 16 * nload)
                if shared:
                    pipeline(pe, groups, (0, count), (0, gate_up), (1, down))
                else:
                    pipeline(pe, groups, (0, count))
                    if m.cap is None:
                        pe.wait_ge(placed.sem, placed.at(groups - 1, "picked"))
                        nc.tensor.matmul(pos_ps[:, 0:E], r.ones[:, :], cum[groups % 2][:, 0, :], start=True, stop=True).then_inc(r.totals, 1)

        r.old_sems.close()
        if m.cap is None:
            lay_out_slots(nc, k, m, r, pos_ps, scattered)


def lay_out_slots(nc, k, m, r, pos_ps, scattered):
    E, K = m.e, m.top
    with ExitStack() as ctx:
        s = Scope(k, ctx, m.name + "s")
        up, whole = s.sb("up", [P, E], I32), s.sb("whole", [P, E], I32)
        size, start = s.sb("size", [P, E]), s.sb("start", [P, E + 1])
        owner, owned, ownerf = s.sb("owner", [1, m.ntiles, E - 1]), s.sb("owned", [1, m.ntiles]), s.sb("ownerf", [1, m.ntiles])
        onehot = s.sb("onehot", [P, T * K, E])
        base, slotf = s.sb("base", [P, T * K]), s.sb("slotf", [P, T * K])
        xs, slot = s.pair("xs", [P, D]), s.pair("slot", [P, K], U32)
        pool_waited = s.sem("poolwaited")
        chain, normed, copied = s.sem("chain"), s.steps("normed"), s.steps("copied")
        with nc.Block() as block:
            @block.vector
            def _(dve):
                for st in (normed, copied):
                    dve.sem_inc(st.sem, 2 * st.n)
                step = 0

                def then(ins):
                    nonlocal step
                    step += 1
                    ins.then_inc(chain, 1)
                    dve.wait_ge(chain, step)

                dve.wait_ge(r.totals, 1)
                then(nc.vector.tensor_scalar(up[:, :], pos_ps[:, 0:E], float(P - 1), None, ALU.add))
                then(nc.vector.tensor_scalar(whole[:, :], up[:, :], P.bit_length() - 1, None, ALU.arith_shift_right))
                then(nc.vector.tensor_copy(size[:, :], whole[:, :]))
                then(nc.vector.memset(start[:, 0:1], 0.0))
                for e in range(E):
                    then(nc.vector.tensor_tensor(start[:, e + 1:e + 2], start[:, e:e + 1], size[:, e:e + 1], ALU.add))
                then(nc.vector.tensor_tensor(owner[:, :, :], r.iota[0:1, 0:m.ntiles].unsqueeze(2).broadcast_to([1, m.ntiles, E - 1]),
                                             start[0:1, 1:E].unsqueeze(1).broadcast_to([1, m.ntiles, E - 1]), ALU.is_ge))
                then(nc.vector.tensor_reduce(ownerf[:, :], owner[:, :, :], AX, ALU.add))
                then(nc.vector.tensor_copy(r.owner[:, :], ownerf[:, :]))
                idxs = r.idxf[:, :, :].rearrange("p t k -> p (t k)")
                then(nc.vector.tensor_tensor(onehot[:, :, :], r.iota[:, 0:E].unsqueeze(1).broadcast_to([P, T * K, E]),
                                             idxs.unsqueeze(2).broadcast_to([P, T * K, E]), ALU.is_equal))
                then(nc.vector.tensor_tensor(onehot[:, :, :], onehot[:, :, :],
                                             start[:, 0:E].unsqueeze(1).broadcast_to([P, T * K, E]), ALU.mult))
                then(nc.vector.tensor_reduce(base[:, :], onehot[:, :, :], AX, ALU.add))
                then(nc.vector.scalar_tensor_tensor(slotf[:, :], base[:, :], float(P), r.pos[:, :, :].rearrange("p t k -> p (t k)"),
                                                    ALU.mult, ALU.add))
                then(nc.vector.tensor_copy(r.slots[:, :, :].rearrange("p t k -> p (t k)"), slotf[:, :]))

                def prepare(t, u):
                    reuse(dve, scattered, t, u, K)
                    nc.vector.tensor_scalar(xs[u][:, :], row(k.x, t), col(k.mean, t), col(k.rstd, t),
                                            ALU.subtract, ALU.mult).then_inc(normed.sem, 1)
                    nc.vector.tensor_copy(slot[u][:, :], row(r.slots, t)).then_inc(copied.sem, 1)
                pipeline(dve, T, (0, prepare), peel=2)

            @block.gpsimd
            def _(pool):
                pool.wait_ge(r.zeroed, 16 * r.nzero)

                def scatter(t, u):
                    pool.wait_ge(normed.sem, normed.at(t, "normed"))
                    pool.wait_ge(copied.sem, copied.at(t, "copied"))
                    stand_alone(pool, pool_waited)
                    for i in range(K):
                        nc.gpsimd.indirect_dma_start(r.xbuf[:, :], bass.IndirectOffsetOnAxis(slot[u][:, i:i + 1], 0), xs[u][:, :], None,
                                                     bounds_check=m.rows - 1, oob_is_err=False).then_inc(scattered[u], 16)
                pipeline(pool, T, (0, scatter))
                for u in range(2):
                    pool.wait_ge(scattered[u], 16 * K * (T // 2))


def narrow_experts(nc, k, m, d, r):
    F, HC = m.hidden, 2
    HP = F // HC
    npair = m.ntiles // 2
    with ExitStack() as ctx:
        s = Scope(k, ctx, m.name + "e")
        xb, xt = s.pair("xb", [P, 2, D]), s.pair("xt", [P, DC, 2, P])
        wgu, wd = s.pair("wgu", [P, 2 * DC, 2 * F]), s.pair("wd", [HP, 2 * HC, D])
        gate, h_t, y = s.pair("gate", [HP, 2, HC * P]), s.pair("ht", [HP, 2, HC * P]), s.pair("y", [P, 2, D])
        turned_ps, y_ps = [s.bank("turned0"), s.bank("turned1")], [s.bank("y0"), s.bank("y1")]
        gu_ps = [s.bank(f"gu{u}", 1024) for u in range(2)]
        x_in, wgu_in, wd_in, stored = s.sems("xin"), s.sems("wguin"), s.sems("wdin"), s.lasting_sems("stored")
        turned, copied, gu_made, gated, hidden = (s.steps(n) for n in ("turned", "copied", "gumade", "gated", "hidden"))
        y_made, y_copied = s.steps("ymade"), s.steps("ycopied")

        def nth(q, u):
            return (q - u) * 8 + 32

        with nc.Block() as block:
            @block.sync
            def _(sp):
                for u in range(2):
                    for sem in (x_in[u], wgu_in[u], wd_in[u]):
                        sp.sem_inc(sem, 16)

                def load_x(q, u):
                    sp.wait_ge(turned.sem, turned.at(q - 2, "turned"))
                    sp.dma_start(xb[u][:, :, :], r.xbuf[bass.ts(q, 2 * P), :].rearrange("(i p) d -> p i d", p=P)).then_inc(x_in[u], 16)

                def load_w(q, u):
                    sp.wait_ge(gu_made.sem, gu_made.at(q - 2, "gumade"))
                    sp.dma_start(wgu[u][:, :, :], d["gu"][bass.ts(q, 2 * D), :].rearrange("(c p) f -> p c f", p=P)).then_inc(wgu_in[u], 16)
                    sp.wait_ge(y_made.sem, y_made.at(q - 2, "ymade"))
                    sp.dma_start(wd[u][:, :, :], d["down"][bass.ts(q, 2 * F), :].rearrange("(c p) f -> p c f", p=HP)).then_inc(wd_in[u], 16)
                pipeline(sp, npair, (0, load_x), (1, load_w))

            @block.gpsimd
            def _(pool):
                def store(q, u):
                    pool.wait_ge(y_copied.sem, y_copied.at(q, "ycopied"))
                    pool.dma_start(r.ybuf[bass.ts(q, 2 * P), :].rearrange("(i p) d -> p i d", p=P), y[u][:, :, :]).then_inc(stored[u], 16)
                pipeline(pool, npair, (0, store))
                for u in range(2):
                    pool.wait_ge(stored[u], 16 * (npair // 2))

            @block.tensor
            def _(pe):
                for st in (turned, gu_made, y_made):
                    pe.sem_inc(st.sem, 2 * st.n)

                def turn(q, u):
                    pe.wait_ge(x_in[u], nth(q, u))
                    pe.wait_ge(copied.sem, copied.at(q - 2, "copied"))
                    for c in range(DC):
                        for i in range(2):
                            o = (2 * c + i) * P
                            last = nc.tensor.transpose(turned_ps[u][:, o:o + P], xb[u][:, i, c * P:(c + 1) * P], k.ident[:, :])
                    last.then_inc(turned.sem, 1)

                def gate_up(q, u):
                    pe.wait_ge(wgu_in[u], nth(q, u))
                    pe.wait_ge(copied.sem, copied.at(q, "copied"))
                    pe.wait_ge(hidden.sem, hidden.at(q - 2, "hidden"))
                    for i in range(2):
                        for j in range(2 * HC):
                            for c in range(DC):
                                last = nc.tensor.matmul(gu_ps[u][0:HP, i * 512 + j * P:i * 512 + (j + 1) * P],
                                                        wgu[u][:, i * DC + c, j * HP:(j + 1) * HP], xt[u][:, c, i, :],
                                                        start=c == 0, stop=c == DC - 1)
                    last.then_inc(gu_made.sem, 1)

                def down(q, u):
                    pe.wait_ge(wd_in[u], nth(q, u))
                    pe.wait_ge(hidden.sem, hidden.at(q, "hidden"))
                    pe.wait_ge(y_copied.sem, y_copied.at(q - 2, "ycopied"))
                    for i in range(2):
                        for c in range(HC):
                            last = nc.tensor.matmul(y_ps[u][:, i * D:(i + 1) * D], h_t[u][:, i, c * P:(c + 1) * P], wd[u][:, i * HC + c, :],
                                                    start=c == 0, stop=c == HC - 1)
                    last.then_inc(y_made.sem, 1)

                pipeline(pe, npair, (0, turn), (3, down), (1, gate_up))

            @block.scalar
            def _(act):
                for st in (gated, copied):
                    act.sem_inc(st.sem, 2 * st.n)

                def copy_x(q, u):
                    act.wait_ge(turned.sem, turned.at(q, "turned"))
                    act.wait_ge(gu_made.sem, gu_made.at(q - 2, "gumade"))
                    nc.scalar.copy(xt[u][:, :, :, :].rearrange("p c i n -> p (c i n)"), turned_ps[u][:, :]).then_inc(copied.sem, 1)

                def silu(q, u):
                    act.wait_ge(gu_made.sem, gu_made.at(q, "gumade"))
                    act.wait_ge(hidden.sem, hidden.at(q - 2, "hidden"))
                    nc.scalar.activation(gate[u][:, :, :], gu_ps[u][0:HP, :].rearrange("p (i f) -> p i f", i=2)[:, :, 0:HC * P],
                                         m.act).then_inc(gated.sem, 1)
                pipeline(act, npair, (0, copy_x), (1, silu))

            @block.vector
            def _(dve):
                for st in (hidden, y_copied):
                    dve.sem_inc(st.sem, 2 * st.n)

                def hide(q, u):
                    dve.wait_ge(gated.sem, gated.at(q, "gated"))
                    dve.wait_ge(y_made.sem, y_made.at(q - 2, "ymade"))
                    nc.vector.tensor_tensor(h_t[u][:, :, :], gate[u][:, :, :],
                                            gu_ps[u][0:HP, :].rearrange("p (i f) -> p i f", i=2)[:, :, HC * P:], ALU.mult).then_inc(hidden.sem, 1)

                def copy_y(q, u):
                    dve.wait_ge(y_made.sem, y_made.at(q, "ymade"))
                    reuse(dve, stored, q, u)
                    nc.vector.tensor_copy(y[u][:, :, :].rearrange("p i d -> p (i d)"), y_ps[u][:, :]).then_inc(y_copied.sem, 1)
                pipeline(dve, npair, (3, copy_y), (1, hide), peel=2)


def wide_experts(nc, k, m, d, r):
    HC = m.hidden // P
    with ExitStack() as ctx:
        s = Scope(k, ctx, m.name + "e")
        xb, xt = s.pair("xb", [P, D]), s.pair("xt", [P, DC, P])
        w1 = s.pair("w1e", [P, DC, m.hidden])
        h_t, y = s.pair("ht", [P, HC, P]), s.pair("y", [P, D])
        turned_ps, y_ps = [s.bank("turned0"), s.bank("turned1")], [s.bank("y0"), s.bank("y1")]
        h_ps = [[s.bank(f"h{u}{half}") for half in range(2)] for u in range(2)]
        x_in, stored = s.sems("xin"), s.sems("stored")
        turned, copied, w1_copied = s.steps("turned"), s.steps("copied"), s.steps("w1copied")
        made, acted = s.steps("made", "0", "1"), s.steps("acted", "0", "1")
        y_made, y_added = s.steps("ymade"), s.steps("yadded")

        def nth(t, u):
            return (t - u) * 8 + 32

        def owner(eng, t):
            return eng.value_load(r.owner[0:1, bass.ts(t, 1)], min_val=0, max_val=m.e - 1)

        with nc.Block() as block:
            @block.sync
            def _(sp):
                for u in range(2):
                    for sem in (x_in[u], stored[u]):
                        sp.sem_inc(sem, 16)

                def load(t, u):
                    sp.wait_ge(turned.sem, turned.at(t - 2, "turned"))
                    sp.dma_start(xb[u][:, :], r.xbuf[bass.ts(t, P), :]).then_inc(x_in[u], 16)

                def store(t, u):
                    sp.wait_ge(y_added.sem, y_added.at(t, "yadded"))
                    sp.dma_start(r.ybuf[bass.ts(t, P), :], y[u][:, :]).then_inc(stored[u], 16)
                pipeline(sp, m.ntiles, (0, load), (3, store))
                for u in range(2):
                    sp.wait_ge(stored[u], 16 * (m.ntiles // 2 + 1))

            @block.tensor
            def _(pe):
                for st in (turned, made, y_made):
                    pe.sem_inc(st.sem, 2 * st.n)
                pe.wait_ge(r.ahead.weights_in, 16 * r.ahead.weights_n)
                pe.wait_ge(r.w_in, 16 * r.nw)

                def turn(t, u):
                    pe.wait_ge(x_in[u], nth(t, u))
                    pe.wait_ge(copied.sem, copied.at(t - 2, "copied"))
                    for c in range(DC):
                        last = nc.tensor.transpose(turned_ps[u][:, c * P:(c + 1) * P], xb[u][:, c * P:(c + 1) * P], k.ident[:, :])
                    last.then_inc(turned.sem, 1)

                def up(t, u):
                    pe.wait_ge(copied.sem, copied.at(t, "copied"))
                    pe.wait_ge(w1_copied.sem, w1_copied.at(t, "w1copied"))
                    for half in range(2):
                        pe.wait_ge(acted.sem, acted.at(t - 2, f"{half}"))
                        for i in range(4):
                            f0 = (4 * half + i) * P
                            for c in range(DC):
                                last = nc.tensor.matmul(h_ps[u][half][:, i * P:(i + 1) * P], w1[u][:, c, f0:f0 + P], xt[u][:, c, :],
                                                        start=c == 0, stop=c == DC - 1)
                        last.then_inc(made.sem, 1)

                def down(t, u):
                    e = owner(pe, t)
                    pe.wait_ge(y_added.sem, y_added.at(t - 2, "yadded"))
                    for c in range(HC):
                        if c % 4 == 0:
                            pe.wait_ge(acted.sem, acted.at(t, f"{c // 4}"))
                        last = nc.tensor.matmul(y_ps[u][:, 0:D], h_t[u][:, c, :], r.w2[:, bass.ts(e, 1), c, :].rearrange("p o f -> p (o f)"),
                                                start=c == 0, stop=c == HC - 1)
                    last.then_inc(y_made.sem, 1)

                pipeline(pe, m.ntiles, (0, turn), (1, up), (2, down))

            @block.scalar
            def _(act):
                act.sem_inc(acted.sem, 2 * acted.n)
                act.wait_ge(r.ahead.weights_in, 16 * r.ahead.weights_n)

                def activate(t, u):
                    e = owner(act, t)
                    act.wait_ge(y_made.sem, y_made.at(t - 2, "ymade"))
                    for half in range(2):
                        act.wait_ge(made.sem, made.at(t, f"{half}"))
                        for i in range(4):
                            last = nc.scalar.activation(h_t[u][:, 4 * half + i, :], h_ps[u][half][:, i * P:(i + 1) * P], m.act,
                                                        bias=r.ahead.b1[:, bass.ds(e * HC + (4 * half + i), 1)])
                        last.then_inc(acted.sem, 1)
                pipeline(act, m.ntiles, (0, activate))

            @block.vector
            def _(dve):
                for st in (copied, w1_copied, y_added):
                    dve.sem_inc(st.sem, 2 * st.n)
                dve.wait_ge(r.ahead.weights_in, 16 * r.ahead.weights_n)

                def copy_x(t, u):
                    dve.wait_ge(turned.sem, turned.at(t, "turned"))
                    dve.wait_ge(made.sem, made.at(t - 2, "1"))
                    nc.vector.tensor_copy(xt[u][:, :, :], turned_ps[u][:, 0:D].rearrange("p (c n) -> p c n", c=DC)).then_inc(copied.sem, 1)

                def copy_w1(t, u):
                    e = owner(dve, t)
                    dve.wait_ge(made.sem, made.at(t - 2, "1"))
                    nc.vector.tensor_copy(w1[u][:, :, :].rearrange("p c f -> p (c f)"),
                                          r.ahead.w1[:, bass.ts(e, 1), :, :].rearrange("p o c f -> p (o c f)")).then_inc(w1_copied.sem, 1)

                def add_b2(t, u):
                    e = owner(dve, t)
                    dve.wait_ge(y_made.sem, y_made.at(t, "ymade"))
                    dve.wait_ge(stored[u], (t - u) * 8 + 16)
                    nc.vector.tensor_tensor(y[u][:, :], y_ps[u][:, 0:D], row(r.ahead.b2, e), ALU.add).then_inc(y_added.sem, 1)
                pipeline(dve, m.ntiles, (0, copy_w1), (0, copy_x), (3, add_b2))


def combine(nc, k, m, r, jobs):
    K = m.top
    G = 8 // K
    with ExitStack() as ctx:
        s = Scope(k, ctx, m.name + "c")
        got = s.pair("got", [P, G, K, D])
        slot = s.pair("slot", [P, G, K], U32)
        pool_waited = s.sem("poolwaited")
        cleared, gathered = s.sem("cleared"), s.lasting_sems("gathered")
        copied = s.steps("copied")
        added = s.steps("added", *(f"{i}" for i in range(K)), "stats")
        with nc.Block() as block:
            @block.gpsimd
            def _(pool):
                def gather(g, u):
                    pool.wait_ge(copied.sem, copied.at(g, "copied"))
                    stand_alone(pool, pool_waited)
                    pool.wait_ge(added.sem, added.at(g - 2, f"{K - 1}"))
                    stand_alone(pool, pool_waited)
                    for j in range(G):
                        for i in range(K):
                            nc.gpsimd.indirect_dma_start(got[u][:, j, i, :], None, r.ybuf[:, :], bass.IndirectOffsetOnAxis(slot[u][:, j, i:i + 1], 0),
                                                         bounds_check=m.rows - 1, oob_is_err=False).then_inc(gathered[u], 16)
                pool.wait_ge(cleared, 2)
                pipeline(pool, T // G, (0, gather))

            @block.vector
            def _(dve):
                for st in (copied, added):
                    dve.sem_inc(st.sem, 2 * st.n)
                for u in range(2):
                    nc.vector.memset(got[u][:, :, :, :], 0.0).then_inc(cleared, 1)

                def index(g, u):
                    reuse(dve, gathered, g, u, G * K)
                    nc.vector.tensor_copy(slot[u][:, :, :], r.slots[:, bass.ts(g, G), :]).then_inc(copied.sem, 1)

                def add(g, u):
                    dve.wait_ge(gathered[u], (g - u) * (8 * G * K) + 16 * G * K)
                    for i in range(K):
                        if i:
                            dve.wait_ge(added.sem, added.at(g, f"{i - 1}"))
                        for j in range(G):
                            t = g * G + j
                            last = nc.vector.scalar_tensor_tensor(row(k.x, t), got[u][:, j, i, :], r.weights[:, bass.ts(t, 1), i], row(k.x, t),
                                                                  ALU.mult, ALU.add)
                        last.then_inc(added.sem, 1)
                    dve.wait_ge(added.sem, added.at(g, f"{K - 1}"))
                    for j in range(G):
                        last = nc.vector.bn_stats(row(k.stats, g * G + j), row(k.x, g * G + j))
                    last.then_inc(added.sem, 1)
                pipeline(dve, T // G, (0, index), (1, add), peel=2)

            if jobs:
                fold_contexts(nc, k, s, block, jobs)


def experts(nc, k, m, d):
    with ExitStack() as ctx:
        s = Scope(k, ctx, m.name)
        r = Shared()
        r.old_sems, r.old_runs = begin_stage(k)
        r.ahead = k.ahead
        r.xbuf, r.zeroed, r.nzero = k.slot_buffers[m.name]
        r.ybuf = nc.dram_tensor(f"{m.name}_ybuf", (m.rows, D), F32, kind="Internal").ap()
        r.iota, r.before, r.ones = k.iota, k.before, k.ones
        r.slots, r.weights = s.sb("slots", [P, T, m.top], U32), s.sb("weights", [P, T, m.top])
        r.pos, r.idxf = s.sb("pos", [P, T, m.top]), s.sb("idxf", [P, T, m.top])
        r.totals, r.w_in = s.sem("totals"), s.sem("win")
        if m is not M0:
            r.owner = r.ahead.owner
            r.w2 = s.sb("w2", [P, m.e, m.hidden // P, D])
            r.nw = m.e
        route(nc, k, m, d, r)
        if m is M0:
            narrow_experts(nc, k, m, d, r)
        else:
            wide_experts(nc, k, m, d, r)
        jobs = k.fold_jobs if m is M0 else []
        for a, _ in jobs:
            k.folded[a.name] = Folded(nc, a)
        combine(nc, k, m, r, jobs)
    k.ahead.ctx.close()



LH, LD = 8, 64
INNER = LH * LD
HID = 682
QUARTER = HID // 2
HID_CHUNKS = [(c, min(P, HID - c)) for c in range(0, HID, P)]
NORM_EPS2 = 1e-24
SHUT = -1e24
SCORE_BANKS = [(0, 2), (1, 3), (4, 6), (5, 7)]


def y_row(a, t):
    return row(a, t + (t // TB + 1))


def y_shift(sp, h, y, t, sem):
    half = D // 2
    here, before = t + (t // TB + 1), t + t // TB
    sp.dma_start(h[:, 0:half], y[:, bass.ts(here, 1), 0:half].rearrange("p o d -> p (o d)")).then_inc(sem, 16)
    sp.dma_start(h[1:P, half:D], y[0:P - 1, bass.ts(here, 1), half:D].rearrange("p o d -> p (o d)")).then_inc(sem, 16)
    sp.dma_start(h[0:1, half:D], y[P - 1:P, bass.ts(before, 1), half:D].rearrange("p o d -> p (o d)")).then_inc(sem, 16)


def local_attention(nc, k, d, l, y_in, y_out, lo):
    with ExitStack() as ctx:
        s = Scope(k, ctx, f"la{l}")
        wqkv, wo = lo.wqkv, lo.wo
        tables = [s.sb(n, [P, TB, LD]) for n in ("cosq", "sinq", "cosk", "sink")]
        scales = s.sb("scales", [P, 4, LD])
        h, h_t = s.pair("h", [P, D]), s.pair("ht", [P, DC, P])
        squares, ss, clamped, inv_norm = s.pair("squares", [P, 2, INNER]), s.pair("ss", [P, 16]), s.pair("clamped", [P, 16]), s.pair("invnorm", [P, 16])
        cosed, sined = s.sb("cosed", [P, 2, LH, LD]), s.sb("sined", [P, 2, LH, LD])
        qk = s.pair("qk", [P, 2, INNER])
        q_t, k_t, v = s.pair("qt", [P, 4, P]), s.pair("kt", [P, 4, P]), s.pair("v", [P, INNER])
        mx, nb, total, inv = s.pair("mx", [P, LH]), s.pair("nb", [P, LH]), s.pair("total", [P, LH]), s.pair("inv", [P, LH])
        probs, probs_t = s.pair("probs", [P, LH, 2 * P]), s.pair("probst", [P, LH, 2, P])
        o, o_t = s.pair("o", [P, INNER]), s.pair("ot", [P, 4, P])
        score_ps = [s.bank(f"score{j}") for j in range(4)]
        q_ps, k_ps, v_ps, c_ps = s.bank("q"), s.bank("k"), s.bank("v"), s.bank("c")
        loaded, ready, h_in = s.sem("loaded"), s.sem("ready"), s.sems("hin")

        turned, copied = s.steps("turned"), s.steps("copied")
        projected = s.steps("projected", "q", "k", "v")
        squared = s.steps("squared", "q", "k")
        roped = s.steps("roped", "ssq", "ssk", "clamp", "qcos", "qsin0", "qsin1", "q", "kcos", "ksin0", "ksin1", "k", "knorm")
        powered = s.steps("powered")
        qk_turned, qk_copied, v_copied = s.steps("qkturned", "q", "k"), s.steps("qkcopied", "q", "k"), s.steps("vcopied")
        scored = s.steps("scored", *"0123")
        maxed = s.steps("maxed", *(f"{w}{j}" for j in range(4) for w in ("max", "bias")))
        exped = s.steps("exped", *"0123")
        p_turned, p_copied = s.steps("pturned", *"0123"), s.steps("pcopied", *"0123")
        mixed, o_scaled = s.steps("mixed"), s.steps("oscaled", "inv", "o")
        o_turned, o_copied, made, added = s.steps("oturned"), s.steps("ocopied"), s.steps("made"), s.steps("added")
        nload = 4 + 4

        with nc.Block() as block:
            @block.sync
            def _(sp):
                for i, n in enumerate(("cosq", "sinq", "cosk", "sink")):
                    sp.dma_start(tables[i][:, :, :], d[n].rearrange("(w p) e -> p w e", p=P)).then_inc(loaded, 16)
                for i, n in enumerate(("qs", "qs_turned", "ks", "ks_turned")):
                    sp.dma_start(scales[:, i, :], d[n][l].partition_broadcast(P)).then_inc(loaded, 16)
                for u in range(2):
                    sp.sem_inc(h_in[u], 16)

                def load(t, u):
                    sp.wait_ge(turned.sem, turned.at(t - 2, "turned"))
                    y_shift(sp, h[u], y_in, t, h_in[u])
                    if isinstance(t, int) and t == 0:
                        lo.load_forward(sp, l)
                pipeline(sp, T, (0, load), peel=2)

            @block.gpsimd
            def _(pool):
                pool.sem_inc(powered.sem, 2)
                pool.wait_ge(ready, 2)

                def power(t, u):
                    pool.wait_ge(roped.sem, roped.at(t, "clamp"))
                    nc.gpsimd.tensor_tensor(inv_norm[u][:, :], clamped[u][:, :], k.minus_half[:, :], ALU.pow).then_inc(powered.sem, 1)
                pipeline(pool, T, (0, power))

            @block.vector
            def _(dve):
                for st in (roped, maxed, o_scaled, added):
                    dve.sem_inc(st.sem, 2 * st.n)
                nc.vector.memset(k_t[1][:, :, :], 0.0).then_inc(ready, 1)
                nc.vector.memset(v[1][:, :], 0.0).then_inc(ready, 1)
                dve.wait_ge(loaded, 16 * nload)
                for i in range(4):
                    nc.vector.tensor_tensor(tables[i][:, :, :], tables[i][:, :, :],
                                            scales[:, i, :].unsqueeze(1).broadcast_to([P, TB, LD]), ALU.mult).then_inc(ready, 1)
                dve.wait_ge(ready, 6)

                def table(i, t, half=None):
                    e0, e1 = (0, LD) if half is None else (half * 32, half * 32 + 32)
                    return tables[i][:, bass.ts(t % TB, 1), e0:e1].broadcast_to([P, LH, e1 - e0])

                def rope(t, u):
                    def done(name):
                        dve.wait_ge(roped.sem, roped.at(t, name))
                    for i, n in enumerate("qk"):
                        dve.wait_ge(squared.sem, squared.at(t, n))
                        nc.vector.tensor_reduce(ss[u][:, i * LH:(i + 1) * LH], squares[u][:, i, :].rearrange("p (h e) -> p h e", h=LH),
                                                AX, ALU.add).then_inc(roped.sem, 1)
                    done("ssk")
                    nc.vector.tensor_scalar(clamped[u][:, :], ss[u][:, :], NORM_EPS2, None, ALU.max).then_inc(roped.sem, 1)
                    for i, (n, ps) in enumerate((("q", q_ps), ("k", k_ps))):
                        src = ps[:, :].rearrange("p (h e) -> p h e", h=LH)
                        nc.vector.tensor_tensor(cosed[:, i, :, :], src, table(2 * i, t), ALU.mult).then_inc(roped.sem, 1)
                        for half in range(2):
                            nc.vector.tensor_tensor(sined[:, i, :, half * 32:half * 32 + 32], src[:, :, 32 - half * 32:64 - half * 32],
                                                    table(2 * i + 1, t, half), ALU.mult).then_inc(roped.sem, 1)
                        done(f"{n}sin1")
                        if i == 0:
                            dve.wait_ge(qk_turned.sem, qk_turned.at(t - 2, "k"))
                        nc.vector.tensor_tensor(qk[u][:, i, :].rearrange("p (h e) -> p h e", h=LH), cosed[:, i, :, :], sined[:, i, :, :],
                                                ALU.add).then_inc(roped.sem, 1)
                    done("k")
                    dve.wait_ge(powered.sem, powered.at(t, "powered"))
                    keys = qk[u][:, 1, :].rearrange("p (h e) -> p h e", h=LH)
                    nc.vector.tensor_tensor(keys, keys, inv_norm[u][:, LH:2 * LH].unsqueeze(2).broadcast_to([P, LH, LD]),
                                            ALU.mult).then_inc(roped.sem, 1)

                def maxima(t, u):
                    dve.wait_ge(exped.sem, exped.at(t - 2, "3"))
                    for j, (h0, h1) in enumerate(SCORE_BANKS):
                        dve.wait_ge(scored.sem, scored.at(t, f"{j}"))
                        nc.vector.tensor_reduce(mx[u][:, h0:h1 + 1:2], score_ps[j][:, :].rearrange("p (h e) -> p h e", h=2), AX, ALU.max).then_inc(maxed.sem, 1)
                        dve.wait_ge(maxed.sem, maxed.at(t, f"max{j}"))
                        nc.vector.scalar_tensor_tensor(nb[u][:, h0:h1 + 1:2], mx[u][:, h0:h1 + 1:2], -1.0, inv_norm[u][:, h0:h1 + 1:2],
                                                       ALU.mult, ALU.mult).then_inc(maxed.sem, 1)

                def scale_o(t, u):
                    dve.wait_ge(exped.sem, exped.at(t, "3"))
                    nc.vector.reciprocal(inv[u][:, :], total[u][:, :]).then_inc(o_scaled.sem, 1)
                    dve.wait_ge(o_scaled.sem, o_scaled.at(t, "inv"))
                    dve.wait_ge(mixed.sem, mixed.at(t, "mixed"))
                    dve.wait_ge(o_turned.sem, o_turned.at(t - 2, "oturned"))
                    nc.vector.tensor_tensor(o[u][:, :].rearrange("p (h e) -> p h e", h=LH), c_ps[:, :].rearrange("p (h e) -> p h e", h=LH),
                                            inv[u][:, :].unsqueeze(2).broadcast_to([P, LH, LD]), ALU.mult).then_inc(o_scaled.sem, 1)

                def add(t, u):
                    dve.wait_ge(made.sem, made.at(t, "made"))
                    nc.vector.tensor_tensor(y_row(y_out, t), y_row(y_in, t), v_ps[:, 0:D], ALU.add).then_inc(added.sem, 1)

                pipeline(dve, T, (2, add), (1, maxima), (0, rope), (1, scale_o))

            @block.scalar
            def _(act):
                for st in (copied, squared, qk_copied, v_copied, exped, p_copied, o_copied):
                    act.sem_inc(st.sem, 2 * st.n)

                def copy_h(t, u):
                    act.wait_ge(turned.sem, turned.at(t, "turned"))
                    act.wait_ge(projected.sem, projected.at(t - 2, "v"))
                    nc.scalar.copy(h_t[u][:, :, :], c_ps[:, 0:D].rearrange("p (c n) -> p c n", c=DC)).then_inc(copied.sem, 1)

                def copy_o(t, u):
                    act.wait_ge(o_turned.sem, o_turned.at(t, "oturned"))
                    act.wait_ge(made.sem, made.at(t - 2, "made"))
                    nc.scalar.copy(o_t[u][:, :, :], v_ps[:, :].rearrange("p (c n) -> p c n", c=4)).then_inc(o_copied.sem, 1)

                def copy_qk(t, u):
                    act.wait_ge(qk_turned.sem, qk_turned.at(t, "q"))
                    act.wait_ge(scored.sem, scored.at(t - 1, "3"))
                    nc.scalar.copy(q_t[u][:, :, :], q_ps[:, :].rearrange("p (c n) -> p c n", c=4)).then_inc(qk_copied.sem, 1)
                    act.wait_ge(qk_turned.sem, qk_turned.at(t, "k"))
                    nc.scalar.copy(k_t[u][:, :, :], k_ps[:, :].rearrange("p (c n) -> p c n", c=4)).then_inc(qk_copied.sem, 1)

                def exp(t, u):
                    act.wait_ge(p_turned.sem, p_turned.at(t - 2, "3"))
                    act.wait_ge(o_scaled.sem, o_scaled.at(t - 2, "inv"))
                    for j, pair in enumerate(SCORE_BANKS):
                        act.wait_ge(maxed.sem, maxed.at(t, f"bias{j}"))
                        for i, hh in enumerate(pair):
                            last = nc.scalar.activation(probs[u][:, hh, :], score_ps[j][:, i * 2 * P:(i + 1) * 2 * P], ACT.Exp,
                                                        bias=nb[u][:, hh:hh + 1], scale=inv_norm[u][:, hh:hh + 1],
                                                        accum_out=total[u][:, hh:hh + 1])
                        last.then_inc(exped.sem, 1)

                def square(t, u):
                    for i, (n, ps) in enumerate((("q", q_ps), ("k", k_ps))):
                        act.wait_ge(projected.sem, projected.at(t, n))
                        act.wait_ge(roped.sem, roped.at(t - 2, "ssk"))
                        nc.scalar.activation(squares[u][:, i, :], ps[:, :], ACT.Square).then_inc(squared.sem, 1)

                def copy_p(t, u):
                    act.wait_ge(mixed.sem, mixed.at(t - 2, "mixed"))
                    for j, (h0, h1) in enumerate(SCORE_BANKS):
                        act.wait_ge(p_turned.sem, p_turned.at(t, f"{j}"))
                        nc.scalar.copy(probs_t[u][:, h0:h1 + 1:2, :, :].rearrange("p h w n -> p h (w n)"),
                                       score_ps[j][:, :].rearrange("p (h n) -> p h n", h=2)).then_inc(p_copied.sem, 1)

                def copy_v(t, u):
                    act.wait_ge(projected.sem, projected.at(t, "v"))
                    act.wait_ge(mixed.sem, mixed.at(t - 1, "mixed"))
                    nc.scalar.copy(v[u][:, :], v_ps[:, :]).then_inc(v_copied.sem, 1)

                pipeline(act, T, (1, copy_qk), (2, copy_o), (0, copy_h), (1, exp), (0, square), (1, copy_p), (0, copy_v))

            @block.tensor
            def _(pe):
                for st in (turned, projected, qk_turned, scored, p_turned, mixed, o_turned, made):
                    pe.sem_inc(st.sem, 2 * st.n)
                pe.wait_ge(lo.attention_in[l], 32)
                pe.wait_ge(ready, 2)

                def turn(t, u):
                    pe.wait_ge(h_in[u], (t - u) * 24 + 64)
                    pe.wait_ge(o_scaled.sem, o_scaled.at(t - 2, "o"))
                    for c in range(DC):
                        last = nc.tensor.transpose(c_ps[:, c * P:(c + 1) * P], h[u][:, c * P:(c + 1) * P], k.ident[:, :])
                    last.then_inc(turned.sem, 1)

                def project(t, u):
                    pe.wait_ge(copied.sem, copied.at(t, "copied"))
                    for i, ps in enumerate((q_ps, k_ps, v_ps)):
                        if i < 2:
                            pe.wait_ge(qk_copied.sem, qk_copied.at(t - 1, "qk"[i]))
                        else:
                            pe.wait_ge(added.sem, added.at(t - 2, "added"))
                        for c in range(DC):
                            last = nc.tensor.matmul(ps[:, :], h_t[u][:, c, :], wqkv[:, c, i * INNER:(i + 1) * INNER],
                                                    start=c == 0, stop=c == DC - 1)
                        last.then_inc(projected.sem, 1)

                def turn_qk(t, u):
                    pe.wait_ge(roped.sem, roped.at(t, "k"))
                    for i, ps in enumerate((q_ps, k_ps)):
                        if i == 1:
                            pe.wait_ge(roped.sem, roped.at(t, "knorm"))
                        for c in range(4):
                            last = nc.tensor.transpose(ps[:, c * P:(c + 1) * P], qk[u][:, i, c * P:(c + 1) * P], k.ident[:, :])
                        last.then_inc(qk_turned.sem, 1)

                def score(t, u):
                    pe.wait_ge(qk_copied.sem, qk_copied.at(t, "k"))
                    first = 1 - (t % TB + (TB - 1)) // TB
                    for j in range(4):
                        pe.wait_ge(p_copied.sem, p_copied.at(t - 1, f"{j}"))
                        nc.tensor.matmul(score_ps[j][:, :], lo.ident16[:, :], lo.shut[:, bass.ts(first, 1), :].rearrange("p o n -> p (o n)"),
                                         start=True, stop=False, skip_group_check=True)
                    for j0 in (0, 2):
                        for i in range(2):
                            for j in (j0, j0 + 1):
                                hh = SCORE_BANKS[j][i]
                                p0 = LD * (hh % 2)
                                for w, kt in enumerate((k_t[1 - u], k_t[u])):
                                    c0 = i * 2 * P + w * P
                                    last = nc.tensor.matmul(score_ps[j][:, c0:c0 + P], q_t[u][p0:p0 + LD, hh // 2, :], kt[p0:p0 + LD, hh // 2, :],
                                                            start=False, stop=True, skip_group_check=True)
                                if i == 1:
                                    last.then_inc(scored.sem, 1)

                def turn_p(t, u):
                    for j, pair in enumerate(SCORE_BANKS):
                        pe.wait_ge(exped.sem, exped.at(t, f"{j}"))
                        for i, hh in enumerate(pair):
                            for w in range(2):
                                c0 = i * 2 * P + w * P
                                last = nc.tensor.transpose(score_ps[j][:, c0:c0 + P], probs[u][:, hh, w * P:(w + 1) * P], k.ident[:, :])
                        last.then_inc(p_turned.sem, 1)

                def mix(t, u):
                    pe.wait_ge(v_copied.sem, v_copied.at(t, "vcopied"))
                    pe.wait_ge(copied.sem, copied.at(t + 1, "copied") if not isinstance(t, int) or t + 1 < T else copied.at(t, "copied"))
                    for j, pair in enumerate(SCORE_BANKS):
                        pe.wait_ge(p_copied.sem, p_copied.at(t, f"{j}"))
                        for hh in pair:
                            for w, vw in enumerate((v[1 - u], v[u])):
                                last = nc.tensor.matmul(c_ps[:, hh * LD:(hh + 1) * LD], probs_t[u][:, hh, w, :], vw[:, hh * LD:(hh + 1) * LD],
                                                        start=w == 0, stop=w == 1)
                    last.then_inc(mixed.sem, 1)

                def turn_o(t, u):
                    pe.wait_ge(o_scaled.sem, o_scaled.at(t, "o"))
                    pe.wait_ge(v_copied.sem, v_copied.at(t + 1, "vcopied") if not isinstance(t, int) or t + 1 < T else v_copied.at(t, "vcopied"))
                    for c in range(4):
                        last = nc.tensor.transpose(v_ps[:, c * P:(c + 1) * P], o[u][:, c * P:(c + 1) * P], k.ident[:, :])
                    last.then_inc(o_turned.sem, 1)

                def output(t, u):
                    pe.wait_ge(o_copied.sem, o_copied.at(t, "ocopied"))
                    for c in range(4):
                        last = nc.tensor.matmul(v_ps[:, 0:D], o_t[u][:, c, :], wo[:, c, :], start=c == 0, stop=c == 3)
                    last.then_inc(made.sem, 1)

                pipeline(pe, T, (1, turn_qk), (2, turn_o), (0, turn), (2, output), (1, score), (0, project), (1, turn_p), (1, mix))


def local_feed_forward(nc, k, d, l, y_in, y_out, lo):
    with ExitStack() as ctx:
        s = Scope(k, ctx, f"lf{l}")
        nch = len(HID_CHUNKS)
        nb = nch // 2
        w1g = s.sb("w1g", [P, DC, 2 * HID])
        w1, w2, gain, offset, b1 = lo.w1, lo.w2, lo.gain, lo.offset, lo.b1
        bias = s.sb("bias", [P, 2 * nch])
        rest, rest2 = s.sb("rest", [1, D]), s.sb("rest2", [1, D])
        b2 = [s.sb(f"b2part{i}", [1, D], BF16) for i in range(3)]
        ones = s.sb("ones", [1, P], BF16)
        h, z, z_t = s.pair("h", [P, D]), s.pair("z", [P, D]), s.pair("zt", [P, DC, P])
        st6, mv, ve, rstd = s.pair("st", [P, 6]), s.pair("mv", [P, 2]), s.pair("ve", [P, 1]), s.pair("rstd", [P, 1])
        gelu, hid_t = s.pair("gelu", [P, nch, P]), s.pair("hidt", [P, nch, P])
        banks = [[s.bank(f"m{u}{i}") for i in range(nb)] for u in range(2)]
        t_ps, y_ps = s.bank("t"), s.bank("y")
        folded, biased, split, h_in, dve_waited = s.sem("folded"), s.sem("biased"), s.sem("split"), s.sems("hin"), s.sem("dvewaited")

        normed = s.steps("normed", "stats", "aggr", "eps", "z")
        powered, turned, copied = s.steps("powered"), s.steps("turned"), s.steps("copied")
        made, gated, hidden = (s.steps(n, *"012") for n in ("made", "gated", "hidden"))
        y_made, added = s.steps("ymade"), s.steps("added", *(["y"] if l == 0 else ["y", "x", "stats"]))

        def column(c, half):
            c0, n = HID_CHUNKS[c]
            return half * HID + c0, n

        with nc.Block() as block:
            @block.sync
            def _(sp):
                for u in range(2):
                    sp.sem_inc(h_in[u], 16)

                def load(t, u):
                    sp.wait_ge(normed.sem, normed.at(t - 2, "z"))
                    y_shift(sp, h[u], y_in, t, h_in[u])
                    if isinstance(t, int) and t == 0 and l == 0:
                        lo.load_attention(sp, 1)
                pipeline(sp, T, (0, load), peel=2)

            @block.gpsimd
            def _(pool):
                pool.sem_inc(powered.sem, 2)

                def power(t, u):
                    pool.wait_ge(normed.sem, normed.at(t, "eps"))
                    nc.gpsimd.tensor_tensor(rstd[u][:, :], ve[u][:, :], k.minus_half[:, 0:1], ALU.pow).then_inc(powered.sem, 1)
                pipeline(pool, T, (0, power))

            @block.vector
            def _(dve):
                for st in (normed, hidden, added):
                    dve.sem_inc(st.sem, 2 * st.n)
                dve.wait_ge(lo.forward_in[l], 16 * lo.forward_n)
                nc.vector.memset(bias[:, :], 0.0).then_inc(folded, 1)
                nc.vector.memset(ones[:, :], 1.0).then_inc(folded, 1)
                for c in range(DC):
                    nc.vector.tensor_scalar(w1g[:, c, :], w1[:, c, :], gain[:, c:c + 1], None, ALU.mult).then_inc(folded, 1)
                dve.wait_ge(folded, 2)
                dve.wait_ge(biased, 1)
                for half in range(2):
                    c0, n = nch * half, HID_CHUNKS[-1][1]
                    nc.vector.tensor_tensor(bias[:, c0:c0 + nch - 1], b1[:, c0:c0 + nch - 1], y_ps[:, c0:c0 + nch - 1], ALU.add).then_inc(folded, 1)
                    nc.vector.tensor_tensor(bias[0:n, c0 + nch - 1:c0 + nch], b1[0:n, c0 + nch - 1:c0 + nch],
                                            y_ps[0:n, c0 + nch - 1:c0 + nch], ALU.add).then_inc(folded, 1)
                nc.vector.tensor_copy(b2[0][:, :], lo.b2[:, :]).then_inc(split, 1)
                dve.wait_ge(split, 1)
                nc.vector.tensor_tensor(rest[:, :], lo.b2[:, :], b2[0][:, :], ALU.subtract).then_inc(split, 1)
                dve.wait_ge(split, 2)
                nc.vector.tensor_copy(b2[1][:, :], rest[:, :]).then_inc(split, 1)
                dve.wait_ge(split, 3)
                nc.vector.tensor_tensor(rest2[:, :], rest[:, :], b2[1][:, :], ALU.subtract).then_inc(split, 1)
                dve.wait_ge(split, 4)
                nc.vector.tensor_copy(b2[2][:, :], rest2[:, :]).then_inc(split, 1)
                dve.wait_ge(folded, 8)

                def stats(t, u):
                    def done(name):
                        dve.wait_ge(normed.sem, normed.at(t, name))
                    dve.wait_ge(h_in[u], (t - u) * 24 + 64)
                    nc.vector.bn_stats(st6[u][:, :], h[u][:, :]).then_inc(normed.sem, 1)
                    done("stats")
                    stand_alone(dve, dve_waited)
                    nc.vector.bn_aggr(mv[u][:, :], st6[u][:, :]).then_inc(normed.sem, 1)
                    done("aggr")
                    nc.vector.tensor_scalar(ve[u][:, :], mv[u][:, 1:2], LN_EPS, None, ALU.add).then_inc(normed.sem, 1)

                def norm(t, u):
                    dve.wait_ge(powered.sem, powered.at(t, "powered"))
                    dve.wait_ge(turned.sem, turned.at(t - 2, "turned"))
                    nc.vector.tensor_scalar(z[u][:, :], h[u][:, :], mv[u][:, 0:1], rstd[u][:, 0:1], ALU.subtract, ALU.mult).then_inc(normed.sem, 1)

                def hide(t, u):
                    dve.wait_ge(y_made.sem, y_made.at(t - 2, "ymade"))
                    for i in range(nb):
                        dve.wait_ge(gated.sem, gated.at(t, f"{i}"))
                        for x in range(2):
                            c = 2 * i + x
                            n = HID_CHUNKS[c][1]
                            last = nc.vector.scalar_tensor_tensor(hid_t[u][0:n, c, :], banks[u][i][0:n, (2 + x) * P:(3 + x) * P], bias[0:n, c:c + 1],
                                                                  gelu[u][0:n, c, :], ALU.add, ALU.mult)
                        last.then_inc(hidden.sem, 1)

                def add(t, u):
                    dve.wait_ge(y_made.sem, y_made.at(t, "ymade"))
                    nc.vector.tensor_tensor(y_row(y_out, t), y_row(y_in, t), y_ps[:, 0:D], ALU.add).then_inc(added.sem, 1)
                    if l == 1:
                        dve.wait_ge(added.sem, added.at(t, "y"))
                        nc.vector.tensor_tensor(row(k.x, t), row(k.x, t), y_row(y_out, t), ALU.add).then_inc(added.sem, 1)
                        dve.wait_ge(added.sem, added.at(t, "x"))
                        nc.vector.bn_stats(row(k.stats, t), row(k.x, t)).then_inc(added.sem, 1)

                pipeline(dve, T, (0, stats), (0, norm), (4, add), (2, hide))

            @block.scalar
            def _(act):
                for st in (copied, gated):
                    act.sem_inc(st.sem, 2 * st.n)
                act.wait_ge(folded, 8)

                def copy_z(t, u):
                    act.wait_ge(turned.sem, turned.at(t, "turned"))
                    act.wait_ge(made.sem, made.at(t - 2, "2"))
                    nc.scalar.copy(z_t[u][:, :, :], t_ps[:, 0:D].rearrange("p (c n) -> p c n", c=DC)).then_inc(copied.sem, 1)

                def gate(t, u):
                    act.wait_ge(hidden.sem, hidden.at(t - 2, "2"))
                    for i in range(nb):
                        act.wait_ge(made.sem, made.at(t, f"{i}"))
                        for x in range(2):
                            c = 2 * i + x
                            n = HID_CHUNKS[c][1]
                            last = nc.scalar.activation(gelu[u][0:n, c, :], banks[u][i][0:n, x * P:(x + 1) * P], ACT.Gelu,
                                                        bias=bias[0:n, nch + c:nch + c + 1])
                        last.then_inc(gated.sem, 1)
                pipeline(act, T, (0, copy_z), (1, gate))

            @block.tensor
            def _(pe):
                for st in (turned, made, y_made):
                    pe.sem_inc(st.sem, 2 * st.n)
                pe.wait_ge(lo.forward_in[l], 16 * lo.forward_n)
                for half in range(2):
                    for c in range(nch):
                        c0, n = column(c, half)
                        for dc in range(DC):
                            last = nc.tensor.matmul(y_ps[0:n, half * nch + c:half * nch + c + 1], w1[:, dc, c0:c0 + n], offset[:, dc:dc + 1],
                                                    start=dc == 0, stop=dc == DC - 1)
                last.then_inc(biased, 1)
                pe.wait_ge(folded, 8)
                pe.wait_ge(split, 5)

                def turn(t, u):
                    pe.wait_ge(normed.sem, normed.at(t, "z"))
                    pe.wait_ge(copied.sem, copied.at(t - 1, "copied"))
                    for c in range(DC):
                        last = nc.tensor.transpose(t_ps[:, c * P:(c + 1) * P], z[u][:, c * P:(c + 1) * P], k.ident[:, :])
                    last.then_inc(turned.sem, 1)

                def up(t, u):
                    pe.wait_ge(copied.sem, copied.at(t, "copied"))
                    for i in range(nb):
                        pe.wait_ge(hidden.sem, hidden.at(t - 2, f"{i}"))
                        for q in range(4):
                            c0, n = column(2 * i + q % 2, 1 - q // 2)
                            for dc in range(DC):
                                last = nc.tensor.matmul(banks[u][i][0:n, q * P:(q + 1) * P], w1g[:, dc, c0:c0 + n], z_t[u][:, dc, :],
                                                        start=dc == 0, stop=dc == DC - 1)
                        last.then_inc(made.sem, 1)

                def down(t, u):
                    pe.wait_ge(added.sem, added.at(t - 1, "y"))
                    for i in range(3):
                        nc.tensor.matmul(y_ps[:, 0:D], ones[:, :], b2[i][:, :], start=i == 0, stop=False)
                    for c, (c0, n) in enumerate(HID_CHUNKS):
                        if c % 2 == 0:
                            pe.wait_ge(hidden.sem, hidden.at(t, f"{c // 2}"))
                        last = nc.tensor.matmul(y_ps[:, 0:D], hid_t[u][0:n, c, :], w2[0:n, c, :], start=False, stop=c == nch - 1)
                    last.then_inc(y_made.sem, 1)

                pipeline(pe, T, (0, turn), (3, down), (1, up))


def local_layers(nc, k, d):
    norm_scales(nc, k)
    with ExitStack() as ctx:
        s = Scope(k, ctx, "lo")
        lo = Shared()
        y = s.pair("y", [P, T + B, D])
        lo.shut, lo.ident16 = s.sb("shut", [P, 2, 4 * P], BF16), s.sb("ident16", [P, P], BF16)
        loaded, ready = s.sem("loaded"), s.sem("ready")
        shut_f = s.sb("shutf", [P, 2, 4 * P])
        lo.wqkv, lo.wo = s.sb("wqkv", [P, DC, 3 * INNER]), s.sb("wo", [P, INNER // P, D])
        nch = len(HID_CHUNKS)
        lo.w1, lo.w2 = s.sb("w1", [P, DC, 2 * HID]), s.sb("w2", [P, nch, D])
        lo.gain, lo.offset, lo.b1, lo.b2 = s.sb("gain", [P, DC]), s.sb("offset", [P, DC]), s.sb("b1", [P, 2 * nch]), s.sb("b2", [1, D])
        lo.attention_in, lo.forward_in, lo.forward_n = s.sems("attentionin"), s.sems("forwardin"), 7

        def load_attention(sp, l):
            sp.dma_start(lo.wqkv[:, :, :], d["wqkv"][l].rearrange("(c p) n -> p c n", p=P)).then_inc(lo.attention_in[l], 16)
            sp.dma_start(lo.wo[:, :, :], d["wo"][l].rearrange("(c p) n -> p c n", p=P)).then_inc(lo.attention_in[l], 16)

        def load_forward(sp, l):
            sem, whole = lo.forward_in[l], nch - 1
            sp.dma_start(lo.w1[:, :, :], d["w1"][l].rearrange("(c p) n -> p c n", p=P)).then_inc(sem, 16)
            sp.dma_start(lo.w2[:, 0:whole, :], d["w2"][l, 0:whole * P].rearrange("(c p) n -> p c n", p=P)).then_inc(sem, 16)
            sp.dma_start(lo.w2[0:HID - whole * P, whole, :], d["w2"][l, whole * P:HID]).then_inc(sem, 16)
            sp.dma_start(lo.gain[:, :], d["gain"][l]).then_inc(sem, 16)
            sp.dma_start(lo.offset[:, :], d["offset"][l]).then_inc(sem, 16)
            sp.dma_start(lo.b1[:, :], d["b1"][l]).then_inc(sem, 16)
            sp.dma_start(lo.b2[:, :], d["b2"][l:l + 1]).then_inc(sem, 16)
        lo.load_attention, lo.load_forward = load_attention, load_forward
        with nc.Block() as block:
            @block.sync
            def _(sp):
                sp.dma_start(shut_f[:, :, :], d["shut"]).then_inc(loaded, 16)
                load_attention(sp, 0)

            @block.vector
            def _(dve):
                for u in range(2):
                    for b in range(B):
                        nc.vector.memset(y[u][:, b * (TB + 1), :], 0.0).then_inc(ready, 1)
                nc.vector.tensor_copy(lo.ident16[:, :], k.ident[:, :]).then_inc(ready, 1)
                dve.wait_ge(loaded, 16)
                nc.vector.tensor_copy(lo.shut[:, :, :], shut_f[:, :, :]).then_inc(ready, 1)
                for t in range(T):
                    nc.vector.tensor_scalar(y[0][:, t + t // TB + 1, :], k.x[:, t, :], k.mean[:, t:t + 1], k.rstd[:, t:t + 1],
                                            ALU.subtract, ALU.mult).then_inc(ready, 1)
                dve.wait_ge(ready, 6 + T)
        for l in range(2):
            local_attention(nc, k, d, l, y[0], y[1], lo)
            local_feed_forward(nc, k, d, l, y[1], y[0], lo)


def local_tables():
    f = np.float32
    half = np.arange(0, LD, 2, dtype=f)
    inv_freq = (f(1.0) / f(10000.0) ** (half / f(LD))).astype(f)
    t = np.arange(S, dtype=f)
    freqs = (t[:, None] * inv_freq[None, :]).astype(f)
    freqs = np.concatenate([freqs, freqs], axis=-1)
    base = ((half + f(0.4 * LD)) / f(1.4 * LD)).astype(f)
    power = ((t - f(S // 2)) / f(P // 2)).astype(f)
    scale = (base[None, :] ** power[:, None]).astype(f)
    scale = np.concatenate([scale, scale], axis=-1)
    sign = np.where(np.arange(LD) < LD // 2, f(-1), f(1))[None, :]
    cos, sin = np.cos(freqs), np.sin(freqs)
    i, j = np.arange(P)[:, None], np.arange(P)[None, :]
    before, here = np.where(i > j, SHUT, 0.0), np.where(i < j, SHUT, 0.0)
    usual, first = np.concatenate([before, here], axis=1), np.concatenate([np.full((P, P), SHUT), here], axis=1)
    shut = np.stack([np.tile(usual, 2), np.tile(first, 2)], axis=1)
    return {"cosq": f(8) * cos * scale, "sinq": f(8) * sin * scale * sign, "cosk": cos / scale, "sink": sin / scale * sign,
            "shut": shut.astype(f)}



def program(nc, d, out, stages=None):
    with ExitStack() as ctx:
        k = Shared()
        k.nc, k.ctx, k.stage = nc, ctx, 0
        k.stage_sems, k.stage_sem_numbers = ExitStack(), []
        s = Scope(k, ctx, "all")
        k.x = s.sb("x", [P, T, D])
        k.stats = s.sb("stats", [P, T, 6])
        k.mv, k.mean, k.var = s.sb("mv", [P, T, 2]), s.sb("mean", [P, T]), s.sb("var", [P, T])
        k.std, k.rstd = s.sb("std", [P, T]), s.sb("rstd", [P, T])
        k.ident = s.sb("ident", [P, P])
        k.ones3 = s.sb("ones3", [3, P], BF16)
        k.ctx_t = s.sb("ctxt", [P, DC, B * J])
        k.folded = {}
        k.iota, k.before, k.ones = s.sb("iota", [P, 64]), s.sb("before", [P, P]), s.sb("ones", [P, P])
        k.minus_half = s.sb("minushalf", [P, 16])
        k.zeros = s.sb("zeros", [P, 1024])
        loaded, ready = s.sem("loaded"), s.sem("ready")
        stored, = s.lasting_sems("stored", 1)
        k.slot_buffers, zeroed = {}, s.lasting_sems("zeroed", 3)
        for m, sem in zip((M0, M2, M3), zeroed):
            if stages is None or m.name in stages:
                k.slot_buffers[m.name] = (nc.dram_tensor(f"{m.name}_xbuf", (m.rows, D), F32, kind="Internal").ap(),
                                          sem, m.rows // 512)
        with nc.Block() as block:
            @block.sync
            def _(sp):
                sp.dma_start(k.x[:, :, :], d["x"].rearrange("(t p) d -> p t d", p=P)).then_inc(loaded, 16)
                sp.dma_start(k.ident[:, :], d["ident"]).then_inc(loaded, 16)
                sp.dma_start(k.ctx_t[:, :, :], d["ctx_t"].rearrange("(c p) n -> p c n", p=P)).then_inc(loaded, 16)
                sp.dma_start(k.iota[:, :], d["iota"]).then_inc(loaded, 16)
                sp.dma_start(k.before[:, :], d["before"]).then_inc(loaded, 16)
                sp.wait_ge(loaded, 80)

            @block.vector
            def _(dve):
                nc.vector.memset(k.zeros[:, :], 0.0)
                nc.vector.memset(k.ones3[:, :], 1.0)
                nc.vector.memset(k.ones[:, :], 1.0)
                nc.vector.memset(k.minus_half[:, :], -0.5)
                dve.wait_ge(loaded, 80)
                for t in range(T):
                    nc.vector.bn_stats(k.stats[:, t, :], k.x[:, t, :]).then_inc(ready, 1)
                dve.wait_ge(ready, T)
        k.buffers_zeroed = False
        k.fold_jobs = [(a, d[a.name]) for a in ATTENTIONS[1:] if a.name in d]
        k.experts_after = {a: (m, d[m.name]) for a, m in (("a0", M0), ("a2", M2), ("a3", M3)) if m.name in d}
        for name, stage in STAGES:
            if stages is None or name in stages:
                stage(nc, k, d.get(name, d))
        with nc.Block() as block:
            @block.sync
            def _(sp):
                sp.dma_start(out.rearrange("(t p) d -> p t d", p=P), k.x[:, :, :]).then_inc(stored, 16)
                sp.wait_ge(stored, 16)


STAGES = []


def att_stage(a):
    STAGES.append((a.name, lambda nc, k, d: attention(nc, k, a, d)))


att_stage(ATTENTIONS[0])
STAGES.append(("m0", lambda nc, k, d: experts(nc, k, M0, d)))
att_stage(ATTENTIONS[1])
STAGES.append(("local", local_layers))
att_stage(ATTENTIONS[2])
STAGES.append(("m2", lambda nc, k, d: experts(nc, k, M2, d)))
att_stage(ATTENTIONS[3])
STAGES.append(("m3", lambda nc, k, d: experts(nc, k, M3, d)))



def block_diagonal(w, heads, a, b):
    out = np.zeros((heads, a, heads, b), w.dtype)
    for h in range(heads):
        out[h, :, h, :] = w[h]
    return out.reshape(heads * a, heads * b)


def by_slot(m, n):
    return m.reshape(n, m.shape[0] // n, -1).transpose(1, 0, 2)


def lay_out(i):
    a0, a1, a2, a3 = ATTENTIONS
    o = {
        "x": i["x"].reshape(B * S, D),
        "ctx_t": i["ctx_1024"].reshape(B * J, D).T,
        "ident": np.eye(P, dtype=np.float32),
        "iota": np.tile(np.arange(64, dtype=np.float32), (P, 1)),
        "before": np.triu(np.ones((P, P), np.float32), 1),
    }

    def att(a, wq, wk, wv, wo, bq, bk, bv, bo, mask=None):
        n = a.nslot
        o[a.name] = {
            "wq": by_slot(wq.T, n), "wk": wk, "wv": wv, "wo": by_slot(wo, n),
            "bq": bq.reshape(n, -1).T, "bk": bk.reshape(n, -1).T, "bv": bv.reshape(n, -1).T, "bo": bo.reshape(1, D),
        }
        if mask is not None:
            o[a.name]["mask"] = mask

    def diag(n):
        return block_diagonal(i[f"L0_xattn_{n}"], 16, 16, 64)

    att(a0, diag("Wq"), diag("Wk"), diag("Wv"), i["L0_xattn_Wo"].T, i["L0_xattn_bq"], i["L0_xattn_bk"],
        i["L0_xattn_bv"], i["L0_xattn_bo"], i["mask_BxSxS2_bk1"].reshape(B * S, J))
    for a, n, mask in ((a1, "L1", i["mask_BxS2_bk0"]), (a2, "L2", None)):
        att(a, *(i[f"{n}_xattn_{w}"] for w in ("Wq", "Wk", "Wv", "Wo", "bq", "bk", "bv", "bo")), mask)
    zero = np.zeros(1024, np.float32)
    wkv = i["L3_xattn_Wkv"]
    att(a3, i["L3_xattn_Wq"], wkv[:, :1024], wkv[:, 1024:], i["L3_xattn_Wo"], zero, zero, zero, i["L3_xattn_bo"])

    o["m0"] = {
        "wr": i["L0_ffn_router_w"].T, "sgu": i["L0_ffn_ws_gate_up"], "sd": i["L0_ffn_ws_down"],
        "gu": np.concatenate([i["L0_ffn_w_gate"], i["L0_ffn_w_up"]], axis=2).reshape(M0.e * D, -1),
        "down": i["L0_ffn_w_down"].reshape(-1, D),
    }
    for m, n in ((M2, "L2"), (M3, "L3")):
        o[m.name] = {
            "wr": i[f"{n}_ffn_Wg"], "w1": i[f"{n}_ffn_W1"], "w2": i[f"{n}_ffn_W2"],
            "b1": i[f"{n}_ffn_b1"].reshape(-1, P).T, "b2": i[f"{n}_ffn_b2"].reshape(-1),
        }
    o["m2"]["owner"] = (np.arange(M2.ntiles, dtype=np.int32) // (M2.stride // P))[None, :]
    o["m3"]["bg"] = i["L3_ffn_bg"]
    lf = {n: i[f"L1_ffn_{n}"] for n in ("wqkv", "q_scale", "k_scale", "wo", "ln_g", "ln_b", "w1", "b1", "w2", "b2")}
    o["local"] = {
        **{n: lf[n] for n in ("wqkv", "wo", "w1", "w2", "b2")},
        "b1": np.pad(lf["b1"].reshape(2, 2, HID), ((0, 0), (0, 0), (0, -HID % P))).reshape(2, -1, P).transpose(0, 2, 1),
        "qs": lf["q_scale"], "qs_turned": np.roll(lf["q_scale"], LD // 2, axis=1),
        "ks": lf["k_scale"], "ks_turned": np.roll(lf["k_scale"], LD // 2, axis=1),
        "gain": lf["ln_g"].reshape(2, DC, P).transpose(0, 2, 1), "offset": lf["ln_b"].reshape(2, DC, P).transpose(0, 2, 1),
        **local_tables(),
    }
    return o


def declare(nc, o, arrays, prefix="in"):
    d = {}
    for name, a in o.items():
        if isinstance(a, dict):
            d[name] = declare(nc, a, arrays, f"{prefix}_{name}")
        else:
            a = np.ascontiguousarray(a)
            arrays[f"{prefix}_{name}"] = a
            d[name] = nc.dram_tensor(f"{prefix}_{name}", a.shape, mybir.dt.from_np(a.dtype), kind="ExternalInput").ap()
    return d


def kernel(**inputs):
    import concourse.bacc as bacc
    from concourse.bass_utils import run_bass_kernel_spmd

    nc = bacc.Bacc("TRN2", target_bir_lowering=False, num_devices=1)
    arrays = {}
    d = declare(nc, lay_out({n: np.asarray(a) for n, a in inputs.items()}), arrays)
    out = nc.dram_tensor("out", (B * S, D), F32, kind="ExternalOutput").ap()
    program(nc, d, out)
    r = run_bass_kernel_spmd(nc, [arrays], core_ids=[0])
    return r.results[0]["out"].reshape(B, S, D)
```
